# Optimizing a Trainium2 kernel written in Bass

```python
import numpy as np
import jax
import jax.numpy as jnp

def _softmax(x, axis=-1):
    return jax.nn.softmax(x, axis=axis)

def _gelu(x):
    return jax.nn.gelu(x, approximate=True)

def _silu(x):
    return jax.nn.silu(x)

def _sigmoid(x):
    return jax.nn.sigmoid(x)

def _layernorm(x, axis=-1, eps=1e-05):
    m = jnp.mean(x, axis=axis, keepdims=True)
    v = jnp.var(x, axis=axis, keepdims=True)
    return (x - m) / jnp.sqrt(v + eps)

def _scatter_add(tgt, idx, src, axis=0):
    return tgt.at[idx].add(src)

def _segment_sum(src, seg, n):
    return jax.ops.segment_sum(src, seg, n)
kernel_name = 'mk_decoder_postln_d1_seqx_r4_9ede7a'

def setup_inputs(seed: int=0):
    np.random.seed(seed)
    _w = jnp.asarray

    def _rec_inputs():
        import jax
        import jax.numpy as jnp
        _rk = jax.random.key(seed)
        x = -0.000125 + 0.9999 * jax.random.normal(jax.random.fold_in(_rk, 1), (4, 512, 512), jnp.float32)
        _lenS = 512 - jax.random.randint(jax.random.fold_in(_rk, 7), (4,), 0, max(1, 512 // 4) + 1, jnp.int32)
        _lenS2 = 512 - jax.random.randint(jax.random.fold_in(_rk, 8), (4,), 0, max(1, 512 // 4) + 1, jnp.int32)
        fside_BxS2xS2_0 = -3.05549e-07 + 0.0199987 * jax.random.normal(jax.random.fold_in(_rk, 11), (4, 512, 512), jnp.float32)
        _ctx_1024P = jax.random.normal(jax.random.fold_in(_rk, 12), (4, 16, 256), jnp.float32)
        _ctx_1024c = jax.random.dirichlet(jax.random.fold_in(_rk, 512), 0.3 * jnp.ones((16,), jnp.float32), (4, 512))
        _ctx_1024t = jnp.einsum('bsk,bkd->bsd', _ctx_1024c, _ctx_1024P)
        _ctx_1024t = _ctx_1024t * jax.lax.rsqrt(jnp.mean(jnp.square(_ctx_1024t)) + 1e-12) * 0.953939
        ctx_1024 = 6.82029e-06 + 0.0200006 * (_ctx_1024t + 0.3 * jax.random.normal(jax.random.fold_in(_rk, 612), (4, 512, 256), jnp.float32))
        return (x, fside_BxS2xS2_0, ctx_1024)
    x, fside_BxS2xS2_0, ctx_1024 = _rec_inputs()

    def _L0_attn_setup():
        import jax, jax.numpy as jnp
        import numpy as np
        from jax import lax
        B, T, D, H, CS = (4, 1024, 512, 16, 64)
        DK = D // H

        def apply_rope(x):
            t, d = (x.shape[-2], x.shape[-1])
            inv_freq = 1.0 / 10000.0 ** (jnp.arange(0, d, 2, dtype=jnp.float32) / d)
            pos = jnp.arange(t, dtype=jnp.float32)
            sinusoid = pos[:, None] * inv_freq[None, :]
            sin, cos = (jnp.sin(sinusoid), jnp.cos(sinusoid))
            x1, x2 = (x[..., ::2], x[..., 1::2])
            out = jnp.stack([x1 * cos - x2 * sin, x1 * sin + x2 * cos], axis=-1)
            return out.reshape(x.shape)
        key = jax.random.key(seed)
        ks = jax.random.split(key, 6)
        s = 0.02
        return {'x': jax.random.normal(ks[0], (B, T, D), dtype=jnp.float32), 'Wq': jax.random.normal(ks[1], (D, D), dtype=jnp.float32) * s, 'bq': jnp.zeros((D,), jnp.float32), 'Wk': jax.random.normal(ks[2], (D, D), dtype=jnp.float32) * s, 'bk': jnp.zeros((D,), jnp.float32), 'Wv': jax.random.normal(ks[3], (D, D), dtype=jnp.float32) * s, 'bv': jnp.zeros((D,), jnp.float32), 'Wg': jax.random.normal(ks[4], (D, D), dtype=jnp.float32) * s, 'bg': jnp.zeros((D,), jnp.float32), 'Wo': jax.random.normal(ks[5], (D, D), dtype=jnp.float32) * s, 'bo': jnp.zeros((D,), jnp.float32)}
    _L0_attn_all = _L0_attn_setup()
    _L0_attn_in = {k: v for k, v in _L0_attn_all.items() if k in ('Wq', 'bq', 'Wk', 'bk', 'Wv', 'bv', 'Wg', 'bg', 'Wo', 'bo')}
    del _L0_attn_all

    def _L0_xattn_setup():
        import jax, jax.numpy as jnp
        import numpy as np
        EPS = 1e-06
        QMAX = 127.0

        def _smooth_quant_linear(x, w):
            amax_x = jnp.max(jnp.abs(x), axis=0)
            amax_w = jnp.max(jnp.abs(w), axis=0)
            s = jnp.sqrt(jnp.maximum(amax_x, EPS) / jnp.maximum(amax_w, EPS))
            s = jnp.maximum(s, EPS)
            xs = x / s
            ws = w * s
            x_scale = jnp.maximum(jnp.max(jnp.abs(xs), axis=-1, keepdims=True), EPS) / QMAX
            w_scale = jnp.maximum(jnp.max(jnp.abs(ws), axis=-1, keepdims=True), EPS) / QMAX
            x_q = jnp.clip(jnp.round(xs / x_scale), -QMAX, QMAX)
            w_q = jnp.clip(jnp.round(ws / w_scale), -QMAX, QMAX)
            return x_q @ w_q.T * x_scale * w_scale.T

        def _expert_forward(xe, guw, dw):
            h = _smooth_quant_linear(xe, guw)
            gate, up = jnp.split(h, 2, axis=-1)
            a = jax.nn.silu(gate) * up
            return _smooth_quant_linear(a, dw)
        key = jax.random.key(seed)
        k1, k2, k3 = jax.random.split(key, 3)
        E, T, D, I = (8, 512, 512, 256)
        x = jax.random.normal(k1, (E, T, D), dtype=jnp.float32)
        gate_up_weight = jax.random.normal(k2, (E, 2 * I, D), dtype=jnp.float32) * 0.02
        down_weight = jax.random.normal(k3, (E, D, I), dtype=jnp.float32) * 0.02
        return {'x': x, 'gate_up_weight': gate_up_weight, 'down_weight': down_weight}
    _L0_xattn_all = _L0_xattn_setup()
    _L0_xattn_in = {k: v for k, v in _L0_xattn_all.items() if k in ()}
    del _L0_xattn_all

    def _L0_ffn_setup():
        import jax, jax.numpy as jnp
        import numpy as np
        TOP_K = 2
        LORA_SCALE = 32.0 / 16.0
        key = jax.random.key(seed)
        ks = jax.random.split(key, 11)
        B, S, D, F, E, R = (4, 256, 512, 1408, 8, 16)
        sd, sf = (1.0 / np.sqrt(D), 1.0 / np.sqrt(F))
        return {'x': jax.random.normal(ks[0], (B, S, D), jnp.float32), 'gate_w': jax.random.normal(ks[1], (E, D), jnp.float32) * 0.02, 'w1': jax.random.normal(ks[2], (F, D), jnp.float32) * sd, 'w3': jax.random.normal(ks[3], (F, D), jnp.float32) * sd, 'w2': jax.random.normal(ks[4], (D, F), jnp.float32) * sf, 'a1': jax.random.normal(ks[5], (E, R, D), jnp.float32) * sd, 'b1': jax.random.normal(ks[6], (E, F, R), jnp.float32) * 0.01, 'a3': jax.random.normal(ks[7], (E, R, D), jnp.float32) * sd, 'b3': jax.random.normal(ks[8], (E, F, R), jnp.float32) * 0.01, 'a2': jax.random.normal(ks[9], (E, R, F), jnp.float32) * sf, 'b2': jax.random.normal(ks[10], (E, D, R), jnp.float32) * 0.01}
    _L0_ffn_all = _L0_ffn_setup()
    _L0_ffn_in = {k: v for k, v in _L0_ffn_all.items() if k in ('gate_w', 'w1', 'w3', 'w2', 'a1', 'b1', 'a3', 'b3', 'a2', 'b2')}
    del _L0_ffn_all
    return {'x': x, 'fside_BxS2xS2_0': fside_BxS2xS2_0, 'ctx_1024': ctx_1024, 'L0_attn_Wq': _L0_attn_in['Wq'], 'L0_attn_bq': _L0_attn_in['bq'], 'L0_attn_Wk': _L0_attn_in['Wk'], 'L0_attn_bk': _L0_attn_in['bk'], 'L0_attn_Wv': _L0_attn_in['Wv'], 'L0_attn_bv': _L0_attn_in['bv'], 'L0_attn_Wg': _L0_attn_in['Wg'], 'L0_attn_bg': _L0_attn_in['bg'], 'L0_attn_Wo': _L0_attn_in['Wo'], 'L0_attn_bo': _L0_attn_in['bo'], 'L0_ffn_gate_w': _L0_ffn_in['gate_w'], 'L0_ffn_w1': _L0_ffn_in['w1'], 'L0_ffn_w3': _L0_ffn_in['w3'], 'L0_ffn_w2': _L0_ffn_in['w2'], 'L0_ffn_a1': _L0_ffn_in['a1'], 'L0_ffn_b1': _L0_ffn_in['b1'], 'L0_ffn_a3': _L0_ffn_in['a3'], 'L0_ffn_b3': _L0_ffn_in['b3'], 'L0_ffn_a2': _L0_ffn_in['a2'], 'L0_ffn_b2': _L0_ffn_in['b2']}

def reference(x, fside_BxS2xS2_0, ctx_1024, L0_attn_Wq, L0_attn_bq, L0_attn_Wk, L0_attn_bk, L0_attn_Wv, L0_attn_bv, L0_attn_Wg, L0_attn_bg, L0_attn_Wo, L0_attn_bo, L0_ffn_gate_w, L0_ffn_w1, L0_ffn_w3, L0_ffn_w2, L0_ffn_a1, L0_ffn_b1, L0_ffn_a3, L0_ffn_b3, L0_ffn_a2, L0_ffn_b2):
    import jax
    import jax.numpy as jnp

    def _L0_attn_ref(x, Wq, bq, Wk, bk, Wv, bv, Wg, bg, Wo, bo):
        import jax, jax.numpy as jnp
        import numpy as np
        from jax import lax
        B, T, D, H, CS = (4, 1024, 512, 16, 64)
        DK = D // H

        def apply_rope(x):
            t, d = (x.shape[-2], x.shape[-1])
            inv_freq = 1.0 / 10000.0 ** (jnp.arange(0, d, 2, dtype=jnp.float32) / d)
            pos = jnp.arange(t, dtype=jnp.float32)
            sinusoid = pos[:, None] * inv_freq[None, :]
            sin, cos = (jnp.sin(sinusoid), jnp.cos(sinusoid))
            x1, x2 = (x[..., ::2], x[..., 1::2])
            out = jnp.stack([x1 * cos - x2 * sin, x1 * sin + x2 * cos], axis=-1)
            return out.reshape(x.shape)
        b, t, c = x.shape
        h, dk, cs = (H, DK, CS)
        nc = t // cs

        def heads(y):
            return y.reshape(b, t, h, dk).transpose(0, 2, 1, 3)
        q = heads(x @ Wq.T + bq)
        k = heads(x @ Wk.T + bk)
        v = heads(x @ Wv.T + bv)
        g = jax.nn.sigmoid(heads(x @ Wg.T + bg))
        q = jax.nn.elu(apply_rope(q)) + 1.0
        k = jax.nn.elu(apply_rope(k)) + 1.0

        def chunked(y):
            return y.reshape(b, h, nc, cs, dk).transpose(2, 0, 1, 3, 4)
        qc, kc, vc, gc = (chunked(q), chunked(k), chunked(v), chunked(g))
        S0 = jnp.zeros((b, h, dk, dk), x.dtype)
        Z0 = jnp.zeros((b, h, dk), x.dtype)

        def step(carry, inp):
            S, Z = carry
            qi, ki, vi, gi = inp
            S = S + jnp.einsum('bhtd,bhte->bhde', ki, vi)
            Z = Z + ki.sum(axis=2)
            num = jnp.einsum('bhtd,bhde->bhte', qi, S)
            den = jnp.einsum('bhtd,bhd->bht', qi, Z)[..., None] + 1e-06
            return ((S, Z), gi * num / den)
        _, out = lax.scan(step, (S0, Z0), (qc, kc, vc, gc))
        out = out.transpose(1, 2, 0, 3, 4).reshape(b, h, t, dk)
        out = out.transpose(0, 2, 1, 3).reshape(b, t, c)
        return out @ Wo.T + bo

    def _L0_xattn_ref(x, gate_up_weight, down_weight):
        import jax, jax.numpy as jnp
        import numpy as np
        EPS = 1e-06
        QMAX = 127.0

        def _smooth_quant_linear(x, w):
            amax_x = jnp.max(jnp.abs(x), axis=0)
            amax_w = jnp.max(jnp.abs(w), axis=0)
            s = jnp.sqrt(jnp.maximum(amax_x, EPS) / jnp.maximum(amax_w, EPS))
            s = jnp.maximum(s, EPS)
            xs = x / s
            ws = w * s
            x_scale = jnp.maximum(jnp.max(jnp.abs(xs), axis=-1, keepdims=True), EPS) / QMAX
            w_scale = jnp.maximum(jnp.max(jnp.abs(ws), axis=-1, keepdims=True), EPS) / QMAX
            x_q = jnp.clip(jnp.round(xs / x_scale), -QMAX, QMAX)
            w_q = jnp.clip(jnp.round(ws / w_scale), -QMAX, QMAX)
            return x_q @ w_q.T * x_scale * w_scale.T

        def _expert_forward(xe, guw, dw):
            h = _smooth_quant_linear(xe, guw)
            gate, up = jnp.split(h, 2, axis=-1)
            a = jax.nn.silu(gate) * up
            return _smooth_quant_linear(a, dw)
        return jax.vmap(_expert_forward)(x, gate_up_weight, down_weight)

    def _L0_ffn_ref(x, gate_w, w1, w3, w2, a1, b1, a3, b3, a2, b2):
        import jax, jax.numpy as jnp
        import numpy as np
        TOP_K = 2
        LORA_SCALE = 32.0 / 16.0
        B, S, D = x.shape
        E = gate_w.shape[0]
        xf = x.reshape(B * S, D)
        N = xf.shape[0]
        logits = xf @ gate_w.T
        top_w, top_i = jax.lax.top_k(logits, TOP_K)
        routing = jax.nn.softmax(top_w, axis=-1)
        w_full = jnp.zeros((N, E), x.dtype).at[jnp.arange(N)[:, None], top_i].add(routing)
        base1 = xf @ w1.T
        base3 = xf @ w3.T

        def expert_step(acc, p):
            A1, B1, A3, B3, A2, B2, we = p
            h1 = base1 + xf @ A1.T @ B1.T * LORA_SCALE
            h3 = base3 + xf @ A3.T @ B3.T * LORA_SCALE
            act = jax.nn.silu(h1) * h3
            out = act @ w2.T + act @ A2.T @ B2.T * LORA_SCALE
            return (acc + we[:, None] * out, None)
        init = jnp.zeros((N, D), x.dtype)
        out, _ = jax.lax.scan(expert_step, init, (a1, b1, a3, b3, a2, b2, w_full.T))
        return out.reshape(B, S, D)
    x = _layernorm(x + _L0_attn_ref(x, L0_attn_Wq, L0_attn_bq, L0_attn_Wk, L0_attn_bk, L0_attn_Wv, L0_attn_bv, L0_attn_Wg, L0_attn_bg, L0_attn_Wo, L0_attn_bo), axis=-1)
    x = _layernorm(x + _L0_xattn_ref(x, fside_BxS2xS2_0, ctx_1024), axis=-1)
    x = _layernorm(x + _L0_ffn_ref(x, L0_ffn_gate_w, L0_ffn_w1, L0_ffn_w3, L0_ffn_w2, L0_ffn_a1, L0_ffn_b1, L0_ffn_a3, L0_ffn_b3, L0_ffn_a2, L0_ffn_b2), axis=-1)
    return x

_drawn_inputs = setup_inputs


def setup_inputs(seed=0):
    import zlib

    import numpy as np

    out = dict(_drawn_inputs(seed))
    spreads = {'L0_attn_bq': (0.0, 2.0),
     'L0_attn_bk': (0.0, 2.0),
     'L0_attn_bv': (0.0, 0.312),
     'L0_attn_bg': (0.0, 2.0),
     'L0_attn_bo': (0.0, 0.1)}
    factors = {'L0_attn_Wq': 67.315, 'L0_attn_Wk': 8.0, 'L0_attn_Wv': 6.299, 'L0_attn_Wg': 8.0}
    for name, (base, spread) in spreads.items():
        noise = np.random.default_rng([zlib.crc32(name.encode()), seed]).standard_normal(out[name].shape)
        drawn = base * np.exp(spread * noise) if base else spread * noise
        out[name] = jnp.asarray(drawn.astype(out[name].dtype))
    for name, factor in factors.items():
        out[name] = (out[name] * factor).astype(out[name].dtype)
    return out
```

```python
from contextlib import ExitStack

import concourse.bass as bass
from concourse import mybir

F32 = mybir.dt.float32
F32R = mybir.dt.float32r
BF16 = mybir.dt.bfloat16
ALU = mybir.AluOpType
ACT = mybir.ActivationFunctionType
AX = mybir.AxisListType

P = 128
B = 4
T = 512
D = 512
H = 16
DK = D // H
CS = 64
TT = T // P
KT = D // P
GH = P // DK
NG = H // GH
E1 = DK + 1
GE = GH * E1
LN_EPS = 1e-5
DEN_EPS = 1e-6

RING = 4
QT, PQ, PK, PV, AT, PG, OUT = range(7)
ITEMS = 7
LEAD = (1, 0, 2, 2)


def matmul_split(pe, out, lhs_hi, lhs_lo, rhs_hi, rhs_lo, start, stop):
    pe.matmul(out, lhs_hi, rhs_hi, start=start, stop=False)
    pe.matmul(out, lhs_lo, rhs_hi, start=False, stop=False)
    return pe.matmul(out, lhs_hi, rhs_lo, start=False, stop=stop)


def moments(dve, stats, part, mean, var_eps, wait):
    dve.tensor_tensor(part[:, :, 0:2], stats[:, :, 1:3], stats[:, :, 4:6], ALU.add)
    wait(dve.tensor_tensor(part[:, :, 2], stats[:, :, 1], stats[:, :, 4], ALU.subtract))
    dve.tensor_scalar(mean, part[:, :, 0], 0.5, None, ALU.mult)
    dve.tensor_scalar(part[:, :, 3], part[:, :, 1], 1.0 / D, LN_EPS, ALU.mult, ALU.add)
    wait(dve.scalar_tensor_tensor(part[:, :, 4], part[:, :, 2], 0.25, part[:, :, 2], ALU.mult, ALU.mult))
    return dve.tensor_tensor(var_eps, part[:, :, 3], part[:, :, 4], ALU.add)


def attention(nc, xT, x, wT, biases, bo, rope, head_mask, ident_in, x1_dram):
    with ExitStack() as ctx:
        def sb(name, shape, dt=F32):
            return ctx.enter_context(nc.sbuf_tensor(name, shape, dt))

        def sem(name):
            return ctx.enter_context(nc.semaphore(name))

        w_raw = sb("w_raw", [P, KT, D])
        w_hi = sb("w_hi", [P, 5, KT, D], F32R)
        w_lo = sb("w_lo", [P, 5, KT, D], F32R)
        bias_raw = sb("bias_raw", [1, 4, D])
        bias_hl = sb("bias_hl", [P, 4, D], F32R)
        ones = sb("ones", [P, P], F32R)
        ident = sb("ident", [P, P])
        mask = sb("mask", [P, GE])
        ropes = sb("ropes", [P, 2, TT, DK])
        bo_bc = sb("bo_bc", [P, D])
        xT_raw = sb("xT_raw", [P, KT, T])
        x_tok = sb("x_tok", [P, TT, D])
        x1 = sb("x1", [P, TT, D])
        xT_hi = sb("xT_hi", [P, TT, KT, P], F32R)
        xT_lo = sb("xT_lo", [P, TT, KT, P], F32R)
        qk = sb("qk", [P, 2 * D])
        rot = sb("rot", [P, 2 * D])
        rot_a = sb("rot_a", [P, 2 * D])
        rot_b = sb("rot_b", [P, 2 * D])
        neg = sb("neg", [P, 2 * D])
        feat = sb("feat", [P, 2 * D])
        v_ext = sb("v_ext", [P, 2, H, E1])
        gate = sb("gate", [P, D])
        q_T = sb("q_T", [P, NG, P])
        s_bd = sb("s_bd", [P, 2, NG, GE])
        rden = sb("rden", [P, 2, H])
        att = sb("att", [P, D])
        att_hi = sb("att_hi", [P, KT, P], F32R)
        att_lo = sb("att_lo", [P, KT, P], F32R)
        stats = sb("stats", [P, TT, 6])
        part = sb("part", [P, TT, 5])
        mean = sb("mean", [P, TT])
        rstd = sb("rstd", [P, 3, TT])

        ring = [ctx.enter_context(nc.psum_tensor(f"ring{i}", [P, 512], F32)) for i in range(RING)]
        s_ps = ctx.enter_context(nc.psum_tensor("s_ps", [P, 2, 512], F32))
        n_ps = ctx.enter_context(nc.psum_tensor("n_ps", [P, 2, 512], F32))

        consts_loaded = sem("consts_loaded")
        w_loaded = sem("w_loaded")
        w_hi_ready = sem("w_hi_ready")
        w_lo_ready = sem("w_lo_ready")
        bias_cleared = sem("bias_cleared")
        bias_ready = sem("bias_ready")
        ones_ready = sem("ones_ready")
        xT_loaded = sem("xT_loaded")
        x_loaded = sem("x_loaded")
        xhi_ready = sem("xhi_ready")
        xlo_ready = sem("xlo_ready")
        filled = [sem(f"filled{i}") for i in range(RING)]
        drained = [sem(f"drained{i}") for i in range(RING)]
        rot_a_ready = sem("rot_a_ready")
        rot_b_ready = sem("rot_b_ready")
        rotated = sem("rotated")
        neg_ready = sem("neg_ready")
        exp_ready = sem("exp_ready")
        feat_ready = sem("feat_ready")
        s_updated = sem("s_updated")
        s_masked = sem("s_masked")
        num_ready = sem("num_ready")
        den_ready = sem("den_ready")
        rden_ready = sem("rden_ready")
        gated = sem("gated")
        att_ready = sem("att_ready")
        att_hi_ready = sem("att_hi_ready")
        xres_ready = sem("xres_ready")
        stats_ready = sem("stats_ready")
        moment_ready = sem("moment_ready")
        var_ready = sem("var_ready")
        std_ready = sem("std_ready")
        rstd_ready = sem("rstd_ready")
        normed = sem("normed")
        x1_stored = sem("x1_stored")

        def slot(b, t, item):
            n = ITEMS * (t if item in (QT, AT, OUT) else t - 1) + item
            before = b * (ITEMS * TT // RING) + n // RING + LEAD[n % RING]
            if isinstance(b, int) and (b, t, item) == (B - 1, TT - 1, OUT):
                before -= 1
            return n % RING, before

        def tile_no(b, t):
            return b * TT + t + 1

        def following(b, t):
            return (b, t + 1) if t + 1 < TT else (b + 1, 0)

        def batches(eng, body):
            with eng.Fori(0, B - 1) as b:
                body(b, False)
            body(B - 1, True)

        block = ctx.enter_context(nc.Block())

        @block.sync
        def _(sp):
            sp.dma_start(xT_raw[:, :, :], xT[:, 0:T].rearrange("(k p) t -> p k t", p=P)).then_inc(xT_loaded, 16)
            for i in range(5):
                if i:
                    sp.wait_ge(w_lo_ready, i)
                sp.dma_start(w_raw[:, :, :], wT[i].rearrange("(k p) n -> p k n", p=P)).then_inc(w_loaded, 16)

            def load_xT(b):
                sp.dma_start(xT_raw[:, :, :], xT[:, bass.ts(b, T)].rearrange("(k p) t -> p k t", p=P))\
                    .then_inc(xT_loaded, 16)

            def load_x(b):
                sp.dma_start(x_tok[:, :, :], x[bass.ts(b, T), :].rearrange("(t p) d -> p t d", p=P))\
                    .then_inc(x_loaded, 16)

            load_x(0)

            def body(b, last):
                if not last:
                    sp.wait_ge(xlo_ready, b * TT + TT)
                    load_xT(b + 1)
                    k, n = slot(b, TT - 1, OUT)
                    sp.wait_ge(drained[k], n + 1)
                    load_x(b + 1)
                sp.wait_ge(normed, b * TT + TT)
                sp.dma_start(x1_dram[bass.ts(b, T), :].rearrange("(t p) d -> p t d", p=P),
                             x1[:, :, :]).then_inc(x1_stored, 16)
            batches(sp, body)
            sp.wait_ge(x1_stored, 16 * B)

        @block.gpsimd
        def _(pool):
            pool.dma_start(bias_raw[:, :, :], biases).then_inc(consts_loaded, 16)
            pool.dma_start(ident[:, :], ident_in).then_inc(consts_loaded, 16)
            pool.dma_start(mask[:, :], head_mask).then_inc(consts_loaded, 16)
            pool.dma_start(ropes[:, :, :, :], rope).then_inc(consts_loaded, 16)
            pool.dma_start(bo_bc[:, :], bo).then_inc(consts_loaded, 16)
            for s in range(2):
                pool.memset(v_ext[:, s, :, DK:E1], 1.0).then_inc(ones_ready, 1)
            pool.wait_ge(consts_loaded, 80)

            def split(b, t):
                pool.wait_ge(xhi_ready, tile_no(b, t))
                pool.tensor_tensor(xT_lo[:, t, :, :], xT_raw[:, :, bass.ts(t, P)],
                                   xT_hi[:, t, :, :].bitcast(F32), ALU.subtract).then_inc(xlo_ready, 1)

            def rotate(b, t):
                for item in (PQ, PK):
                    k, n = slot(b, t, item)
                    pool.wait_ge(drained[k], n + 1)
                pool.wait_ge(rotated, tile_no(b, t) - 1)
                q4 = qk[:, :].rearrange("p (h i two) -> p h i two", i=DK // 2, two=2)
                b4 = rot_b[:, :].rearrange("p (h i two) -> p h i two", i=DK // 2, two=2)
                cos = ropes[:, 0, t, :].unsqueeze(1).to_broadcast([P, 2 * H, DK])
                sin = ropes[:, 1, t, :].rearrange("p (i two) -> p i two", two=2)
                pool.tensor_tensor(rot_a[:, :].rearrange("p (h i) -> p h i", i=DK),
                                   qk[:, :].rearrange("p (h i) -> p h i", i=DK), cos, ALU.mult)\
                    .then_inc(rot_a_ready, 1)
                for two in range(2):
                    pool.tensor_tensor(b4[:, :, :, two], q4[:, :, :, 1 - two],
                                       sin[:, :, two].unsqueeze(1).to_broadcast([P, 2 * H, DK // 2]),
                                       ALU.mult).then_inc(rot_b_ready, 1)

            def residual(b, t):
                if t == 0:
                    pool.wait_ge(x_loaded, b * 16 + 16)
                pool.tensor_tensor(x_tok[:, t, :], x_tok[:, t, :], bo_bc[:, :], ALU.add).then_inc(xres_ready, 1)

            for t in range(TT):
                split(0, t)
            rotate(0, 0)

            def body(b, last):
                for t in range(TT):
                    residual(b, t)
                    if not (last and t == TT - 1):
                        rotate(*following(b, t))
                    if not last and t:
                        split(b + 1, t - 1)
                if not last:
                    split(b + 1, TT - 1)
            batches(pool, body)

        @block.scalar
        def _(act):
            def x_hi(b, t):
                if t == 0:
                    act.wait_ge(xT_loaded, b * 16 + 16)
                if not isinstance(b, int):
                    k, n = slot(b - 1, t, PG)
                    act.wait_ge(filled[k], n + 1)
                act.activation(xT_hi[:, t, :, :], xT_raw[:, :, bass.ts(t, P)], ACT.Copy).then_inc(xhi_ready, 1)

            for t in range(TT):
                x_hi(0, t)
            for i in range(5):
                act.wait_ge(w_loaded, 16 * (i + 1))
                act.activation(w_hi[:, i, :, :], w_raw[:, :, :], ACT.Copy).then_inc(w_hi_ready, 1)

            def qk_out(b, t, item):
                k, n = slot(b, t, item)
                act.wait_ge(filled[k], n + 1)
                if item == PQ:
                    act.wait_ge(rot_a_ready, tile_no(b, t) - 1)
                    act.wait_ge(rot_b_ready, 2 * (tile_no(b, t) - 1))
                twice = isinstance(b, int) and b == 0 and t == 0 and item == PK
                act.activation(qk[:, bass.ts(item - PQ, D)], ring[k][:, :], ACT.Copy)\
                    .then_inc(drained[k], 2 if twice else 1)

            def v_out(b, t):
                k, n = slot(b, t, PV)
                act.wait_ge(filled[k], n + 1)
                act.wait_ge(s_updated, 2 * (tile_no(b, t) - 1))
                if t < 2:
                    act.wait_ge(ones_ready, 2)
                act.activation(v_ext[:, t % 2, :, 0:DK], ring[k][:, :].rearrange("p (h e) -> p h e", e=DK),
                               ACT.Copy).then_inc(drained[k], 1)

            def gate_out(b, t):
                k, n = slot(b, t, PG)
                act.wait_ge(filled[k], n + 1)
                act.wait_ge(gated, 2 * (tile_no(b, t) - 1))
                act.activation(gate[:, :], ring[k][:, :], ACT.Tanh, scale=0.5).then_inc(drained[k], 1)

            def exponential(b, t):
                act.wait_ge(neg_ready, tile_no(b, t))
                act.activation(neg[:, :], neg[:, :], ACT.Exp).then_inc(exp_ready, 1)

            def qT_out(b, t):
                k, n = slot(b, t, QT)
                act.wait_ge(filled[k], n + 1)
                act.wait_ge(num_ready, 2 * (tile_no(b, t) - 1))
                act.activation(q_T[:, :, :], ring[k][:, :].rearrange("p (g t) -> p g t", g=NG), ACT.Copy)\
                    .then_inc(drained[k], 1)

            def attT_hi(b, t):
                k, n = slot(b, t, AT)
                act.wait_ge(filled[k], n + 1)
                ko, no = slot(b, t - 1, OUT)
                act.wait_ge(filled[ko], no + 1)
                act.activation(att_hi[:, :, :], ring[k][:, :].rearrange("p (g t) -> p g t", g=KT), ACT.Copy)\
                    .then_inc(att_hi_ready, 1)

            def standard_deviation(b):
                act.wait_ge(var_ready, b + 1)
                act.activation(rstd[:, 1, :], rstd[:, 0, :], ACT.Sqrt).then_inc(std_ready, 1)

            qk_out(0, 0, PQ)
            qk_out(0, 0, PK)
            v_out(0, 0)
            gate_out(0, 0)
            exponential(0, 0)

            def body(b, last):
                for t in range(TT):
                    qT_out(b, t)
                    if last and t == TT - 1:
                        attT_hi(b, t)
                    else:
                        nb, nt = following(b, t)
                        qk_out(nb, nt, PQ)
                        qk_out(nb, nt, PK)
                        v_out(nb, nt)
                        attT_hi(b, t)
                        gate_out(nb, nt)
                        exponential(nb, nt)
                    if not last and t:
                        x_hi(b + 1, t - 1)
                if not last:
                    x_hi(b + 1, TT - 1)
                standard_deviation(b)
            batches(act, body)

        @block.vector
        def _(dve):
            for i in range(5):
                dve.wait_ge(w_hi_ready, i + 1)
                if i == 0:
                    dve.memset(bias_hl[:, :, :].bitcast(F32), 0.0).then_inc(bias_cleared, 1)
                    dve.memset(ones[:, :].bitcast(F32), 1.0).then_inc(bias_cleared, 1)
                    dve.wait_ge(bias_cleared, 2)
                    dve.wait_ge(consts_loaded, 80)
                    dve.tensor_copy(bias_hl[0:1, :, :], bias_raw[:, :, :]).then_inc(bias_ready, 1)
                    dve.wait_ge(bias_ready, 1)
                    dve.tensor_tensor(bias_hl[32:33, :, :], bias_raw[:, :, :],
                                      bias_hl[0:1, :, :].bitcast(F32), ALU.subtract).then_inc(bias_ready, 1)
                dve.tensor_tensor(w_lo[:, i, :, :], w_raw[:, :, :], w_hi[:, i, :, :].bitcast(F32),
                                  ALU.subtract).then_inc(w_lo_ready, 1)

            def rotated_sum(b, t):
                dve.wait_ge(rot_a_ready, tile_no(b, t))
                dve.wait_ge(rot_b_ready, 2 * tile_no(b, t))
                dve.wait_ge(feat_ready, tile_no(b, t) - 1)
                dve.tensor_tensor(rot[:, :], rot_a[:, :], rot_b[:, :], ALU.add).then_inc(rotated, 1)
                dve.wait_ge(rotated, tile_no(b, t))
                dve.tensor_scalar(neg[:, :], rot[:, :], 0.0, None, ALU.min).then_inc(neg_ready, 1)

            def features(b, t):
                dve.wait_ge(exp_ready, tile_no(b, t))
                dve.wait_ge(s_updated, 2 * (tile_no(b, t) - 1))
                dve.scalar_tensor_tensor(feat[:, :], rot[:, :], 0.0, neg[:, :], ALU.max, ALU.add)\
                    .then_inc(feat_ready, 1)

            def mask_state(b, t, c):
                dve.wait_ge(s_updated, 2 * (tile_no(b, t) - 1) + c + 1)
                dve.wait_ge(num_ready, 2 * (tile_no(b, t) - 1))
                dve.tensor_tensor(s_bd[:, c, :, :].rearrange("p (a g) n -> p a g n", a=2),
                                  s_ps[:, :, 0:2 * GE].rearrange("p a (g n) -> p a g n", g=2),
                                  mask[:, :].unsqueeze(1).unsqueeze(1).to_broadcast([P, 2, 2, GE]),
                                  ALU.mult).then_inc(s_masked, 1)

            def attend(b, t):
                dve.wait_ge(num_ready, 2 * tile_no(b, t))
                n4 = n_ps[:, :, 0:2 * GE].rearrange("p a (h e) -> p a h e", e=E1)
                dve.tensor_scalar(rden[:, 0, :].rearrange("p (a h) -> p a h", a=2), n4[:, :, :, DK],
                                  DEN_EPS, 2.0, ALU.add, ALU.mult).then_inc(den_ready, 1)
                k, n = slot(b, t, PG)
                dve.wait_ge(drained[k], n + 1)
                k, n = slot(b, t - 1, AT)
                dve.wait_ge(filled[k], n + 1)
                for a in range(2):
                    half = bass.ts(a, D // 2)
                    dve.scalar_tensor_tensor(att[:, half].rearrange("p (h e) -> p h e", e=DK),
                                             gate[:, half].rearrange("p (h e) -> p h e", e=DK), 1.0,
                                             n4[:, a, :, 0:DK], ALU.add, ALU.mult).then_inc(gated, 1)
                dve.wait_ge(den_ready, tile_no(b, t))
                dve.reciprocal(rden[:, 1, :], rden[:, 0, :]).then_inc(rden_ready, 1)
                dve.wait_ge(rden_ready, tile_no(b, t))
                dve.wait_ge(gated, 2 * tile_no(b, t))
                att3 = att[:, :].rearrange("p (h e) -> p h e", e=DK)
                dve.tensor_tensor(att3, att3, rden[:, 1, :].unsqueeze(2).to_broadcast([P, H, DK]), ALU.mult)\
                    .then_inc(att_ready, 1)

            def attT_lo(b, t):
                k, n = slot(b, t, AT)
                dve.wait_ge(att_hi_ready, tile_no(b, t))
                dve.tensor_tensor(att_lo[:, :, :], ring[k][:, :].rearrange("p (g t) -> p g t", g=KT),
                                  att_hi[:, :, :].bitcast(F32), ALU.subtract).then_inc(drained[k], 1)

            def add_residual(b, t):
                k, n = slot(b, t, OUT)
                dve.wait_ge(filled[k], n + 1)
                dve.wait_ge(xres_ready, tile_no(b, t))
                if t == 0:
                    dve.wait_ge(x1_stored, 16 * b)
                dve.tensor_tensor(x1[:, t, :], ring[k][:, :], x_tok[:, t, :], ALU.add).then_inc(drained[k], 1)
                dve.wait_ge(drained[k], n + 1)
                dve.bn_stats(stats[:, t, :], x1[:, t, :]).then_inc(stats_ready, 1)

            def normalise(b):
                dve.wait_ge(stats_ready, b * TT + TT)
                level = [0]

                def wait(last):
                    level[0] += 1
                    last.then_inc(moment_ready, 1)
                    dve.wait_ge(moment_ready, b * 2 + level[0])

                moments(dve, stats, part, mean[:, :], rstd[:, 0, :], wait).then_inc(var_ready, 1)
                dve.wait_ge(std_ready, b + 1)
                dve.reciprocal(rstd[:, 2, :], rstd[:, 1, :]).then_inc(rstd_ready, 1)
                dve.wait_ge(rstd_ready, b + 1)
                for t in range(TT):
                    dve.tensor_scalar(x1[:, t, :], x1[:, t, :], mean[:, t:t + 1], rstd[:, 2, t:t + 1],
                                      ALU.subtract, ALU.mult).then_inc(normed, 1)

            rotated_sum(0, 0)
            features(0, 0)

            def body(b, last):
                for t in range(TT):
                    mask_state(b, t, 0)
                    mask_state(b, t, 1)
                    attend(b, t)
                    attT_lo(b, t)
                    more = not (last and t == TT - 1)
                    if more:
                        rotated_sum(*following(b, t))
                    add_residual(b, t)
                    if more:
                        features(*following(b, t))
                normalise(b)
            batches(dve, body)

        @block.tensor
        def _(pe):
            def project(b, t, item):
                k, n = slot(b, t, item)
                i = (PQ, PK, PV, PG).index(item)
                if item == PQ:
                    pe.wait_ge(xlo_ready, tile_no(b, t))
                pe.wait_ge(drained[k], n)
                pe.matmul(ring[k][:, :], ones[:, :], bias_hl[:, i, :], start=True, stop=False)
                for c in range(KT):
                    last = matmul_split(pe, ring[k][:, :], xT_hi[:, t, c, :], xT_lo[:, t, c, :],
                                        w_hi[:, i, c, :], w_lo[:, i, c, :], False, c == KT - 1)
                twice = isinstance(b, int) and b == 0 and t == 0 and item == PK
                last.then_inc(filled[k], 2 if twice else 1)

            def q_transposed(b, t):
                k, n = slot(b, t, QT)
                pe.wait_ge(feat_ready, tile_no(b, t))
                pe.wait_ge(drained[k], n)
                for g in range(NG):
                    last = pe.transpose(ring[k][:, bass.ts(g, P)], feat[:, bass.ts(g, P)], ident[:, :])
                last.then_inc(filled[k], 1)

            def update_state(b, t, c):
                if c == 0:
                    k, n = slot(b, t, PV)
                    pe.wait_ge(drained[k], n + 1)
                pe.wait_ge(s_masked, 2 * (tile_no(b, t) - 1) + c)
                rows = slice(c * CS, (c + 1) * CS)
                for g in range(NG):
                    first = t == 0 and c == 0 and g % 2 == 0
                    last = pe.matmul(s_ps[:, g // 2, (g % 2) * GE:(g % 2 + 1) * GE],
                                     feat[rows, D + g * P:D + (g + 1) * P],
                                     v_ext[rows, t % 2, g * GH:(g + 1) * GH, :].rearrange("p h e -> p (h e)"),
                                     start=first, stop=True, skip_group_check=True)
                last.then_inc(s_updated, 1)

            def numerators(b, t, c):
                pe.wait_ge(s_masked, 2 * (tile_no(b, t) - 1) + c + 1)
                if c == 0:
                    k, n = slot(b, t, QT)
                    pe.wait_ge(drained[k], n + 1)
                    pe.wait_ge(gated, 2 * (tile_no(b, t) - 1))
                    pe.wait_ge(den_ready, tile_no(b, t) - 1)
                rows = slice(c * CS, (c + 1) * CS)
                for g in range(NG):
                    last = pe.matmul(n_ps[rows, g // 2, (g % 2) * GE:(g % 2 + 1) * GE],
                                     q_T[:, g, rows], s_bd[:, c, g, :], start=True, stop=True)
                last.then_inc(num_ready, 1)

            def att_transposed(b, t):
                k, n = slot(b, t, AT)
                pe.wait_ge(att_ready, tile_no(b, t))
                pe.wait_ge(drained[k], n)
                for g in range(NG):
                    last = pe.transpose(ring[k][:, bass.ts(g, P)], att[:, bass.ts(g, P)], ident[:, :])
                last.then_inc(filled[k], 1)

            def output(b, t):
                k, n = slot(b, t, OUT)
                ka, na = slot(b, t, AT)
                pe.wait_ge(drained[ka], na + 1)
                pe.wait_ge(drained[k], n)
                for c in range(KT):
                    last = matmul_split(pe, ring[k][:, :], att_hi[:, c, :], att_lo[:, c, :],
                                        w_hi[:, 4, c, :], w_lo[:, 4, c, :], c == 0, c == KT - 1)
                last.then_inc(filled[k], 1)

            pe.wait_ge(bias_ready, 2)
            pe.wait_ge(consts_loaded, 80)
            pe.wait_ge(ones_ready, 2)
            for i, item in enumerate((PQ, PK, PV, PG)):
                pe.wait_ge(w_lo_ready, i + 1)
                project(0, 0, item)
            pe.wait_ge(w_lo_ready, 5)

            def body(b, last):
                for t in range(TT):
                    more = not (last and t == TT - 1)
                    nb, nt = following(b, t)
                    q_transposed(b, t)
                    update_state(b, t, 0)
                    if more:
                        project(nb, nt, PQ)
                    numerators(b, t, 0)
                    update_state(b, t, 1)
                    if more:
                        project(nb, nt, PK)
                    numerators(b, t, 1)
                    if more:
                        project(nb, nt, PV)
                    att_transposed(b, t)
                    if more:
                        project(nb, nt, PG)
                    output(b, t)
            batches(pe, body)




Q_EPS = 1e-6
QMAX = 127.0
ROUND = 1.5 * 2.0 ** 23
QB = 8
MX, MW, RS, SS, XT0, XT1, SW, WT0, WT1, O0 = range(10)
Q_ORDER = [(0, i) for i in (MX, MW, RS, SS, XT0, XT1, SW, WT0, WT1, O0, O0 + 1, O0 + 2, O0 + 3)] + \
          [(1, i) for i in (MX, MW, RS, SS, XT0, SW, WT0, O0, O0 + 1, O0 + 2, O0 + 3)]
CHANNELS = (D, D // 2)


def experts(nc, x1_dram, w1, w2, ident_in, x2_dram):
    with ExitStack() as ctx:
        def sb(name, shape, dt=F32):
            return ctx.enter_context(nc.sbuf_tensor("q_" + name, shape, dt))

        def sem(name):
            return ctx.enter_context(nc.semaphore("q_" + name))

        def sems(name):
            return [sem(name + "1"), sem(name + "2")]

        ident = sb("ident", [P, P])
        ident16 = sb("ident16", [P, P], BF16)
        ones = sb("ones", [P, P])
        x1 = sb("x1", [P, TT, D])
        w_nat = [sb("w_nat1", [P, TT, D]), sb("w_nat2", [P, TT, D // 2])]
        scaled_x = sb("scaled_x", [P, TT, D])
        scaled_w = sb("scaled_w", [P, TT, D])
        top = sb("top", [P, 2, D])
        amax = sb("amax", [P, 2, KT])
        small = sb("small", [P, 4, KT])
        diag = sb("diag", [P, 2, KT, P])
        rows = sb("rows", [P, 3, D])
        row_max = sb("row_max", [P, 2, TT])
        scale = sb("scale", [P, 2, TT])
        inverse = sb("inverse", [P, 2, TT])
        q = [sb("qx", [P, TT, D], BF16), sb("qw", [P, TT, D], BF16)]
        qT = [sb("qxT", [P, KT, T], BF16), sb("qwT", [P, KT, D], BF16)]
        gu = sb("gu", [P, TT, D])
        sl = sb("sl", [P, TT, D // 2])
        act_in = sb("act_in", [P, TT, D // 2])
        stats = sb("stats", [P, TT, 6])
        part = sb("part", [P, TT, 5])
        mean = sb("mean", [P, TT])
        rstd = sb("rstd", [P, 3, TT])

        bank = [ctx.enter_context(nc.psum_tensor(f"q_bank{i}", [P, 512], F32)) for i in range(QB)]

        consts_loaded = sem("consts_loaded")
        consts_ready = sem("consts_ready")
        x1_loaded = sem("x1_loaded")
        w_loaded = sems("w_loaded")
        filled = [sem(f"filled{i}") for i in range(QB)]
        drained = [sem(f"drained{i}") for i in range(QB)]
        top_ready = sems("top_ready")
        ratio_ready = sems("ratio_ready")
        root_ready = sems("root_ready")
        s_ready = sems("s_ready")
        chain = sem("chain")
        diag_ready = sems("diag_ready")
        scaled_ready = sems("scaled_ready")
        scale_ready = sems("scale_ready")
        sw_diag_ready = sems("sw_diag_ready")
        shifted = sems("shifted")
        clamped = sems("clamped")
        q_ready = sems("q_ready")
        silu_ready = sem("silu_ready")
        act_ready = sem("act_ready")
        var_ready = sem("var_ready")
        std_ready = sem("std_ready")
        normed = sem("normed")
        x2_stored = sem("x2_stored")

        per_bank = len(Q_ORDER) // QB

        def slot(b, which, item):
            n = Q_ORDER.index((which, item))
            return n % QB, b * per_bank + n // QB

        block = ctx.enter_context(nc.Block())

        @block.sync
        def _(sp):
            sp.dma_start(ident[:, :], ident_in).then_inc(consts_loaded, 16)
            with sp.Fori(0, B) as b:
                sp.wait_ge(x2_stored, 16 * b)
                sp.dma_start(x1[:, :, :], x1_dram[bass.ts(b, T), :].rearrange("(t p) d -> p t d", p=P))\
                    .then_inc(x1_loaded, 16)
                for which, w in enumerate((w1, w2)):
                    sp.wait_ge(scaled_ready[which], 2 * b)
                    sp.dma_start(w_nat[which][:, :, :],
                                 w[bass.ts(b, D), :].rearrange("(t p) d -> p t d", p=P))\
                        .then_inc(w_loaded[which], 16)
                sp.wait_ge(normed, b * TT + TT)
                sp.dma_start(x2_dram[bass.ts(b, T), :].rearrange("(t p) d -> p t d", p=P), x1[:, :, :])\
                    .then_inc(x2_stored, 16)
            sp.wait_ge(x2_stored, 16 * B)

        @block.gpsimd
        def _(pool):
            with pool.Fori(0, B) as b:
                for which in range(2):
                    C = CHANNELS[which]
                    kc = C // P
                    src = x1 if which == 0 else act_in
                    pool.wait_ge(s_ready[which], b + 1)
                    pool.wait_ge(consts_ready, 3)
                    for i in range(2):
                        pool.tensor_tensor(diag[:, i, 0:kc, :],
                                           ident[:, :].unsqueeze(1).to_broadcast([P, kc, P]),
                                           small[:, 3 - i, 0:kc].unsqueeze(2).to_broadcast([P, kc, P]),
                                           ALU.mult).then_inc(diag_ready[which], 1)
                    for i, (a, out, item) in enumerate(((src, scaled_x, RS), (w_nat[which], scaled_w, SS))):
                        k, n = slot(b, which, item)
                        pool.wait_ge(drained[k], n + 1)
                        pool.tensor_tensor(out[:, :, 0:C], a[:, :, 0:C],
                                           rows[:, i, 0:C].unsqueeze(1).to_broadcast([P, TT, C]),
                                           ALU.mult).then_inc(scaled_ready[which], 1)
                    pool.wait_ge(scale_ready[which], 2 * b + 2)
                    pool.tensor_tensor(diag[:, 0, :, :],
                                       ident[:, :].unsqueeze(1).to_broadcast([P, KT, P]),
                                       scale[:, 1, :].unsqueeze(2).to_broadcast([P, KT, P]),
                                       ALU.mult).then_inc(sw_diag_ready[which], 1)

        @block.scalar
        def _(act):
            with act.Fori(0, B) as b:
                for which in range(2):
                    C = CHANNELS[which]
                    kc = C // P
                    act.wait_ge(ratio_ready[which], b + 1)
                    act.activation(small[:, 2, 0:kc], small[:, 1, 0:kc], ACT.Sqrt).then_inc(root_ready[which], 1)
                    for i, item in enumerate((RS, SS)):
                        k, n = slot(b, which, item)
                        act.wait_ge(filled[k], n + 1)
                        act.activation(rows[:, i, 0:C], bank[k][:, 0:C], ACT.Copy).then_inc(drained[k], 1)
                    for i, out in enumerate((scaled_x, scaled_w)):
                        act.wait_ge(clamped[which], 2 * b + i + 1)
                        act.activation(q[i][:, :, 0:C], out[:, :, 0:C], ACT.Copy, bias=-ROUND)\
                            .then_inc(q_ready[which], 1)
                    for i, items in enumerate(((XT0, XT1), (WT0, WT1))):
                        for j in range(kc // 2):
                            k, n = slot(b, which, items[j])
                            act.wait_ge(filled[k], n + 1)
                            act.activation(qT[i][:, 2 * j:2 * j + 2, :],
                                           bank[k][:, :].bitcast(BF16).rearrange("p (c t) -> p c t", c=2),
                                           ACT.Copy).then_inc(drained[k], 1)
                        if i == 0:
                            k, n = slot(b, which, SW)
                            act.wait_ge(filled[k], n + 1)
                            act.activation(rows[:, 2, :], bank[k][:, :], ACT.Copy).then_inc(drained[k], 1)
                    if which == 0:
                        k, n = slot(b, 0, O0 + TT - 1)
                        act.wait_ge(drained[k], n + 1)
                        act.activation(sl[:, :, :], gu[:, :, 0:D // 2], ACT.Silu).then_inc(silu_ready, 1)
                act.wait_ge(var_ready, b + 1)
                act.activation(rstd[:, 1, :], rstd[:, 0, :], ACT.Sqrt).then_inc(std_ready, 1)

        @block.vector
        def _(dve):
            dve.memset(ones[:, :], 1.0).then_inc(consts_ready, 1)
            dve.wait_ge(consts_loaded, 16)
            dve.tensor_copy(ident16[:, :], ident[:, :]).then_inc(consts_ready, 1)
            dve.memset(scale[:, :, :], 0.0).then_inc(consts_ready, 1)
            dve.wait_ge(consts_ready, 3)
            with dve.Fori(0, B) as b:
                links = 19
                done = [0]

                def link(ins):
                    done[0] += 1
                    ins.then_inc(chain, 1)
                    dve.wait_ge(chain, b * links + done[0])

                for which in range(2):
                    C = CHANNELS[which]
                    kc = C // P
                    if which == 0:
                        dve.wait_ge(x1_loaded, 16 * b + 16)
                    dve.wait_ge(w_loaded[which], 16 * b + 16)
                    src = x1 if which == 0 else act_in
                    for i, a in enumerate((src, w_nat[which])):
                        dve.tensor_reduce(top[:, i, 0:C], a[:, :, 0:C].rearrange("p t c -> p c t"), AX.X, ALU.max,
                                          apply_absolute_value=True).then_inc(top_ready[which], 1)
                    for i, item in enumerate((MX, MW)):
                        k, n = slot(b, which, item)
                        dve.wait_ge(filled[k], n + 1)
                        dve.tensor_reduce(amax[:, i, 0:kc], bank[k][:, 0:C].rearrange("p (c t) -> p c t", t=P),
                                          AX.X, ALU.max).then_inc(drained[k], 1)
                        dve.wait_ge(drained[k], n + 1)
                    link(dve.tensor_scalar(amax[:, :, 0:kc], amax[:, :, 0:kc], Q_EPS, None, ALU.max))
                    link(dve.reciprocal(small[:, 0, 0:kc], amax[:, 1, 0:kc]))
                    dve.tensor_tensor(small[:, 1, 0:kc], amax[:, 0, 0:kc], small[:, 0, 0:kc], ALU.mult)\
                        .then_inc(ratio_ready[which], 1)
                    dve.wait_ge(root_ready[which], b + 1)
                    link(dve.tensor_scalar(small[:, 2, 0:kc], small[:, 2, 0:kc], Q_EPS, None, ALU.max))
                    dve.reciprocal(small[:, 3, 0:kc], small[:, 2, 0:kc]).then_inc(s_ready[which], 1)
                    for i, out in enumerate((scaled_x, scaled_w)):
                        dve.wait_ge(scaled_ready[which], 2 * b + i + 1)
                        link(dve.tensor_reduce(row_max[:, i, :], out[:, :, 0:C], AX.X, ALU.max,
                                               apply_absolute_value=True))
                        dve.tensor_scalar(scale[:, i, :], row_max[:, i, :], Q_EPS, 1.0 / QMAX, ALU.max, ALU.mult)\
                            .then_inc(scale_ready[which], 1)
                        dve.wait_ge(scale_ready[which], 2 * b + i + 1)
                        link(dve.reciprocal(inverse[:, i, :], scale[:, i, :]))
                        for t in range(TT):
                            dve.tensor_scalar(out[:, t, 0:C], out[:, t, 0:C], inverse[:, i, t:t + 1], ROUND,
                                              ALU.mult, ALU.add).then_inc(shifted[which], 1)
                        dve.wait_ge(shifted[which], b * 2 * TT + (i + 1) * TT)
                        dve.tensor_scalar(out[:, :, 0:C], out[:, :, 0:C], ROUND + QMAX, ROUND - QMAX,
                                          ALU.min, ALU.max).then_inc(clamped[which], 1)
                    k, n = slot(b, which, SW)
                    dve.wait_ge(drained[k], n + 1)
                    for t in range(TT):
                        k, n = slot(b, which, O0 + t)
                        dve.wait_ge(filled[k], n + 1)
                        dve.scalar_tensor_tensor(gu[:, t, :], bank[k][:, :], scale[:, 0, t:t + 1], rows[:, 2, :],
                                                 ALU.mult, ALU.mult).then_inc(drained[k], 1)
                    if which == 0:
                        dve.wait_ge(silu_ready, b + 1)
                        dve.tensor_tensor(act_in[:, :, :], sl[:, :, :], gu[:, :, D // 2:D], ALU.mult)\
                            .then_inc(act_ready, 1)
                        dve.wait_ge(act_ready, b + 1)
                k, n = slot(b, 1, O0 + TT - 1)
                dve.wait_ge(drained[k], n + 1)
                link(dve.tensor_tensor(x1[:, :, :], x1[:, :, :], gu[:, :, :], ALU.add))
                for t in range(TT):
                    last = dve.bn_stats(stats[:, t, :], x1[:, t, :])
                link(last)
                moments(dve, stats, part, mean[:, :], rstd[:, 0, :], link).then_inc(var_ready, 1)
                dve.wait_ge(std_ready, b + 1)
                link(dve.reciprocal(rstd[:, 2, :], rstd[:, 1, :]))
                for t in range(TT):
                    dve.tensor_scalar(x1[:, t, :], x1[:, t, :], mean[:, t:t + 1], rstd[:, 2, t:t + 1],
                                      ALU.subtract, ALU.mult).then_inc(normed, 1)
                dve.wait_ge(normed, b * TT + TT)
                assert done[0] == links

        @block.tensor
        def _(pe):
            pe.wait_ge(consts_ready, 3)
            with pe.Fori(0, B) as b:
                for which in range(2):
                    C = CHANNELS[which]
                    kc = C // P
                    for i, item in enumerate((MX, MW)):
                        k, n = slot(b, which, item)
                        pe.wait_ge(top_ready[which], 2 * b + i + 1)
                        pe.wait_ge(drained[k], n)
                        for c in range(kc):
                            last = pe.transpose(bank[k][:, bass.ts(c, P)], top[:, i, bass.ts(c, P)], ident[:, :])
                        last.then_inc(filled[k], 1)
                    for i, item in enumerate((RS, SS)):
                        k, n = slot(b, which, item)
                        pe.wait_ge(diag_ready[which], 2 * b + i + 1)
                        pe.wait_ge(drained[k], n)
                        pe.matmul(bank[k][:, 0:C], ones[:, :], diag[:, i, 0:kc, :].rearrange("p c t -> p (c t)"),
                                  start=True, stop=True).then_inc(filled[k], 1)

                    def transposed(i, items):
                        pe.wait_ge(q_ready[which], 2 * b + i + 1)
                        for j in range(kc // 2):
                            k, n = slot(b, which, items[j])
                            pe.wait_ge(drained[k], n)
                            half = bank[k][:, :].bitcast(BF16).rearrange("p (c t m) -> p c t m", c=2, t=TT)
                            for c in range(2):
                                for t in range(TT):
                                    last = pe.transpose(half[:, c, t, :], q[i][:, t, bass.ts(2 * j + c, P)],
                                                        ident16[:, :])
                            last.then_inc(filled[k], 1)

                    transposed(0, (XT0, XT1))
                    k, n = slot(b, which, SW)
                    pe.wait_ge(sw_diag_ready[which], b + 1)
                    pe.wait_ge(drained[k], n)
                    pe.matmul(bank[k][:, :], ones[:, :], diag[:, 0, :, :].rearrange("p c t -> p (c t)"),
                              start=True, stop=True).then_inc(filled[k], 1)
                    transposed(1, (WT0, WT1))
                    for items in ((XT0, XT1), (WT0, WT1)):
                        for j in range(kc // 2):
                            k, n = slot(b, which, items[j])
                            pe.wait_ge(drained[k], n + 1)
                    for t in range(TT):
                        k, n = slot(b, which, O0 + t)
                        pe.wait_ge(drained[k], n)
                        for c in range(kc):
                            last = pe.matmul(bank[k][:, :], qT[0][:, c, bass.ts(t, P)], qT[1][:, c, :],
                                             start=c == 0, stop=c == kc - 1)
                        last.then_inc(filled[k], 1)




F = 1408
FT = F // P
E = 8
R = 16
LORA_SCALE = 2.0
NU = 2 * P + E
UP = 2 * D + 2 * P
DOWN = P + D
RAW = 3
FAR = -3.0e38
YB = 4
XC0, U0, UM0, MT, WB0 = 0, 4, 8, 12, 13
Y_BEFORE = (4, 4, 4, 3)
Y_TOTAL = (5, 5, 5, 4)


def mixture(nc, x2_dram, a13g, stream, b2T, ident_in, descending, out_dram):
    with ExitStack() as ctx:
        def sb(name, shape, dt=F32):
            return ctx.enter_context(nc.sbuf_tensor("f_" + name, shape, dt))

        def sem(name):
            return ctx.enter_context(nc.semaphore("f_" + name))

        def pb(name):
            return ctx.enter_context(nc.psum_tensor("f_" + name, [P, 512], F32))

        ident = sb("ident", [P, P])
        ident16 = sb("ident16", [P, P], BF16)
        desc = sb("desc", [P, E])
        a_raw = sb("a_raw", [P, KT, NU])
        a_hi = sb("a_hi", [P, KT, NU], F32R)
        a_lo = sb("a_lo", [P, KT, NU], F32R)
        b2_raw = sb("b2_raw", [P, D])
        b2_hi = sb("b2_hi", [P, D], F32R)
        b2_lo = sb("b2_lo", [P, D], F32R)
        w_raw = sb("w_raw", [P, RAW, UP + DOWN])
        up_hi = sb("up_hi", [P, 2, UP], F32R)
        up_lo = sb("up_lo", [P, 2, UP], F32R)
        down_hi = sb("down_hi", [P, 3, DOWN], F32R)
        down_lo = sb("down_lo", [P, 3, DOWN], F32R)
        x2 = sb("x2", [P, TT, D])
        xT_hi = sb("xT_hi", [P, KT, T], F32R)
        xT_lo = sb("xT_lo", [P, KT, T], F32R)
        logits = sb("logits", [P, TT, E])
        pick = sb("pick", [P, 4, TT, E])
        best = sb("best", [P, 4, TT])
        soft = sb("soft", [P, 4, TT])
        weight = sb("weight", [P, 2, TT])
        coef = sb("coef", [P, 2, TT, E])
        masks = sb("masks", [P, 2, TT, E, R], BF16)
        weight_bc = sb("weight_bc", [P, 2, TT, P])
        um = sb("um", [P, TT, 2, 2, P])
        umT_hi = sb("umT_hi", [P, 4, T], F32R)
        umT_lo = sb("umT_lo", [P, 4, T], F32R)
        maskT = sb("maskT", [P, 2, T], BF16)
        weightT = sb("weightT", [P, 2, T])
        silu = sb("silu", [P, 2, T])
        gated = sb("gated", [P, 2, T])
        act = sb("act", [P, 3, T])
        act_hi = sb("act_hi", [P, 2, T], F32R)
        act_lo = sb("act_lo", [P, 2, T], F32R)
        zm = sb("zm", [P, 3, T])
        z_hi = sb("z_hi", [P, T], F32R)
        z_lo = sb("z_lo", [P, T], F32R)
        x3 = sb("x3", [P, TT, D])
        stats = sb("stats", [P, TT, 6])
        part = sb("part", [P, TT, 5])
        mean = sb("mean", [P, TT])
        rstd = sb("rstd", [P, 3, TT])

        h_ps = [pb("h1"), pb("h3")]
        z_ps = [pb("z_sum"), pb("z_second")]
        bank = [pb(f"y{i}") for i in range(YB)]

        consts_loaded = sem("consts_loaded")
        consts_ready = sem("consts_ready")
        x2_loaded = sem("x2_loaded")
        streamed = [sem(f"streamed{i}") for i in range(RAW)]
        w_hi_ready = sem("w_hi_ready")
        w_lo_ready = sem("w_lo_ready")
        filled = [sem(f"filled{i}") for i in range(YB)]
        drained = [sem(f"drained{i}") for i in range(YB)]
        xT_hi_ready = sem("xT_hi_ready")
        step_done = sem("step_done")
        gap_ready = sem("gap_ready")
        exp_ready = sem("exp_ready")
        weight_ready = sem("weight_ready")
        masks_ready = sem("masks_ready")
        um_hi_ready = sem("um_hi_ready")
        h_ready = [sem("h1_ready"), sem("h3_ready")]
        silu_ready = sem("silu_ready")
        gated_ready = sem("gated_ready")
        act_ready = sem("act_ready")
        sum_ready = sem("sum_ready")
        act_hi_ready = sem("act_hi_ready")
        act_lo_ready = sem("act_lo_ready")
        y_done = sem("y_done")
        z_done = sem("z_done")
        z_masked = sem("z_masked")
        z_summed = sem("z_summed")
        z_hi_ready = sem("z_hi_ready")
        z_lo_ready = sem("z_lo_ready")
        var_ready = sem("var_ready")
        std_ready = sem("std_ready")
        normed = sem("normed")
        out_stored = sem("out_stored")

        def slot(b, n):
            return n % YB, b * Y_TOTAL[n % YB] + n // YB

        def y_slot(b, t):
            return t, b * Y_TOTAL[t] + Y_BEFORE[t]

        def tiles(b, f):
            return b * FT + f + 1

        block = ctx.enter_context(nc.Block())

        @block.sync
        def _(sp):
            for dst, src in ((ident[:, :], ident_in), (desc[:, :], descending),
                             (a_raw[:, :, :], a13g.rearrange("(k p) n -> p k n", p=P)), (b2_raw[:, :], b2T)):
                sp.dma_start(dst, src).then_inc(consts_loaded, 16)
            with sp.Fori(0, B) as b:
                sp.wait_ge(drained[TT - 1], b * Y_TOTAL[TT - 1])
                sp.dma_start(x2[:, :, :], x2_dram[bass.ts(b, T), :].rearrange("(t p) d -> p t d", p=P))\
                    .then_inc(x2_loaded, 16)
                sp.wait_ge(normed, b * TT + TT)
                sp.dma_start(out_dram[bass.ts(b, T), :].rearrange("(t p) d -> p t d", p=P), x3[:, :, :])\
                    .then_inc(out_stored, 16)
            sp.wait_ge(out_stored, 16 * B)

        @block.gpsimd
        def _(pool):
            def gate(b, f, choice):
                n = 2 * (tiles(b, f) - 1) + choice
                pool.wait_ge(silu_ready, n + 1)
                pool.wait_ge(act_ready, 2 * (tiles(b, f) - 1))
                pool.tensor_tensor(gated[:, choice, :], silu[:, choice, :], weightT[:, choice, :], ALU.mult)\
                    .then_inc(gated_ready, 1)

            def total(b, f):
                pool.wait_ge(act_ready, 2 * tiles(b, f))
                pool.wait_ge(act_lo_ready, 2 * (tiles(b, f) - 1))
                pool.tensor_tensor(act[:, 2, :], act[:, 0, :], act[:, 1, :], ALU.add).then_inc(sum_ready, 1)

            def split_lo(b, f):
                pool.wait_ge(w_hi_ready, 2 * tiles(b, f))
                r = f % RAW
                for dst, hi, cols in ((up_lo[:, f % 2, :], up_hi[:, f % 2, :], slice(0, UP)),
                                      (down_lo[:, f % 3, :], down_hi[:, f % 3, :], slice(UP, UP + DOWN))):
                    pool.tensor_tensor(dst, w_raw[:, r, cols], hi.bitcast(F32), ALU.subtract)\
                        .then_inc(w_lo_ready, 1)

            with pool.Fori(0, B) as b:
                for f in range(2):
                    split_lo(b, f)
                for k in range(2):
                    kk, n = slot(b, WB0 + k)
                    pool.wait_ge(drained[kk], n + 1)
                for f in range(FT):
                    gate(b, f, 0)
                    gate(b, f, 1)
                    total(b, f)
                    if f + 2 < FT:
                        split_lo(b, f + 2)

        @block.scalar
        def _(sc):
            def fetch(b, f):
                r = f % RAW
                before = b * FT + f - RAW + 1
                if f >= RAW:
                    sc.wait_ge(w_lo_ready, 2 * before)
                else:
                    sc.wait_ge(w_lo_ready, 2 * b * FT)
                sc.dma_start(w_raw[:, r, :], stream[f, :, :]).then_inc(streamed[r], 16)

            PER = [len(range(r, FT, RAW)) for r in range(RAW)]

            def split_hi(b, f):
                r = f % RAW
                sc.wait_ge(streamed[r], 16 * (b * PER[r] + f // RAW + 1))
                if f >= 2:
                    sc.wait_ge(h_ready[1], 2 * (tiles(b, f) - 2))
                else:
                    sc.wait_ge(h_ready[1], 2 * b * FT)
                sc.activation(up_hi[:, f % 2, :], w_raw[:, r, 0:UP], ACT.Copy).then_inc(w_hi_ready, 1)
                if f >= 3:
                    sc.wait_ge(z_done, tiles(b, f) - 3)
                else:
                    sc.wait_ge(z_done, b * FT)
                sc.activation(down_hi[:, f % 3, :], w_raw[:, r, UP:UP + DOWN], ACT.Copy).then_inc(w_hi_ready, 1)

            sc.wait_ge(consts_loaded, 64)
            sc.activation(a_hi[:, :, :], a_raw[:, :, :], ACT.Copy).then_inc(consts_ready, 1)
            sc.activation(b2_hi[:, :], b2_raw[:, :], ACT.Copy).then_inc(consts_ready, 1)
            with sc.Fori(0, B) as b:
                for f in range(RAW):
                    fetch(b, f)
                for c in range(KT):
                    k, n = slot(b, XC0 + c)
                    sc.wait_ge(filled[k], n + 1)
                    sc.activation(xT_hi[:, c, :], bank[k][:, :], ACT.Copy).then_inc(xT_hi_ready, 1)
                for f in range(2):
                    split_hi(b, f)
                sc.wait_ge(gap_ready, b + 1)
                sc.activation(soft[:, 1, :], soft[:, 0, :], ACT.Exp).then_inc(exp_ready, 1)
                for a in range(4):
                    k, n = slot(b, UM0 + a)
                    sc.wait_ge(filled[k], n + 1)
                    sc.activation(umT_hi[:, a, :], bank[k][:, :], ACT.Copy).then_inc(um_hi_ready, 1)
                k, n = slot(b, MT)
                sc.wait_ge(filled[k], n + 1)
                sc.activation(maskT[:, :, :], bank[k][:, :].bitcast(BF16).rearrange("p (a t) -> p a t", a=2),
                              ACT.Copy).then_inc(drained[k], 1)
                for a in range(2):
                    k, n = slot(b, WB0 + a)
                    sc.wait_ge(filled[k], n + 1)
                    sc.activation(weightT[:, a, :], bank[k][:, :], ACT.Copy).then_inc(drained[k], 1)
                for f in range(FT):
                    if f + RAW < FT:
                        fetch(b, f + RAW)
                    for choice in range(2):
                        n = 2 * (tiles(b, f) - 1) + choice
                        sc.wait_ge(h_ready[0], n + 1)
                        sc.wait_ge(gated_ready, 2 * (tiles(b, f) - 1))
                        sc.activation(silu[:, choice, :], h_ps[0][:, :], ACT.Silu).then_inc(silu_ready, 1)
                    sc.wait_ge(z_done, tiles(b, f) - 1)
                    sc.wait_ge(act_ready, 2 * tiles(b, f))
                    sc.activation(act_hi[:, 0, :], act[:, 1, :], ACT.Copy).then_inc(act_hi_ready, 1)
                    sc.wait_ge(sum_ready, tiles(b, f))
                    sc.activation(act_hi[:, 1, :], act[:, 2, :], ACT.Copy).then_inc(act_hi_ready, 1)
                    if f + 2 < FT:
                        split_hi(b, f + 2)
                sc.wait_ge(z_summed, b + 1)
                sc.activation(z_hi[:, :], zm[:, 2, :], ACT.Copy).then_inc(z_hi_ready, 1)
                sc.wait_ge(var_ready, b + 1)
                sc.activation(rstd[:, 1, :], rstd[:, 0, :], ACT.Sqrt).then_inc(std_ready, 1)

        @block.vector
        def _(dve):
            dve.wait_ge(consts_loaded, 64)
            dve.tensor_copy(ident16[:, :], ident[:, :]).then_inc(consts_ready, 1)
            dve.wait_ge(consts_ready, 3)
            dve.tensor_tensor(a_lo[:, :, :], a_raw[:, :, :], a_hi[:, :, :].bitcast(F32), ALU.subtract)\
                .then_inc(consts_ready, 1)
            dve.tensor_tensor(b2_lo[:, :], b2_raw[:, :], b2_hi[:, :].bitcast(F32), ALU.subtract)\
                .then_inc(consts_ready, 1)
            with dve.Fori(0, B) as b:
                links = 19
                done = [0]

                def link(ins):
                    done[0] += 1
                    ins.then_inc(step_done, 1)
                    dve.wait_ge(step_done, b * links + done[0])

                for c in range(KT):
                    k, n = slot(b, XC0 + c)
                    dve.wait_ge(xT_hi_ready, b * KT + c + 1)
                    dve.tensor_tensor(xT_lo[:, c, :], bank[k][:, :], xT_hi[:, c, :].bitcast(F32), ALU.subtract)\
                        .then_inc(drained[k], 1)
                for t in range(TT):
                    k, n = slot(b, U0 + t)
                    dve.wait_ge(filled[k], n + 1)
                    last = dve.tensor_copy(logits[:, t, :], bank[k][:, 2 * P:NU])
                link(last)

                def one_hot(values, m, where):
                    link(dve.tensor_reduce(best[:, m, :], values, AX.X, ALU.max))
                    link(dve.tensor_tensor(where, values, best[:, m, :].unsqueeze(2).to_broadcast([P, TT, E]),
                                           ALU.is_equal))
                    link(dve.tensor_tensor(where, where, desc[:, :].unsqueeze(1).to_broadcast([P, TT, E]), ALU.mult))
                    link(dve.tensor_reduce(best[:, m + 1, :], where, AX.X, ALU.max))
                    link(dve.tensor_tensor(where, where, best[:, m + 1, :].unsqueeze(2).to_broadcast([P, TT, E]),
                                           ALU.is_equal))

                one_hot(logits[:, :, :], 0, pick[:, 1, :, :])
                link(dve.scalar_tensor_tensor(pick[:, 2, :, :], pick[:, 1, :, :], FAR, logits[:, :, :],
                                              ALU.mult, ALU.add))
                one_hot(pick[:, 2, :, :], 2, pick[:, 3, :, :])
                dve.tensor_tensor(soft[:, 0, :], best[:, 2, :], best[:, 0, :], ALU.subtract).then_inc(gap_ready, 1)
                link(dve.tensor_tensor(pick[:, 0, :, :], pick[:, 3, :, :], pick[:, 1, :, :], ALU.subtract))
                for a in range(2):
                    last = dve.tensor_scalar(coef[:, a, :, :], pick[:, 1 - a, :, :], LORA_SCALE, None, ALU.mult)
                link(last)
                for a in range(2):
                    dve.tensor_copy(masks[:, a, :, :, :],
                                    coef[:, a, :, :].unsqueeze(3).to_broadcast([P, TT, E, R])).then_inc(masks_ready, 1)
                for t in range(TT):
                    k, n = slot(b, U0 + t)
                    for a in range(2):
                        ins = dve.tensor_tensor(
                            um[:, t, a, :, :].rearrange("p s (e r) -> p s e r", e=E),
                            bank[k][:, 0:2 * P].rearrange("p (s e r) -> p s e r", s=2, e=E),
                            coef[:, a, t, :].unsqueeze(1).unsqueeze(3).to_broadcast([P, 2, E, R]), ALU.mult)
                    ins.then_inc(drained[k], 1)
                dve.wait_ge(exp_ready, b + 1)
                link(dve.tensor_scalar(soft[:, 2, :], soft[:, 1, :], 1.0, None, ALU.add))
                dve.reciprocal(weight[:, 0, :], soft[:, 2, :]).then_inc(weight_ready, 1)
                dve.wait_ge(weight_ready, 3 * b + 1)
                dve.tensor_tensor(weight[:, 1, :], soft[:, 1, :], weight[:, 0, :], ALU.mult).then_inc(weight_ready, 1)
                dve.wait_ge(weight_ready, 3 * b + 2)
                dve.tensor_copy(weight_bc[:, :, :, :], weight[:, :, :].unsqueeze(3).to_broadcast([P, 2, TT, P]))\
                    .then_inc(weight_ready, 1)
                for a in range(4):
                    k, n = slot(b, UM0 + a)
                    dve.wait_ge(um_hi_ready, b * 4 + a + 1)
                    dve.tensor_tensor(umT_lo[:, a, :], bank[k][:, :], umT_hi[:, a, :].bitcast(F32), ALU.subtract)\
                        .then_inc(drained[k], 1)
                for f in range(FT):
                    for choice in range(2):
                        n = 2 * (tiles(b, f) - 1) + choice
                        dve.wait_ge(gated_ready, n + 1)
                        dve.wait_ge(h_ready[1], n + 1)
                        dve.wait_ge(sum_ready, tiles(b, f) - 1)
                        dve.tensor_tensor(act[:, choice, :], h_ps[1][:, :], gated[:, choice, :], ALU.mult)\
                            .then_inc(act_ready, 1)
                    for i in range(2):
                        dve.wait_ge(act_hi_ready, 2 * (tiles(b, f) - 1) + i + 1)
                        dve.tensor_tensor(act_lo[:, i, :], act[:, 1 + i, :], act_hi[:, i, :].bitcast(F32),
                                          ALU.subtract).then_inc(act_lo_ready, 1)
                dve.wait_ge(z_done, b * FT + FT)
                for i in range(2):
                    dve.tensor_tensor(zm[:, i, :], z_ps[i][:, :], maskT[:, i, :], ALU.mult).then_inc(z_masked, 1)
                dve.wait_ge(z_masked, 2 * b + 2)
                dve.tensor_tensor(zm[:, 2, :], zm[:, 0, :], zm[:, 1, :], ALU.add).then_inc(z_summed, 1)
                dve.wait_ge(z_hi_ready, b + 1)
                dve.tensor_tensor(z_lo[:, :], zm[:, 2, :], z_hi[:, :].bitcast(F32), ALU.subtract)\
                    .then_inc(z_lo_ready, 1)
                dve.wait_ge(out_stored, 16 * b)
                for t in range(TT):
                    k, n = y_slot(b, t)
                    dve.wait_ge(filled[k], n + 1)
                    dve.tensor_tensor(x3[:, t, :], bank[k][:, :], x2[:, t, :], ALU.add).then_inc(drained[k], 1)
                    dve.wait_ge(drained[k], n + 1)
                    last = dve.bn_stats(stats[:, t, :], x3[:, t, :])
                link(last)
                moments(dve, stats, part, mean[:, :], rstd[:, 0, :], link).then_inc(var_ready, 1)
                dve.wait_ge(std_ready, b + 1)
                link(dve.reciprocal(rstd[:, 2, :], rstd[:, 1, :]))
                for t in range(TT):
                    dve.tensor_scalar(x3[:, t, :], x3[:, t, :], mean[:, t:t + 1], rstd[:, 2, t:t + 1],
                                      ALU.subtract, ALU.mult).then_inc(normed, 1)
                assert done[0] == links

        @block.tensor
        def _(pe):
            def up(b, f, i):
                if i == 0:
                    pe.wait_ge(w_lo_ready, 2 * tiles(b, f) - 1)
                    pe.wait_ge(silu_ready, 2 * (tiles(b, f) - 1))
                else:
                    pe.wait_ge(act_ready, 2 * (tiles(b, f) - 1))
                s = f % 2
                for c in range(KT):
                    cols = slice(i * D + c * P, i * D + (c + 1) * P)
                    matmul_split(pe, h_ps[i][:, :], up_hi[:, s, cols], up_lo[:, s, cols],
                                 xT_hi[:, c, :], xT_lo[:, c, :], c == 0, False)
                cols = slice(2 * D + i * P, 2 * D + (i + 1) * P)
                matmul_split(pe, h_ps[i][:, :], up_hi[:, s, cols], up_lo[:, s, cols],
                             umT_hi[:, i, :], umT_lo[:, i, :], False, True).then_inc(h_ready[i], 1)

            def second(b, f, i):
                if i == 0:
                    pe.wait_ge(silu_ready, 2 * tiles(b, f) - 1)
                else:
                    pe.wait_ge(act_ready, 2 * tiles(b, f) - 1)
                s = f % 2
                cols = slice(2 * D + i * P, 2 * D + (i + 1) * P)
                rhs = 2 + i
                last = None
                for l, r in ((up_hi, umT_hi), (up_lo, umT_hi), (up_hi, umT_lo)):
                    last = pe.matmul(h_ps[i][:, :], l[:, s, cols], r[:, rhs, :], start=False, stop=True,
                                     skip_group_check=True)
                last.then_inc(h_ready[i], 1)

            def down(b, f):
                pe.wait_ge(act_lo_ready, 2 * tiles(b, f))
                pe.wait_ge(w_lo_ready, 2 * tiles(b, f))
                s = f % 3
                for t in range(TT):
                    matmul_split(pe, bank[t][:, :], act_hi[:, 1, bass.ts(t, P)], act_lo[:, 1, bass.ts(t, P)],
                                 down_hi[:, s, P:DOWN], down_lo[:, s, P:DOWN], f == 0, False)

            def adapters(b, f):
                s = f % 3
                for i in (1, 0):
                    last = matmul_split(pe, z_ps[i][:, :], down_hi[:, s, 0:P], down_lo[:, s, 0:P],
                                        act_hi[:, 1 - i, :], act_lo[:, 1 - i, :], f == 0, f == FT - 1)
                last.then_inc(z_done, 1)

            pe.wait_ge(consts_ready, 5)
            with pe.Fori(0, B) as b:
                pe.wait_ge(x2_loaded, 16 * b + 16)
                for c in range(KT):
                    k, n = slot(b, XC0 + c)
                    pe.wait_ge(drained[k], n)
                    for t in range(TT):
                        last = pe.transpose(bank[k][:, bass.ts(t, P)], x2[:, t, bass.ts(c, P)], ident[:, :])
                    last.then_inc(filled[k], 1)
                for c in range(KT):
                    k, n = slot(b, XC0 + c)
                    pe.wait_ge(drained[k], n + 1)
                for t in range(TT):
                    k, n = slot(b, U0 + t)
                    for c in range(KT):
                        last = matmul_split(pe, bank[k][:, 0:NU], xT_hi[:, c, bass.ts(t, P)],
                                            xT_lo[:, c, bass.ts(t, P)], a_hi[:, c, :], a_lo[:, c, :],
                                            c == 0, c == KT - 1)
                    last.then_inc(filled[k], 1)
                for t in range(TT):
                    k, n = slot(b, U0 + t)
                    pe.wait_ge(drained[k], n + 1)
                for a in range(4):
                    k, n = slot(b, UM0 + a)
                    for t in range(TT):
                        last = pe.transpose(bank[k][:, bass.ts(t, P)], um[:, t, a // 2, a % 2, :], ident[:, :])
                    last.then_inc(filled[k], 1)
                k, n = slot(b, MT)
                pe.wait_ge(masks_ready, 2 * b + 2)
                pe.wait_ge(drained[k], n)
                half = bank[k][:, :].bitcast(BF16).rearrange("p (a t m) -> p a t m", a=2, t=TT)
                for a in range(2):
                    for t in range(TT):
                        last = pe.transpose(half[:, a, t, :], masks[:, a, t, :, :].rearrange("p e r -> p (e r)"),
                                            ident16[:, :])
                last.then_inc(filled[k], 1)
                pe.wait_ge(weight_ready, 3 * b + 3)
                for a in range(2):
                    k, n = slot(b, WB0 + a)
                    pe.wait_ge(drained[k], n)
                    for t in range(TT):
                        last = pe.matmul(bank[k][:, bass.ts(t, P)], weight_bc[:, a, t, :], ident[:, :],
                                         start=True, stop=True)
                    last.then_inc(filled[k], 1)
                for a in range(4):
                    k, n = slot(b, UM0 + a)
                    pe.wait_ge(drained[k], n + 1)
                for f in range(FT + 1):
                    if f < FT:
                        up(b, f, 0)
                        up(b, f, 1)
                    if f:
                        if f == 1:
                            for t in range(TT):
                                k, n = y_slot(b, t)
                                pe.wait_ge(drained[k], n)
                        down(b, f - 1)
                    if f < FT:
                        second(b, f, 0)
                        second(b, f, 1)
                    if f:
                        adapters(b, f - 1)
                pe.wait_ge(z_lo_ready, b + 1)
                for t in range(TT):
                    k, n = y_slot(b, t)
                    matmul_split(pe, bank[k][:, :], z_hi[:, bass.ts(t, P)], z_lo[:, bass.ts(t, P)],
                                 b2_hi[:, :], b2_lo[:, :], False, True).then_inc(filled[k], 1)



def decoder_layer(nc, a, out):
    x1 = nc.dram_tensor("x1_scratch", (B * T, D), F32, kind="Internal").ap()
    x2 = nc.dram_tensor("x2_scratch", (B * T, D), F32, kind="Internal").ap()
    attention(nc, a["xT"], a["x"], a["wT"], a["biases"], a["bo"], a["rope"], a["head_mask"], a["ident"], x1)
    experts(nc, x1, a["w1"], a["w2"], a["ident"], x2)
    mixture(nc, x2, a["a13g"], a["stream"], a["b2T"], a["ident"], a["descending"], out)



def host_arrays(inputs):
    import numpy as np
    x = np.ascontiguousarray(inputs["x"]).reshape(B * T, D)
    pos = np.arange(T, dtype=np.float32)
    inv = (1.0 / 10000.0 ** (np.arange(0, DK, 2, dtype=np.float32) / DK)).astype(np.float32)
    ang = pos[:, None] * inv[None, :]
    sin, cos = np.sin(ang), np.cos(ang)
    rope = np.empty((P, 2, TT, DK), np.float32)
    rope[:, 0] = np.repeat(cos, 2, axis=1).reshape(TT, P, DK).transpose(1, 0, 2)
    rope[:, 1] = np.stack([-sin, sin], axis=-1).reshape(TT, P, DK).transpose(1, 0, 2)
    mask = np.zeros((P, GH, E1), np.float32)
    for j in range(GH):
        mask[j * DK:(j + 1) * DK, j] = 1.0
    ffn = {k[7:]: np.asarray(v) for k, v in inputs.items() if k.startswith("L0_ffn")}
    stream = np.empty((FT, P, UP + DOWN), np.float32)
    for i, w in enumerate(("w1", "w3")):
        stream[:, :, i * D:(i + 1) * D] = ffn[w].reshape(FT, P, KT, P).transpose(0, 3, 2, 1).reshape(FT, P, D)
    for i, w in enumerate(("b1", "b3")):
        stream[:, :, 2 * D + i * P:2 * D + (i + 1) * P] = \
            ffn[w].transpose(0, 2, 1).reshape(P, FT, P).transpose(1, 0, 2)
    stream[:, :, UP:UP + P] = ffn["a2"].reshape(P, FT, P).transpose(1, 2, 0)
    stream[:, :, UP + P:] = ffn["w2"].T.reshape(FT, P, D)
    return dict(
        stream=stream,
        a13g=np.concatenate([ffn["a1"].reshape(P, D), ffn["a3"].reshape(P, D), ffn["gate_w"]]).T.copy(),
        b2T=np.ascontiguousarray(ffn["b2"].transpose(0, 2, 1).reshape(P, D)),
        descending=np.ascontiguousarray(np.broadcast_to(np.arange(E, 0, -1, dtype=np.float32), (P, E))),
        xT=np.ascontiguousarray(x.T), x=x,
        wT=np.stack([inputs[f"L0_attn_W{c}"].T for c in "qkvgo"]),
        biases=np.stack([inputs[f"L0_attn_b{c}"] for c in "qkvg"])[None],
        bo=np.ascontiguousarray(np.broadcast_to(inputs["L0_attn_bo"], (P, D))),
        w1=np.ascontiguousarray(inputs["fside_BxS2xS2_0"].reshape(B * D, D)),
        w2=np.ascontiguousarray(inputs["ctx_1024"].reshape(B * D, D // 2)),
        rope=rope, head_mask=mask.reshape(P, GE), ident=np.eye(P, dtype=np.float32))


def kernel(**inputs):
    import concourse.bacc as bacc
    from concourse.bass_utils import run_bass_kernel_spmd

    nc = bacc.Bacc("TRN2", target_bir_lowering=False, num_devices=1)
    arrays = host_arrays(inputs)
    a = {name: nc.dram_tensor("in_" + name, v.shape, mybir.dt.from_np(v.dtype), kind="ExternalInput").ap()
         for name, v in arrays.items()}
    out = nc.dram_tensor("out", (B * T, D), F32, kind="ExternalOutput").ap()
    decoder_layer(nc, a, out)
    r = run_bass_kernel_spmd(nc, [{"in_" + name: v for name, v in arrays.items()}], core_ids=[0])
    return r.results[0]["out"].reshape(B, T, D)
```

```python
from contextlib import ExitStack

import concourse.bass as bass
from concourse import mybir

F32 = mybir.dt.float32
F32R = mybir.dt.float32r
BF16 = mybir.dt.bfloat16
ALU = mybir.AluOpType
ACT = mybir.ActivationFunctionType
AX = mybir.AxisListType

P = 128
B = 4
T = 512
D = 512
H = 16
DK = D // H
CS = 64
TT = T // P
KT = D // P
GH = P // DK
NG = H // GH
E1 = DK + 1
GE = GH * E1
LN_EPS = 1e-5
DEN_EPS = 1e-6

Q_EPS = 1e-6
QMAX = 127.0
ROUND = 1.5 * 2.0 ** 23
CHANNELS = (D, D // 2)

PRIMED = 1

RING = 4
QT, PQ, PK, PV, AT, PG, OUT = ("qT", "q", "k", "v", "attT", "gate", "out")
MX, MW, RS, SS, XT0, XT1, SW, WT0, WT1 = ("amax_x", "amax_w", "1/s", "s", "xT0", "xT1", "w_scale", "wT0", "wT1")
OX = tuple(f"out{t}" for t in range(TT))


def section(t):
    linear, second = divmod(t, 2)
    half = ((MX, MW), (RS, SS)) if not second else \
        (((XT0, XT1, SW, WT0, WT1), (XT0, SW, WT0))[linear], OX)
    own = [(t, QT), (t + 1, PQ), (t + 1, PK), (t + 1, PV)]
    own += [(linear, item) for item in half[0]]
    own += [(t, AT), (t + 1, PG), (t, OUT)]
    return own + [(linear, item) for item in half[1]]


ORDER = [item for t in range(TT) for item in section(t)]
PER_BANK = len(ORDER) // RING
ATTENTION_ITEMS = (QT, PQ, PK, PV, AT, PG, OUT)


def present(iteration, place):
    t, item = ORDER[place]
    if item not in ATTENTION_ITEMS:
        return 1 <= iteration <= B
    if item in (PQ, PK, PV, PG):
        return 0 <= iteration * TT + t < B * TT
    return 0 <= iteration < B


def ring_steps():
    steps, value = {}, [0] * RING
    for iteration in range(-1, B + 1):
        for k in range(RING):
            there = [n for n in range(k, len(ORDER), RING) if present(iteration, n)]
            for n in there:
                after = (iteration + 1) * PER_BANK + (PER_BANK if n == there[-1] else n // RING + 1)
                steps[iteration, n] = (value[k], after - value[k])
                value[k] = after
    return steps


STEPS = ring_steps()
CONSTS = 16 * 7


def matmul_split(pe, out, lhs_hi, lhs_lo, rhs_hi, rhs_lo, start, stop):
    pe.matmul(out, lhs_hi, rhs_hi, start=start, stop=False)
    pe.matmul(out, lhs_lo, rhs_hi, start=False, stop=False)
    return pe.matmul(out, lhs_hi, rhs_lo, start=False, stop=stop)


def moments(dve, stats, part, mean, var_eps, wait):
    dve.tensor_tensor(part[:, :, 0:2], stats[:, :, 1:3], stats[:, :, 4:6], ALU.add)
    wait(dve.tensor_tensor(part[:, :, 2], stats[:, :, 1], stats[:, :, 4], ALU.subtract))
    dve.tensor_scalar(mean, part[:, :, 0], 0.5, None, ALU.mult)
    dve.tensor_scalar(part[:, :, 3], part[:, :, 1], 1.0 / D, LN_EPS, ALU.mult, ALU.add)
    wait(dve.scalar_tensor_tensor(part[:, :, 4], part[:, :, 2], 0.25, part[:, :, 2], ALU.mult, ALU.mult))
    return dve.tensor_tensor(var_eps, part[:, :, 3], part[:, :, 4], ALU.add)


def attention_and_experts(nc, xT, x, wT, bias_rows, bias_parts, bias_pick, bo, rope, head_mask, ident_in,
                          w1, w2, x2_dram):
    with ExitStack() as ctx:
        def sb(name, shape, dt=F32):
            return ctx.enter_context(nc.sbuf_tensor(name, shape, dt))

        primed = []

        def sem(name):
            primed.append(ctx.enter_context(nc.semaphore(name)))
            return primed[-1]

        def sems(name):
            return [sem(name + "1"), sem(name + "2")]

        w_raw = sb("w_raw", [P, KT, D])
        w_hi = sb("w_hi", [P, 5, KT, D], F32R)
        w_lo = sb("w_lo", [P, 5, KT, D], F32R)
        bias_hl = sb("bias_hl", [P, D], F32R)
        bias_part = sb("bias_part", [P, 2])
        pick = sb("pick", [P, 4, P], F32R)
        ident = sb("ident", [P, P])
        ident16 = sb("ident16", [P, P], BF16)
        ones = sb("ones", [P, P])
        mask = sb("mask", [P, GE])
        ropes = sb("ropes", [P, 2, TT, DK])
        bo_bc = sb("bo_bc", [P, D])
        x_tok = sb("x_tok", [P, TT, D])
        stats = sb("stats", [P, TT, 6])
        part = sb("part", [P, TT, 5])
        mean = sb("mean", [P, TT])
        rstd = sb("rstd", [P, 3, TT])
        xT_raw = sb("xT_raw", [P, 2, KT, P])
        xT_hi = sb("xT_hi", [P, 2, KT, P], F32R)
        xT_lo = sb("xT_lo", [P, 2, KT, P], F32R)
        qk = sb("qk", [P, 2 * D])
        rot_a = sb("rot_a", [P, 2 * D])
        rot_b = sb("rot_b", [P, 2 * D])
        feat = sb("feat", [P, 2 * D])
        v_ext = sb("v_ext", [P, 2, H, E1])
        gate = sb("gate", [P, D])
        q_T = sb("q_T", [P, NG, P])
        s_bd = sb("s_bd", [P, 2, NG, GE])
        rden = sb("rden", [P, 2, H])
        att = sb("att", [P, D])
        att_hi = sb("att_hi", [P, KT, P], F32R)
        att_lo = sb("att_lo", [P, KT, P], F32R)
        x1 = sb("x1", [P, TT, D])
        top = sb("top", [P, 2, D])
        diag = top[:, :, :].rearrange("p i (c t) -> p i c t", t=P)
        amax = sb("amax", [P, 2, KT])
        small = sb("small", [P, 4, KT])
        rows = sb("rows", [P, 2, D])
        row_max = sb("row_max", [P, 2, TT])
        scale = sb("scale", [P, 2, TT])
        inverse = sb("inverse", [P, 2, TT])
        scaled = [sb("scaled_x", [P, TT, D]), sb("scaled_w", [P, TT, D])]
        q = [sb("qx", [P, TT, D], BF16), sb("qw", [P, TT, D], BF16)]
        qT = [sb("qxT", [P, KT, T], BF16), sb("qwT", [P, KT, D], BF16)]
        gu = scaled[0]
        sl = scaled[1]
        act_in = sb("act_in", [P, TT, D // 2])
        e_stats = stats
        e_part = sb("e_part", [P, TT, 5])
        e_mean = sb("e_mean", [P, TT])
        e_rstd = sb("e_rstd", [P, 3, TT])

        ring = [ctx.enter_context(nc.psum_tensor(f"ring{i}", [P, 512], F32)) for i in range(RING)]
        s_ps = ctx.enter_context(nc.psum_tensor("s_ps", [P, 2, 512], F32))
        n_ps = ctx.enter_context(nc.psum_tensor("n_ps", [P, 2, 512], F32))

        consts_loaded = sem("consts_loaded")
        w_loaded = sem("w_loaded")
        w_hi_ready = sem("w_hi_ready")
        w_lo_ready = sem("w_lo_ready")
        bias_hi_ready = sem("bias_hi_ready")
        bias_ready = sem("bias_ready")
        ones_ready = sem("ones_ready")
        v_ones_ready = sem("v_ones_ready")
        xT_loaded = sems("xT_loaded")
        x_loaded = sem("x_loaded")
        xhi_ready = sem("xhi_ready")
        xlo_ready = sem("xlo_ready")
        filled = [sem(f"filled{i}") for i in range(RING)]
        drained = [sem(f"drained{i}") for i in range(RING)]
        rot_a_ready = sem("rot_a_ready")
        rot_b_ready = sem("rot_b_ready")
        rotated = sem("rotated")
        neg_ready = sem("neg_ready")
        exp_ready = sem("exp_ready")
        feat_ready = sem("feat_ready")
        s_updated = sem("s_updated")
        s_masked = sem("s_masked")
        num_ready = sem("num_ready")
        den_ready = sem("den_ready")
        rden_ready = sem("rden_ready")
        gated = sem("gated")
        att_ready = sem("att_ready")
        att_hi_ready = sem("att_hi_ready")
        xres_ready = sem("xres_ready")
        stats_ready = sem("stats_ready")
        moment_ready = sem("moment_ready")
        var_ready = sem("var_ready")
        std_ready = sem("std_ready")
        rstd_ready = sem("rstd_ready")
        normed = sem("normed")
        ew_loaded = sems("ew_loaded")
        top_ready = sems("top_ready")
        small_done = sem("small_done")
        ratio_ready = sems("ratio_ready")
        root_ready = sems("root_ready")
        s_ready = sems("s_ready")
        diag_ready = sems("diag_ready")
        scaled_ready = sems("scaled_ready")
        scale_ready = sems("scale_ready")
        sw_diag_ready = sems("sw_diag_ready")
        shifted = sems("shifted")
        clamped = sems("clamped")
        q_ready = sems("q_ready")
        silu_ready = sem("silu_ready")
        act_ready = sem("act_ready")
        summed = sem("summed")
        e_stats_ready = sem("e_stats_ready")
        e_moment_ready = sem("e_moment_ready")
        e_var_ready = sem("e_var_ready")
        e_std_ready = sem("e_std_ready")
        e_rstd_ready = sem("e_rstd_ready")
        e_normed = sem("e_normed")
        x2_stored = sem("x2_stored")

        def place(iteration, key):
            n = ORDER.index(key)
            if isinstance(iteration, int):
                before, step = STEPS[iteration, n]
            else:
                before, step = (iteration + 1) * PER_BANK + n // RING, 1
            return n % RING, before, before + step, step

        def slot(b, t, item):
            if item in (PQ, PK, PV, PG):
                return place(b - 1, (TT, item)) if t == 0 else place(b, (t, item))
            return place(b, (t, item))

        def tile_no(b, t):
            return b * TT + t + 1

        def ahead(b, t, n):
            return b + (t + n) // TT, (t + n) % TT

        def following(b, t):
            return ahead(b, t, 1)

        def exists(b, t):
            return not isinstance(b, int) or tile_no(b, t) <= B * TT

        def has_next(b, t):
            return exists(*following(b, t))

        def has_expert(b):
            return not isinstance(b, int) or b > 0

        def iterations(eng, body):
            body(0)
            with eng.Fori(1, B - 1) as b:
                body(b)
            body(B - 1)

        def expert_tokens(i, which):
            return (x1, act_in)[which] if i == 0 else w_raw

        with nc.Block() as start:
            @start.gpsimd
            def _(pool):
                for semaphore in primed:
                    pool.sem_inc(semaphore, PRIMED)

        block = ctx.enter_context(nc.Block())

        @block.sync
        def _(sp):
            for t in range(2):
                sp.dma_start(xT_raw[:, t, :, :], xT[:, bass.ts(t, P)]
                             .rearrange("(k p) t -> p k t", p=P)).then_inc(xT_loaded[t], 16)
            for i in range(5):
                if i:
                    sp.wait_ge(w_lo_ready, PRIMED + i)
                sp.dma_start(w_raw[:, :, :], wT[i].rearrange("(k p) n -> p k n", p=P)).then_inc(w_loaded, 16)
            sp.dma_start(x_tok[:, :, :], x[0:T, :].rearrange("(t p) d -> p t d", p=P)).then_inc(x_loaded, 16)
            sp.wait_ge(w_lo_ready, PRIMED + 5)

            def load_w(e, which):
                C = CHANNELS[which]
                if which:
                    sp.wait_ge(scaled_ready[0], PRIMED + 2 * e + 2)
                elif not (isinstance(e, int) and e == 0):
                    sp.wait_ge(scaled_ready[1], PRIMED + 2 * e)
                sp.dma_start(w_raw[:, :, 0:C], (w1, w2)[which][bass.ts(e, D), :]
                             .rearrange("(t p) d -> p t d", p=P)).then_inc(ew_loaded[which], 16)

            def store_x2(e):
                sp.wait_ge(e_normed, PRIMED + (e + 1) * TT)
                sp.dma_start(x2_dram[bass.ts(e, T), :].rearrange("(t p) d -> p t d", p=P),
                             gu[:, :, :]).then_inc(x2_stored, 16)

            def body(b):
                if has_expert(b):
                    load_w(b - 1, 1)
                load_w(b, 0)
                if has_expert(b):
                    store_x2(b - 1)
                if has_next(b, TT - 1):
                    sp.wait_ge(normed, PRIMED + b * TT + TT)
                    sp.dma_start(x_tok[:, :, :], x[bass.ts(b + 1, T), :]
                                 .rearrange("(t p) d -> p t d", p=P)).then_inc(x_loaded, 16)
            iterations(sp, body)
            load_w(B - 1, 1)
            store_x2(B - 1)
            sp.wait_ge(x2_stored, PRIMED + 16 * B)

        @block.gpsimd
        def _(pool):
            for s in range(2):
                pool.memset(v_ext[:, s, :, DK:E1], 1.0).then_inc(v_ones_ready, 1)
            pool.wait_ge(consts_loaded, PRIMED + CONSTS)

            def split(b, t):
                pool.wait_ge(xhi_ready, PRIMED + tile_no(b, t))
                pool.tensor_tensor(xT_lo[:, t % 2, :, :], xT_raw[:, t % 2, :, :],
                                   xT_hi[:, t % 2, :, :].bitcast(F32), ALU.subtract).then_inc(xlo_ready, 1)

            def rotate(b, t):
                for item in (PQ, PK):
                    k, _, done, _ = slot(b, t, item)
                    pool.wait_ge(drained[k], PRIMED + done)
                pool.wait_ge(feat_ready, PRIMED + tile_no(b, t) - 1)
                q4 = qk[:, :].rearrange("p (h i two) -> p h i two", i=DK // 2, two=2)
                b4 = rot_b[:, :].rearrange("p (h i two) -> p h i two", i=DK // 2, two=2)
                cos = ropes[:, 0, t, :].unsqueeze(1).to_broadcast([P, 2 * H, DK])
                sin = ropes[:, 1, t, :].rearrange("p (i two) -> p i two", two=2)
                pool.tensor_tensor(rot_a[:, :].rearrange("p (h i) -> p h i", i=DK),
                                   qk[:, :].rearrange("p (h i) -> p h i", i=DK), cos, ALU.mult)\
                    .then_inc(rot_a_ready, 1)
                for two in range(2):
                    pool.tensor_tensor(b4[:, :, :, two], q4[:, :, :, 1 - two],
                                       sin[:, :, two].unsqueeze(1).to_broadcast([P, 2 * H, DK // 2]),
                                       ALU.mult).then_inc(rot_b_ready, 1)

            def residual(b, t):
                if t == 0:
                    pool.wait_ge(x_loaded, PRIMED + b * 16 + 16)
                pool.tensor_tensor(x_tok[:, t, :], x_tok[:, t, :], bo_bc[:, :], ALU.add).then_inc(xres_ready, 1)

            def diagonals(e, which):
                kc = CHANNELS[which] // P
                pool.wait_ge(s_ready[which], PRIMED + e + 1)
                if isinstance(e, int) and e == 0:
                    pool.wait_ge(consts_loaded, PRIMED + CONSTS)
                for i in range(2):
                    pool.tensor_tensor(diag[:, i, 0:kc, :],
                                       ident[:, :].unsqueeze(1).to_broadcast([P, kc, P]),
                                       small[:, 3 - i, 0:kc].unsqueeze(2).to_broadcast([P, kc, P]),
                                       ALU.mult).then_inc(diag_ready[which], 1)

            def scale_channels(e, which):
                C = CHANNELS[which]
                for i, item in enumerate((RS, SS)):
                    k, _, done, _ = place(e + 1, (which, item))
                    if (which, i) == (0, 0) and not (isinstance(e, int) and e == 0):
                        pool.wait_ge(x2_stored, PRIMED + 16 * e)
                    pool.wait_ge(drained[k], PRIMED + done)
                    pool.tensor_tensor(scaled[i][:, :, 0:C], expert_tokens(i, which)[:, :, 0:C],
                                       rows[:, i, 0:C].unsqueeze(1).to_broadcast([P, TT, C]),
                                       ALU.mult).then_inc(scaled_ready[which], 1)

            def scales_diagonal(e, which):
                pool.wait_ge(scale_ready[which], PRIMED + 2 * e + 2)
                pool.tensor_tensor(diag[:, 0, :, :],
                                   ident[:, :].unsqueeze(1).to_broadcast([P, KT, P]),
                                   scale[:, 1, :].unsqueeze(2).to_broadcast([P, KT, P]),
                                   ALU.mult).then_inc(sw_diag_ready[which], 1)

            def expert_residual(e):
                for t in range(TT):
                    k, _, done, _ = place(e + 1, (1, OX[t]))
                    pool.wait_ge(drained[k], PRIMED + done)
                pool.tensor_tensor(gu[:, :, :], gu[:, :, :], x1[:, :, :], ALU.add).then_inc(summed, 1)

            for t in range(2):
                split(0, t)
            rotate(0, 0)

            def body(b):
                for t in range(TT):
                    which, second = divmod(t, 2)
                    residual(b, t)
                    if has_expert(b) and second:
                        scales_diagonal(b - 1, which)
                    if has_next(b, t):
                        rotate(*following(b, t))
                    if exists(*ahead(b, t, 2)):
                        split(*ahead(b, t, 2))
                    if has_expert(b) and not second:
                        diagonals(b - 1, which)
                        scale_channels(b - 1, which)
                if has_expert(b):
                    expert_residual(b - 1)
            iterations(pool, body)
            for which in range(2):
                diagonals(B - 1, which)
                scale_channels(B - 1, which)
                scales_diagonal(B - 1, which)
            expert_residual(B - 1)

        @block.scalar
        def _(act):
            for dst, src in ((bias_part[:, :], bias_parts), (att[:, :], bias_rows),
                             (gate[:, :], bias_pick), (ident[:, :], ident_in), (mask[:, :], head_mask),
                             (ropes[:, :, :, :], rope), (bo_bc[:, :], bo)):
                act.dma_start(dst, src).then_inc(consts_loaded, 16)

            def x_hi(b, t):
                act.wait_ge(xT_loaded[t % 2], PRIMED + 16 * (b * 2 + t // 2 + 1))
                if not (isinstance(b, int) and tile_no(b, t) <= 2):
                    k, _, done, _ = slot(*ahead(b, t, -2), PG)
                    act.wait_ge(filled[k], PRIMED + done)
                act.activation(xT_hi[:, t % 2, :, :], xT_raw[:, t % 2, :, :], ACT.Copy).then_inc(xhi_ready, 1)

            def load_xT(b, t):
                act.wait_ge(xlo_ready, PRIMED + tile_no(b, t) - 2)
                act.dma_start(xT_raw[:, t % 2, :, :], xT[:, bass.ds(b * T + t * P, P)]
                              .rearrange("(k p) t -> p k t", p=P)).then_inc(xT_loaded[t % 2], 16)

            for t in range(2):
                x_hi(0, t)
            load_xT(0, 2)
            for i in range(5):
                act.wait_ge(w_loaded, PRIMED + 16 * (i + 1))
                act.activation(w_hi[:, i, :, :], w_raw[:, :, :], ACT.Copy).then_inc(w_hi_ready, 1)

            def qk_out(b, t, item):
                k, _, done, step = slot(b, t, item)
                act.wait_ge(filled[k], PRIMED + done)
                if item == PQ:
                    act.wait_ge(rot_a_ready, PRIMED + tile_no(b, t) - 1)
                    act.wait_ge(rot_b_ready, PRIMED + 2 * (tile_no(b, t) - 1))
                act.activation(qk[:, bass.ts((PQ, PK).index(item), D)], ring[k][:, :], ACT.Copy)\
                    .then_inc(drained[k], step)

            def v_out(b, t):
                k, _, done, step = slot(b, t, PV)
                act.wait_ge(filled[k], PRIMED + done)
                act.wait_ge(s_updated, PRIMED + 2 * (tile_no(b, t) - 1))
                if t < 2:
                    act.wait_ge(v_ones_ready, PRIMED + 2)
                act.activation(v_ext[:, t % 2, :, 0:DK], ring[k][:, :].rearrange("p (h e) -> p h e", e=DK),
                               ACT.Copy).then_inc(drained[k], step)

            def gate_out(b, t):
                k, _, done, step = slot(b, t, PG)
                act.wait_ge(filled[k], PRIMED + done)
                if isinstance(b, int) and b == 0 and t == 0:
                    act.wait_ge(bias_ready, PRIMED + 2)
                act.wait_ge(gated, PRIMED + 2 * (tile_no(b, t) - 1))
                act.activation(gate[:, :], ring[k][:, :], ACT.Tanh, scale=0.5).then_inc(drained[k], step)

            def exponential(b, t):
                act.wait_ge(neg_ready, PRIMED + tile_no(b, t))
                act.activation(rot_b[:, :], rot_b[:, :], ACT.Exp).then_inc(exp_ready, 1)

            def qT_out(b, t):
                k, _, done, step = slot(b, t, QT)
                act.wait_ge(filled[k], PRIMED + done)
                act.wait_ge(num_ready, PRIMED + 2 * (tile_no(b, t) - 1))
                act.activation(q_T[:, :, :], ring[k][:, :].rearrange("p (g t) -> p g t", g=NG), ACT.Copy)\
                    .then_inc(drained[k], step)

            def attT_hi(b, t):
                k, _, done, _ = slot(b, t, AT)
                act.wait_ge(filled[k], PRIMED + done)
                if not (isinstance(b, int) and tile_no(b, t) == 1):
                    before = ahead(b, t, -1)
                    k_out, _, done, _ = slot(*before, OUT)
                    act.wait_ge(filled[k_out], PRIMED + done)
                act.activation(att_hi[:, :, :], ring[k][:, :].rearrange("p (g t) -> p g t", g=KT), ACT.Copy)\
                    .then_inc(att_hi_ready, 1)

            def roots(e, which):
                kc = CHANNELS[which] // P
                act.wait_ge(ratio_ready[which], PRIMED + e + 1)
                act.activation(small[:, 2, 0:kc], small[:, 1, 0:kc], ACT.Sqrt).then_inc(root_ready[which], 1)

            def channel_rows(e, which):
                C = CHANNELS[which]
                for i, item in enumerate((RS, SS)):
                    k, _, done, step = place(e + 1, (which, item))
                    act.wait_ge(filled[k], PRIMED + done)
                    act.activation(rows[:, i, 0:C], ring[k][:, 0:C], ACT.Copy).then_inc(drained[k], step)

            def quantised(e, which, i):
                C = CHANNELS[which]
                act.wait_ge(clamped[which], PRIMED + 2 * e + i + 1)
                act.activation(q[i][:, :, 0:C], scaled[i][:, :, 0:C], ACT.Copy, bias=-ROUND)\
                    .then_inc(q_ready[which], 1)

            def transposed_out(e, which, i):
                for j in range(CHANNELS[which] // P // 2):
                    k, _, done, step = place(e + 1, (which, ((XT0, XT1), (WT0, WT1))[i][j]))
                    act.wait_ge(filled[k], PRIMED + done)
                    act.activation(qT[i][:, 2 * j:2 * j + 2, :],
                                   ring[k][:, :].bitcast(BF16).rearrange("p (c t) -> p c t", c=2),
                                   ACT.Copy).then_inc(drained[k], step)

            def scales_row(e, which):
                k, _, done, step = place(e + 1, (which, SW))
                act.wait_ge(filled[k], PRIMED + done)
                act.activation(rows[:, 0, :], ring[k][:, :], ACT.Copy).then_inc(drained[k], step)

            def silu(e):
                k, _, done, _ = place(e + 1, (0, OX[TT - 1]))
                act.wait_ge(drained[k], PRIMED + done)
                act.activation(sl[:, :, 0:D // 2], gu[:, :, 0:D // 2], ACT.Silu).then_inc(silu_ready, 1)

            def quantise_part(e, which):
                quantised(e, which, 0)
                quantised(e, which, 1)
                transposed_out(e, which, 0)
                scales_row(e, which)
                transposed_out(e, which, 1)

            def expert_deviation(e):
                act.wait_ge(e_var_ready, PRIMED + e + 1)
                act.activation(e_rstd[:, 1, :], e_rstd[:, 0, :], ACT.Sqrt).then_inc(e_std_ready, 1)

            def deviation(b):
                act.wait_ge(var_ready, PRIMED + b + 1)
                act.activation(rstd[:, 1, :], rstd[:, 0, :], ACT.Sqrt).then_inc(std_ready, 1)

            qk_out(0, 0, PQ)
            qk_out(0, 0, PK)
            v_out(0, 0)
            gate_out(0, 0)
            exponential(0, 0)

            def body(b):
                for t in range(TT):
                    which, second = divmod(t, 2)
                    expert, more = has_expert(b), has_next(b, t)
                    qT_out(b, t)
                    if more:
                        qk_out(*following(b, t), PQ)
                    if expert and t == 2:
                        silu(b - 1)
                    if more:
                        qk_out(*following(b, t), PK)
                        v_out(*following(b, t))
                    if expert and second:
                        quantise_part(b - 1, which)
                    attT_hi(b, t)
                    if more:
                        gate_out(*following(b, t))
                        exponential(*following(b, t))
                    if exists(*ahead(b, t, 3)):
                        load_xT(*ahead(b, t, 3))
                    if exists(*ahead(b, t, 2)):
                        x_hi(*ahead(b, t, 2))
                    if expert and not second:
                        roots(b - 1, which)
                        channel_rows(b - 1, which)
                deviation(b)
                if has_expert(b):
                    expert_deviation(b - 1)
            iterations(act, body)
            for which in range(2):
                roots(B - 1, which)
                channel_rows(B - 1, which)
                quantise_part(B - 1, which)
                if which == 0:
                    silu(B - 1)
            expert_deviation(B - 1)

        @block.vector
        def _(dve):
            dve.wait_ge(consts_loaded, PRIMED + CONSTS)
            dve.tensor_copy(ident16[:, :], ident[:, :]).then_inc(ones_ready, 1)
            dve.memset(ones[:, :], 1.0).then_inc(ones_ready, 1)
            dve.memset(scale[:, :, :], 0.0).then_inc(ones_ready, 1)
            dve.tensor_copy(pick[:, :, :], gate[:, :].rearrange("p (i m) -> p i m", m=P)).then_inc(bias_ready, 1)
            hi = att_hi[:, :, :].rearrange("p k t -> p (k t)")
            dve.tensor_copy(hi, att[:, :]).then_inc(bias_hi_ready, 1)
            dve.wait_ge(bias_hi_ready, PRIMED + 1)
            dve.tensor_tensor(att[:, :], att[:, :], hi.bitcast(F32), ALU.subtract).then_inc(bias_hi_ready, 1)
            dve.tensor_scalar(feat[:, 0:D], hi.bitcast(F32), bias_part[:, 0:1], None, ALU.mult)\
                .then_inc(bias_hi_ready, 1)
            dve.wait_ge(bias_hi_ready, PRIMED + 3)
            dve.scalar_tensor_tensor(bias_hl[:, :], att[:, :], bias_part[:, 1:2], feat[:, 0:D],
                                     ALU.mult, ALU.add).then_inc(bias_ready, 1)
            for i in range(5):
                dve.wait_ge(w_hi_ready, PRIMED + i + 1)
                dve.tensor_tensor(w_lo[:, i, :, :], w_raw[:, :, :], w_hi[:, i, :, :].bitcast(F32),
                                  ALU.subtract).then_inc(w_lo_ready, 1)

            def rotated_sum(b, t):
                dve.wait_ge(rot_a_ready, PRIMED + tile_no(b, t))
                dve.wait_ge(rot_b_ready, PRIMED + 2 * tile_no(b, t))
                dve.tensor_tensor(rot_a[:, :], rot_a[:, :], rot_b[:, :], ALU.add).then_inc(rotated, 1)
                dve.wait_ge(rotated, PRIMED + tile_no(b, t))
                dve.tensor_scalar(rot_b[:, :], rot_a[:, :], 0.0, None, ALU.min).then_inc(neg_ready, 1)

            def features(b, t):
                dve.wait_ge(exp_ready, PRIMED + tile_no(b, t))
                dve.wait_ge(s_updated, PRIMED + 2 * (tile_no(b, t) - 1))
                dve.scalar_tensor_tensor(feat[:, :], rot_a[:, :], 0.0, rot_b[:, :], ALU.max, ALU.add)\
                    .then_inc(feat_ready, 1)

            def mask_state(b, t, c):
                dve.wait_ge(s_updated, PRIMED + 2 * (tile_no(b, t) - 1) + c + 1)
                dve.wait_ge(num_ready, PRIMED + 2 * (tile_no(b, t) - 1))
                dve.tensor_tensor(s_bd[:, c, :, :].rearrange("p (a g) n -> p a g n", a=2),
                                  s_ps[:, :, 0:2 * GE].rearrange("p a (g n) -> p a g n", g=2),
                                  mask[:, :].unsqueeze(1).unsqueeze(1).to_broadcast([P, 2, 2, GE]),
                                  ALU.mult).then_inc(s_masked, 1)

            def attend(b, t):
                dve.wait_ge(num_ready, PRIMED + 2 * tile_no(b, t))
                n4 = n_ps[:, :, 0:2 * GE].rearrange("p a (h e) -> p a h e", e=E1)
                dve.tensor_scalar(rden[:, 0, :].rearrange("p (a h) -> p a h", a=2), n4[:, :, :, DK],
                                  DEN_EPS, 2.0, ALU.add, ALU.mult).then_inc(den_ready, 1)
                k, _, done, _ = slot(b, t, PG)
                dve.wait_ge(drained[k], PRIMED + done)
                if not (isinstance(b, int) and tile_no(b, t) == 1):
                    before = ahead(b, t, -1)
                    k, _, done, _ = slot(*before, AT)
                    dve.wait_ge(filled[k], PRIMED + done)
                for a in range(2):
                    half = bass.ts(a, D // 2)
                    dve.scalar_tensor_tensor(att[:, half].rearrange("p (h e) -> p h e", e=DK),
                                             gate[:, half].rearrange("p (h e) -> p h e", e=DK), 1.0,
                                             n4[:, a, :, 0:DK], ALU.add, ALU.mult).then_inc(gated, 1)
                dve.wait_ge(den_ready, PRIMED + tile_no(b, t))
                dve.reciprocal(rden[:, 1, :], rden[:, 0, :]).then_inc(rden_ready, 1)
                dve.wait_ge(rden_ready, PRIMED + tile_no(b, t))
                dve.wait_ge(gated, PRIMED + 2 * tile_no(b, t))
                att3 = att[:, :].rearrange("p (h e) -> p h e", e=DK)
                dve.tensor_tensor(att3, att3, rden[:, 1, :].unsqueeze(2).to_broadcast([P, H, DK]), ALU.mult)\
                    .then_inc(att_ready, 1)

            def attT_lo(b, t):
                k, _, _, step = slot(b, t, AT)
                dve.wait_ge(att_hi_ready, PRIMED + tile_no(b, t))
                dve.tensor_tensor(att_lo[:, :, :], ring[k][:, :].rearrange("p (g t) -> p g t", g=KT),
                                  att_hi[:, :, :].bitcast(F32), ALU.subtract).then_inc(drained[k], step)

            def add_residual(b, t):
                k, _, done, step = slot(b, t, OUT)
                dve.wait_ge(filled[k], PRIMED + done)
                dve.wait_ge(xres_ready, PRIMED + tile_no(b, t))
                dve.tensor_tensor(x_tok[:, t, :], ring[k][:, :], x_tok[:, t, :], ALU.add).then_inc(drained[k], step)
                dve.wait_ge(drained[k], PRIMED + done)
                dve.bn_stats(stats[:, t, :], x_tok[:, t, :]).then_inc(stats_ready, 1)

            def waiter(semaphore, before):
                level = [0]

                def wait(ins):
                    level[0] += 1
                    ins.then_inc(semaphore, 1)
                    dve.wait_ge(semaphore, PRIMED + before + level[0])
                return wait

            def variance(b):
                dve.wait_ge(stats_ready, PRIMED + b * TT + TT)
                moments(dve, stats, part, mean[:, :], rstd[:, 0, :], waiter(moment_ready, b * 2))\
                    .then_inc(var_ready, 1)

            def normalise(b):
                dve.wait_ge(std_ready, PRIMED + b + 1)
                dve.reciprocal(rstd[:, 2, :], rstd[:, 1, :]).then_inc(rstd_ready, 1)
                dve.wait_ge(rstd_ready, PRIMED + b + 1)
                if has_expert(b):
                    dve.wait_ge(summed, PRIMED + b)
                for t in range(TT):
                    dve.tensor_scalar(x1[:, t, :], x_tok[:, t, :], mean[:, t:t + 1], rstd[:, 2, t:t + 1],
                                      ALU.subtract, ALU.mult).then_inc(normed, 1)

            LINKED = 7

            def linked(e, which, first):
                return waiter(small_done, (e * 2 + which) * LINKED + first)

            def channel_top(e, which, i):
                C = CHANNELS[which]
                if i == 0 and which == 0:
                    dve.wait_ge(normed, PRIMED + e * TT + TT)
                if i == 1:
                    dve.wait_ge(ew_loaded[which], PRIMED + 16 * e + 16)
                dve.tensor_reduce(top[:, i, 0:C], expert_tokens(i, which)[:, :, 0:C].rearrange("p t c -> p c t"),
                                  AX.X, ALU.max, apply_absolute_value=True).then_inc(top_ready[which], 1)

            def channel_ratio(e, which):
                C, kc = CHANNELS[which], CHANNELS[which] // P
                link = linked(e, which, 0)
                for i, item in enumerate((MX, MW)):
                    k, _, done, step = place(e + 1, (which, item))
                    dve.wait_ge(filled[k], PRIMED + done)
                    dve.tensor_reduce(amax[:, i, 0:kc], ring[k][:, 0:C].rearrange("p (c t) -> p c t", t=P),
                                      AX.X, ALU.max).then_inc(drained[k], step)
                    dve.wait_ge(drained[k], PRIMED + done)
                link(dve.tensor_scalar(amax[:, :, 0:kc], amax[:, :, 0:kc], Q_EPS, None, ALU.max))
                link(dve.reciprocal(small[:, 0, 0:kc], amax[:, 1, 0:kc]))
                dve.tensor_tensor(small[:, 1, 0:kc], amax[:, 0, 0:kc], small[:, 0, 0:kc], ALU.mult)\
                    .then_inc(ratio_ready[which], 1)

            def channel_scale(e, which):
                kc = CHANNELS[which] // P
                link = linked(e, which, 2)
                dve.wait_ge(root_ready[which], PRIMED + e + 1)
                link(dve.tensor_scalar(small[:, 2, 0:kc], small[:, 2, 0:kc], Q_EPS, None, ALU.max))
                dve.reciprocal(small[:, 3, 0:kc], small[:, 2, 0:kc]).then_inc(s_ready[which], 1)

            def quantise(e, which, i):
                C = CHANNELS[which]
                out = scaled[i]
                link = linked(e, which, 3 + 2 * i)
                dve.wait_ge(scaled_ready[which], PRIMED + 2 * e + i + 1)
                link(dve.tensor_reduce(row_max[:, i, :], out[:, :, 0:C], AX.X, ALU.max,
                                       apply_absolute_value=True))
                dve.tensor_scalar(scale[:, i, :], row_max[:, i, :], Q_EPS, 1.0 / QMAX, ALU.max, ALU.mult)\
                    .then_inc(scale_ready[which], 1)
                dve.wait_ge(scale_ready[which], PRIMED + 2 * e + i + 1)
                link(dve.reciprocal(inverse[:, i, :], scale[:, i, :]))
                for t in range(TT):
                    dve.tensor_scalar(out[:, t, 0:C], out[:, t, 0:C], inverse[:, i, t:t + 1], ROUND,
                                      ALU.mult, ALU.add).then_inc(shifted[which], 1)
                dve.wait_ge(shifted[which], PRIMED + (2 * e + i + 1) * TT)
                dve.tensor_scalar(out[:, :, 0:C], out[:, :, 0:C], ROUND + QMAX, ROUND - QMAX,
                                  ALU.min, ALU.max).then_inc(clamped[which], 1)

            def linear_out(e, which):
                k, _, done, _ = place(e + 1, (which, SW))
                dve.wait_ge(drained[k], PRIMED + done)
                for t in range(TT):
                    k, _, done, step = place(e + 1, (which, OX[t]))
                    dve.wait_ge(filled[k], PRIMED + done)
                    dve.scalar_tensor_tensor(gu[:, t, :], ring[k][:, :], scale[:, 0, t:t + 1], rows[:, 0, :],
                                             ALU.mult, ALU.mult).then_inc(drained[k], step)

            def activated(e):
                dve.wait_ge(silu_ready, PRIMED + e + 1)
                dve.tensor_tensor(act_in[:, :, :], sl[:, :, 0:D // 2], gu[:, :, D // 2:D], ALU.mult)\
                    .then_inc(act_ready, 1)
                dve.wait_ge(act_ready, PRIMED + e + 1)

            def expert_variance(e):
                dve.wait_ge(summed, PRIMED + e + 1)
                for t in range(TT):
                    dve.bn_stats(e_stats[:, t, :], gu[:, t, :]).then_inc(e_stats_ready, 1)
                dve.wait_ge(e_stats_ready, PRIMED + e * TT + TT)
                moments(dve, e_stats, e_part, e_mean[:, :], e_rstd[:, 0, :], waiter(e_moment_ready, e * 2))\
                    .then_inc(e_var_ready, 1)

            def expert_normalise(e):
                dve.wait_ge(e_std_ready, PRIMED + e + 1)
                dve.reciprocal(e_rstd[:, 2, :], e_rstd[:, 1, :]).then_inc(e_rstd_ready, 1)
                dve.wait_ge(e_rstd_ready, PRIMED + e + 1)
                for t in range(TT):
                    dve.tensor_scalar(gu[:, t, :], gu[:, t, :], e_mean[:, t:t + 1], e_rstd[:, 2, t:t + 1],
                                      ALU.subtract, ALU.mult).then_inc(e_normed, 1)

            rotated_sum(0, 0)
            features(0, 0)
            mask_state(0, 0, 0)

            def body(b):
                expert = has_expert(b)
                for t in range(TT):
                    which, second = divmod(t, 2)
                    if expert and not second:
                        if which:
                            activated(b - 1)
                        channel_top(b - 1, which, 0)
                    elif expert:
                        quantise(b - 1, which, 0)
                    mask_state(b, t, 1)
                    if expert and not second:
                        channel_top(b - 1, which, 1)
                    elif expert:
                        quantise(b - 1, which, 1)
                    attend(b, t)
                    attT_lo(b, t)
                    if has_next(b, t):
                        rotated_sum(*following(b, t))
                    if expert and not second:
                        channel_ratio(b - 1, which)
                    add_residual(b, t)
                    if has_next(b, t):
                        features(*following(b, t))
                    if expert and not second:
                        channel_scale(b - 1, which)
                    elif expert:
                        linear_out(b - 1, which)
                    if has_next(b, t):
                        mask_state(*following(b, t), 0)
                variance(b)
                if expert:
                    expert_variance(b - 1)
                normalise(b)
                if expert:
                    expert_normalise(b - 1)
            iterations(dve, body)
            e = B - 1
            for which in range(2):
                if which:
                    activated(e)
                channel_top(e, which, 0)
                channel_top(e, which, 1)
                channel_ratio(e, which)
                channel_scale(e, which)
                quantise(e, which, 0)
                quantise(e, which, 1)
                linear_out(e, which)
            expert_variance(e)
            expert_normalise(e)

        @block.tensor
        def _(pe):
            def project(b, t, item):
                k, free, _, step = slot(b, t, item)
                i = (PQ, PK, PV, PG).index(item)
                if item == PQ:
                    pe.wait_ge(xlo_ready, PRIMED + tile_no(b, t))
                pe.wait_ge(drained[k], PRIMED + free)
                pe.matmul(ring[k][:, :], pick[:, i, :], bias_hl[:, :], start=True, stop=False)
                for c in range(KT):
                    last = matmul_split(pe, ring[k][:, :], xT_hi[:, t % 2, c, :], xT_lo[:, t % 2, c, :],
                                        w_hi[:, i, c, :], w_lo[:, i, c, :], False, c == KT - 1)
                last.then_inc(filled[k], step)

            def q_transposed(b, t):
                k, free, _, step = slot(b, t, QT)
                pe.wait_ge(feat_ready, PRIMED + tile_no(b, t))
                pe.wait_ge(drained[k], PRIMED + free)
                for g in range(NG):
                    last = pe.transpose(ring[k][:, bass.ts(g, P)], feat[:, bass.ts(g, P)], ident[:, :])
                last.then_inc(filled[k], step)

            def update_state(b, t, c):
                if c == 0:
                    k, _, done, _ = slot(b, t, PV)
                    pe.wait_ge(drained[k], PRIMED + done)
                pe.wait_ge(s_masked, PRIMED + 2 * (tile_no(b, t) - 1) + c)
                rows_c = slice(c * CS, (c + 1) * CS)
                for g in range(NG):
                    first = t == 0 and c == 0 and g % 2 == 0
                    last = pe.matmul(s_ps[:, g // 2, (g % 2) * GE:(g % 2 + 1) * GE],
                                     feat[rows_c, D + g * P:D + (g + 1) * P],
                                     v_ext[rows_c, t % 2, g * GH:(g + 1) * GH, :].rearrange("p h e -> p (h e)"),
                                     start=first, stop=True, skip_group_check=True)
                last.then_inc(s_updated, 1)

            def numerators(b, t, c):
                pe.wait_ge(s_masked, PRIMED + 2 * (tile_no(b, t) - 1) + c + 1)
                if c == 0:
                    k, _, done, _ = slot(b, t, QT)
                    pe.wait_ge(drained[k], PRIMED + done)
                    pe.wait_ge(gated, PRIMED + 2 * (tile_no(b, t) - 1))
                    pe.wait_ge(den_ready, PRIMED + tile_no(b, t) - 1)
                rows_c = slice(c * CS, (c + 1) * CS)
                for g in range(NG):
                    last = pe.matmul(n_ps[rows_c, g // 2, (g % 2) * GE:(g % 2 + 1) * GE],
                                     q_T[:, g, rows_c], s_bd[:, c, g, :], start=True, stop=True)
                last.then_inc(num_ready, 1)

            def att_transposed(b, t):
                k, free, _, step = slot(b, t, AT)
                pe.wait_ge(att_ready, PRIMED + tile_no(b, t))
                pe.wait_ge(drained[k], PRIMED + free)
                for g in range(NG):
                    last = pe.transpose(ring[k][:, bass.ts(g, P)], att[:, bass.ts(g, P)], ident[:, :])
                last.then_inc(filled[k], step)

            def output(b, t):
                k, free, _, step = slot(b, t, OUT)
                k_at, _, done, _ = slot(b, t, AT)
                pe.wait_ge(drained[k_at], PRIMED + done)
                pe.wait_ge(drained[k], PRIMED + free)
                for c in range(KT):
                    last = matmul_split(pe, ring[k][:, :], att_hi[:, c, :], att_lo[:, c, :],
                                        w_hi[:, 4, c, :], w_lo[:, 4, c, :], c == 0, c == KT - 1)
                last.then_inc(filled[k], step)

            def maxima(e, which):
                for i, item in enumerate((MX, MW)):
                    k, free, _, step = place(e + 1, (which, item))
                    pe.wait_ge(top_ready[which], PRIMED + 2 * e + i + 1)
                    pe.wait_ge(drained[k], PRIMED + free)
                    for c in range(CHANNELS[which] // P):
                        last = pe.transpose(ring[k][:, bass.ts(c, P)], top[:, i, bass.ts(c, P)], ident[:, :])
                    last.then_inc(filled[k], step)

            def channel_rows(e, which):
                C = CHANNELS[which]
                for i, item in enumerate((RS, SS)):
                    k, free, _, step = place(e + 1, (which, item))
                    pe.wait_ge(diag_ready[which], PRIMED + 2 * e + i + 1)
                    pe.wait_ge(drained[k], PRIMED + free)
                    pe.matmul(ring[k][:, 0:C], ones[:, :], diag[:, i, 0:C // P, :].rearrange("p c t -> p (c t)"),
                              start=True, stop=True).then_inc(filled[k], step)

            def transposed(e, which, i):
                pe.wait_ge(q_ready[which], PRIMED + 2 * e + i + 1)
                for j in range(CHANNELS[which] // P // 2):
                    k, free, _, step = place(e + 1, (which, ((XT0, XT1), (WT0, WT1))[i][j]))
                    pe.wait_ge(drained[k], PRIMED + free)
                    half = ring[k][:, :].bitcast(BF16).rearrange("p (c t m) -> p c t m", c=2, t=TT)
                    for c in range(2):
                        for t in range(TT):
                            last = pe.transpose(half[:, c, t, :], q[i][:, t, bass.ts(2 * j + c, P)],
                                                ident16[:, :])
                    last.then_inc(filled[k], step)

            def quantised(e, which):
                transposed(e, which, 0)
                k, free, _, step = place(e + 1, (which, SW))
                pe.wait_ge(sw_diag_ready[which], PRIMED + e + 1)
                pe.wait_ge(drained[k], PRIMED + free)
                pe.matmul(ring[k][:, :], ones[:, :], diag[:, 0, :, :].rearrange("p c t -> p (c t)"),
                          start=True, stop=True).then_inc(filled[k], step)
                transposed(e, which, 1)

            def linear(e, which):
                kc = CHANNELS[which] // P
                for items in ((XT0, XT1), (WT0, WT1)):
                    for j in range(kc // 2):
                        k, _, done, _ = place(e + 1, (which, items[j]))
                        pe.wait_ge(drained[k], PRIMED + done)
                for t in range(TT):
                    k, free, _, step = place(e + 1, (which, OX[t]))
                    pe.wait_ge(drained[k], PRIMED + free)
                    for c in range(kc):
                        last = pe.matmul(ring[k][:, :], qT[0][:, c, bass.ts(t, P)], qT[1][:, c, :],
                                         start=c == 0, stop=c == kc - 1)
                    last.then_inc(filled[k], step)

            pe.wait_ge(bias_ready, PRIMED + 2)
            pe.wait_ge(consts_loaded, PRIMED + CONSTS)
            pe.wait_ge(ones_ready, PRIMED + 3)
            pe.wait_ge(v_ones_ready, PRIMED + 2)
            for i, item in enumerate((PQ, PK, PV, PG)):
                pe.wait_ge(w_lo_ready, PRIMED + i + 1)
                project(0, 0, item)
            pe.wait_ge(w_lo_ready, PRIMED + 5)

            def body(b):
                for t in range(TT):
                    which, second = divmod(t, 2)
                    expert, more = has_expert(b), has_next(b, t)
                    q_transposed(b, t)
                    update_state(b, t, 0)
                    if more:
                        project(*following(b, t), PQ)
                    numerators(b, t, 0)
                    update_state(b, t, 1)
                    if more:
                        project(*following(b, t), PK)
                    numerators(b, t, 1)
                    if more:
                        project(*following(b, t), PV)
                    if expert:
                        (quantised if second else maxima)(b - 1, which)
                    att_transposed(b, t)
                    if more:
                        project(*following(b, t), PG)
                    output(b, t)
                    if expert:
                        (linear if second else channel_rows)(b - 1, which)
            iterations(pe, body)
            for which in range(2):
                maxima(B - 1, which)
                channel_rows(B - 1, which)
                quantised(B - 1, which)
                linear(B - 1, which)



F = 1408
FT = F // P
E = 8
R = 16
LORA_SCALE = 2.0
NU = 2 * P + E
UP = 2 * D + 2 * P
DOWN = P + D
RAW = 3
FAR = -3.0e38
YB = 4
XC0, U0, UM0, MT, WB0 = 0, 4, 8, 12, 13
Y_BEFORE = (4, 4, 4, 3)
Y_TOTAL = (5, 5, 5, 4)


def mixture(nc, x2_dram, a13g, stream, b2T, ident_in, descending, out_dram):
    with ExitStack() as ctx:
        def sb(name, shape, dt=F32):
            return ctx.enter_context(nc.sbuf_tensor("f_" + name, shape, dt))

        primed = []

        def sem(name):
            primed.append(ctx.enter_context(nc.semaphore("f_" + name)))
            return primed[-1]

        def pb(name):
            return ctx.enter_context(nc.psum_tensor("f_" + name, [P, 512], F32))

        ident = sb("ident", [P, P])
        ident16 = sb("ident16", [P, P], BF16)
        desc = sb("desc", [P, E])
        a_raw = sb("a_raw", [P, KT, NU])
        a_hi = sb("a_hi", [P, KT, NU], F32R)
        a_lo = sb("a_lo", [P, KT, NU], F32R)
        b2_raw = sb("b2_raw", [P, D])
        b2_hi = sb("b2_hi", [P, D], F32R)
        b2_lo = sb("b2_lo", [P, D], F32R)
        w_raw = sb("w_raw", [P, RAW, UP + DOWN])
        up_hi = sb("up_hi", [P, 2, UP], F32R)
        up_lo = sb("up_lo", [P, 2, UP], F32R)
        down_hi = sb("down_hi", [P, 3, DOWN], F32R)
        down_lo = sb("down_lo", [P, 3, DOWN], F32R)
        x2 = sb("x2", [P, TT, D])
        xT_hi = sb("xT_hi", [P, KT, T], F32R)
        xT_lo = sb("xT_lo", [P, KT, T], F32R)
        logits = sb("logits", [P, TT, E])
        pick = sb("pick", [P, 4, TT, E])
        best = sb("best", [P, 4, TT])
        soft = sb("soft", [P, 4, TT])
        weight = sb("weight", [P, 2, TT])
        coef = sb("coef", [P, 2, TT, E])
        masks = sb("masks", [P, 2, TT, E, R], BF16)
        weight_bc = sb("weight_bc", [P, 2, TT, P])
        um = sb("um", [P, TT, 2, 2, P])
        umT_hi = sb("umT_hi", [P, 4, T], F32R)
        umT_lo = sb("umT_lo", [P, 4, T], F32R)
        maskT = sb("maskT", [P, 2, T], BF16)
        weightT = sb("weightT", [P, 2, T])
        silu = sb("silu", [P, 2, T])
        gated = sb("gated", [P, 2, T])
        act = sb("act", [P, 3, T])
        act_hi = sb("act_hi", [P, 2, T], F32R)
        act_lo = sb("act_lo", [P, 2, T], F32R)
        zm = sb("zm", [P, 3, T])
        z_hi = sb("z_hi", [P, T], F32R)
        z_lo = sb("z_lo", [P, T], F32R)
        x3 = sb("x3", [P, TT, D])
        stats = sb("stats", [P, TT, 6])
        part = sb("part", [P, TT, 5])
        mean = sb("mean", [P, TT])
        rstd = sb("rstd", [P, 3, TT])

        h_ps = [pb("h1"), pb("h3")]
        z_ps = [pb("z_sum"), pb("z_second")]
        bank = [pb(f"y{i}") for i in range(YB)]

        consts_loaded = sem("consts_loaded")
        consts_ready = sem("consts_ready")
        x2_loaded = sem("x2_loaded")
        streamed = [sem(f"streamed{i}") for i in range(RAW)]
        w_hi_ready = sem("w_hi_ready")
        w_lo_ready = sem("w_lo_ready")
        filled = [sem(f"filled{i}") for i in range(YB)]
        drained = [sem(f"drained{i}") for i in range(YB)]
        xT_hi_ready = sem("xT_hi_ready")
        step_done = sem("step_done")
        gap_ready = sem("gap_ready")
        exp_ready = sem("exp_ready")
        weight_ready = sem("weight_ready")
        masks_ready = sem("masks_ready")
        um_hi_ready = sem("um_hi_ready")
        h_ready = [sem("h1_ready"), sem("h3_ready")]
        silu_ready = sem("silu_ready")
        gated_ready = sem("gated_ready")
        act_ready = sem("act_ready")
        sum_ready = sem("sum_ready")
        act_hi_ready = sem("act_hi_ready")
        act_lo_ready = sem("act_lo_ready")
        y_done = sem("y_done")
        z_done = sem("z_done")
        z_masked = sem("z_masked")
        z_summed = sem("z_summed")
        z_hi_ready = sem("z_hi_ready")
        z_lo_ready = sem("z_lo_ready")
        var_ready = sem("var_ready")
        std_ready = sem("std_ready")
        normed = sem("normed")
        out_stored = sem("out_stored")

        def slot(b, n):
            return n % YB, b * Y_TOTAL[n % YB] + n // YB

        def y_slot(b, t):
            return t, b * Y_TOTAL[t] + Y_BEFORE[t]

        def tiles(b, f):
            return b * FT + f + 1

        with nc.Block() as start:
            @start.gpsimd
            def _(pool):
                for semaphore in primed:
                    pool.sem_inc(semaphore, PRIMED)

        block = ctx.enter_context(nc.Block())

        @block.sync
        def _(sp):
            for dst, src in ((ident[:, :], ident_in), (desc[:, :], descending),
                             (a_raw[:, :, :], a13g.rearrange("(k p) n -> p k n", p=P)), (b2_raw[:, :], b2T)):
                sp.dma_start(dst, src).then_inc(consts_loaded, 16)
            with sp.Fori(0, B) as b:
                sp.wait_ge(drained[TT - 1], PRIMED + b * Y_TOTAL[TT - 1])
                sp.dma_start(x2[:, :, :], x2_dram[bass.ts(b, T), :].rearrange("(t p) d -> p t d", p=P))\
                    .then_inc(x2_loaded, 16)
                sp.wait_ge(normed, PRIMED + b * TT + TT)
                sp.dma_start(out_dram[bass.ts(b, T), :].rearrange("(t p) d -> p t d", p=P), x3[:, :, :])\
                    .then_inc(out_stored, 16)
            sp.wait_ge(out_stored, PRIMED + 16 * B)

        @block.gpsimd
        def _(pool):
            def gate(b, f, choice):
                n = 2 * (tiles(b, f) - 1) + choice
                pool.wait_ge(silu_ready, PRIMED + n + 1)
                pool.wait_ge(act_ready, PRIMED + 2 * (tiles(b, f) - 1))
                pool.tensor_tensor(gated[:, choice, :], silu[:, choice, :], weightT[:, choice, :], ALU.mult)\
                    .then_inc(gated_ready, 1)

            def total(b, f):
                pool.wait_ge(act_ready, PRIMED + 2 * tiles(b, f))
                pool.wait_ge(act_lo_ready, PRIMED + 2 * (tiles(b, f) - 1))
                pool.tensor_tensor(act[:, 2, :], act[:, 0, :], act[:, 1, :], ALU.add).then_inc(sum_ready, 1)

            def split_lo(b, f):
                pool.wait_ge(w_hi_ready, PRIMED + 2 * tiles(b, f))
                r = f % RAW
                for dst, hi, cols in ((up_lo[:, f % 2, :], up_hi[:, f % 2, :], slice(0, UP)),
                                      (down_lo[:, f % 3, :], down_hi[:, f % 3, :], slice(UP, UP + DOWN))):
                    pool.tensor_tensor(dst, w_raw[:, r, cols], hi.bitcast(F32), ALU.subtract)\
                        .then_inc(w_lo_ready, 1)

            with pool.Fori(0, B) as b:
                for f in range(2):
                    split_lo(b, f)
                for k in range(2):
                    kk, n = slot(b, WB0 + k)
                    pool.wait_ge(drained[kk], PRIMED + n + 1)
                for f in range(FT):
                    gate(b, f, 0)
                    gate(b, f, 1)
                    total(b, f)
                    if f + 2 < FT:
                        split_lo(b, f + 2)

        @block.scalar
        def _(sc):
            def fetch(b, f):
                r = f % RAW
                before = b * FT + f - RAW + 1
                if f >= RAW:
                    sc.wait_ge(w_lo_ready, PRIMED + 2 * before)
                else:
                    sc.wait_ge(w_lo_ready, PRIMED + 2 * b * FT)
                sc.dma_start(w_raw[:, r, :], stream[f, :, :]).then_inc(streamed[r], 16)

            PER = [len(range(r, FT, RAW)) for r in range(RAW)]

            def split_hi(b, f):
                r = f % RAW
                sc.wait_ge(streamed[r], PRIMED + 16 * (b * PER[r] + f // RAW + 1))
                if f >= 2:
                    sc.wait_ge(h_ready[1], PRIMED + 2 * (tiles(b, f) - 2))
                else:
                    sc.wait_ge(h_ready[1], PRIMED + 2 * b * FT)
                sc.activation(up_hi[:, f % 2, :], w_raw[:, r, 0:UP], ACT.Copy).then_inc(w_hi_ready, 1)
                if f >= 3:
                    sc.wait_ge(z_done, PRIMED + tiles(b, f) - 3)
                else:
                    sc.wait_ge(z_done, PRIMED + b * FT)
                sc.activation(down_hi[:, f % 3, :], w_raw[:, r, UP:UP + DOWN], ACT.Copy).then_inc(w_hi_ready, 1)

            sc.wait_ge(consts_loaded, PRIMED + 64)
            sc.activation(a_hi[:, :, :], a_raw[:, :, :], ACT.Copy).then_inc(consts_ready, 1)
            sc.activation(b2_hi[:, :], b2_raw[:, :], ACT.Copy).then_inc(consts_ready, 1)
            with sc.Fori(0, B) as b:
                for f in range(RAW):
                    fetch(b, f)
                for c in range(KT):
                    k, n = slot(b, XC0 + c)
                    sc.wait_ge(filled[k], PRIMED + n + 1)
                    sc.activation(xT_hi[:, c, :], bank[k][:, :], ACT.Copy).then_inc(xT_hi_ready, 1)
                for f in range(2):
                    split_hi(b, f)
                sc.wait_ge(gap_ready, PRIMED + b + 1)
                sc.activation(soft[:, 1, :], soft[:, 0, :], ACT.Exp).then_inc(exp_ready, 1)
                for a in range(4):
                    k, n = slot(b, UM0 + a)
                    sc.wait_ge(filled[k], PRIMED + n + 1)
                    sc.activation(umT_hi[:, a, :], bank[k][:, :], ACT.Copy).then_inc(um_hi_ready, 1)
                k, n = slot(b, MT)
                sc.wait_ge(filled[k], PRIMED + n + 1)
                sc.activation(maskT[:, :, :], bank[k][:, :].bitcast(BF16).rearrange("p (a t) -> p a t", a=2),
                              ACT.Copy).then_inc(drained[k], 1)
                for a in range(2):
                    k, n = slot(b, WB0 + a)
                    sc.wait_ge(filled[k], PRIMED + n + 1)
                    sc.activation(weightT[:, a, :], bank[k][:, :], ACT.Copy).then_inc(drained[k], 1)
                for f in range(FT):
                    if f + RAW < FT:
                        fetch(b, f + RAW)
                    for choice in range(2):
                        n = 2 * (tiles(b, f) - 1) + choice
                        sc.wait_ge(h_ready[0], PRIMED + n + 1)
                        sc.wait_ge(gated_ready, PRIMED + 2 * (tiles(b, f) - 1))
                        sc.activation(silu[:, choice, :], h_ps[0][:, :], ACT.Silu).then_inc(silu_ready, 1)
                    sc.wait_ge(z_done, PRIMED + tiles(b, f) - 1)
                    sc.wait_ge(act_ready, PRIMED + 2 * tiles(b, f))
                    sc.activation(act_hi[:, 0, :], act[:, 1, :], ACT.Copy).then_inc(act_hi_ready, 1)
                    sc.wait_ge(sum_ready, PRIMED + tiles(b, f))
                    sc.activation(act_hi[:, 1, :], act[:, 2, :], ACT.Copy).then_inc(act_hi_ready, 1)
                    if f + 2 < FT:
                        split_hi(b, f + 2)
                sc.wait_ge(z_summed, PRIMED + b + 1)
                sc.activation(z_hi[:, :], zm[:, 2, :], ACT.Copy).then_inc(z_hi_ready, 1)
                sc.wait_ge(var_ready, PRIMED + b + 1)
                sc.activation(rstd[:, 1, :], rstd[:, 0, :], ACT.Sqrt).then_inc(std_ready, 1)

        @block.vector
        def _(dve):
            dve.wait_ge(consts_loaded, PRIMED + 64)
            dve.tensor_copy(ident16[:, :], ident[:, :]).then_inc(consts_ready, 1)
            dve.wait_ge(consts_ready, PRIMED + 3)
            dve.tensor_tensor(a_lo[:, :, :], a_raw[:, :, :], a_hi[:, :, :].bitcast(F32), ALU.subtract)\
                .then_inc(consts_ready, 1)
            dve.tensor_tensor(b2_lo[:, :], b2_raw[:, :], b2_hi[:, :].bitcast(F32), ALU.subtract)\
                .then_inc(consts_ready, 1)
            with dve.Fori(0, B) as b:
                links = 19
                done = [0]

                def link(ins):
                    done[0] += 1
                    ins.then_inc(step_done, 1)
                    dve.wait_ge(step_done, PRIMED + b * links + done[0])

                for c in range(KT):
                    k, n = slot(b, XC0 + c)
                    dve.wait_ge(xT_hi_ready, PRIMED + b * KT + c + 1)
                    dve.tensor_tensor(xT_lo[:, c, :], bank[k][:, :], xT_hi[:, c, :].bitcast(F32), ALU.subtract)\
                        .then_inc(drained[k], 1)
                for t in range(TT):
                    k, n = slot(b, U0 + t)
                    dve.wait_ge(filled[k], PRIMED + n + 1)
                    last = dve.tensor_copy(logits[:, t, :], bank[k][:, 2 * P:NU])
                link(last)

                def one_hot(values, m, where):
                    link(dve.tensor_reduce(best[:, m, :], values, AX.X, ALU.max))
                    link(dve.tensor_tensor(where, values, best[:, m, :].unsqueeze(2).to_broadcast([P, TT, E]),
                                           ALU.is_equal))
                    link(dve.tensor_tensor(where, where, desc[:, :].unsqueeze(1).to_broadcast([P, TT, E]), ALU.mult))
                    link(dve.tensor_reduce(best[:, m + 1, :], where, AX.X, ALU.max))
                    link(dve.tensor_tensor(where, where, best[:, m + 1, :].unsqueeze(2).to_broadcast([P, TT, E]),
                                           ALU.is_equal))

                one_hot(logits[:, :, :], 0, pick[:, 1, :, :])
                link(dve.scalar_tensor_tensor(pick[:, 2, :, :], pick[:, 1, :, :], FAR, logits[:, :, :],
                                              ALU.mult, ALU.add))
                one_hot(pick[:, 2, :, :], 2, pick[:, 3, :, :])
                dve.tensor_tensor(soft[:, 0, :], best[:, 2, :], best[:, 0, :], ALU.subtract).then_inc(gap_ready, 1)
                link(dve.tensor_tensor(pick[:, 0, :, :], pick[:, 3, :, :], pick[:, 1, :, :], ALU.subtract))
                for a in range(2):
                    last = dve.tensor_scalar(coef[:, a, :, :], pick[:, 1 - a, :, :], LORA_SCALE, None, ALU.mult)
                link(last)
                for a in range(2):
                    dve.tensor_copy(masks[:, a, :, :, :],
                                    coef[:, a, :, :].unsqueeze(3).to_broadcast([P, TT, E, R])).then_inc(masks_ready, 1)
                for t in range(TT):
                    k, n = slot(b, U0 + t)
                    for a in range(2):
                        ins = dve.tensor_tensor(
                            um[:, t, a, :, :].rearrange("p s (e r) -> p s e r", e=E),
                            bank[k][:, 0:2 * P].rearrange("p (s e r) -> p s e r", s=2, e=E),
                            coef[:, a, t, :].unsqueeze(1).unsqueeze(3).to_broadcast([P, 2, E, R]), ALU.mult)
                    ins.then_inc(drained[k], 1)
                dve.wait_ge(exp_ready, PRIMED + b + 1)
                link(dve.tensor_scalar(soft[:, 2, :], soft[:, 1, :], 1.0, None, ALU.add))
                dve.reciprocal(weight[:, 0, :], soft[:, 2, :]).then_inc(weight_ready, 1)
                dve.wait_ge(weight_ready, PRIMED + 3 * b + 1)
                dve.tensor_tensor(weight[:, 1, :], soft[:, 1, :], weight[:, 0, :], ALU.mult).then_inc(weight_ready, 1)
                dve.wait_ge(weight_ready, PRIMED + 3 * b + 2)
                dve.tensor_copy(weight_bc[:, :, :, :], weight[:, :, :].unsqueeze(3).to_broadcast([P, 2, TT, P]))\
                    .then_inc(weight_ready, 1)
                for a in range(4):
                    k, n = slot(b, UM0 + a)
                    dve.wait_ge(um_hi_ready, PRIMED + b * 4 + a + 1)
                    dve.tensor_tensor(umT_lo[:, a, :], bank[k][:, :], umT_hi[:, a, :].bitcast(F32), ALU.subtract)\
                        .then_inc(drained[k], 1)
                for f in range(FT):
                    for choice in range(2):
                        n = 2 * (tiles(b, f) - 1) + choice
                        dve.wait_ge(gated_ready, PRIMED + n + 1)
                        dve.wait_ge(h_ready[1], PRIMED + n + 1)
                        dve.wait_ge(sum_ready, PRIMED + tiles(b, f) - 1)
                        dve.tensor_tensor(act[:, choice, :], h_ps[1][:, :], gated[:, choice, :], ALU.mult)\
                            .then_inc(act_ready, 1)
                    for i in range(2):
                        dve.wait_ge(act_hi_ready, PRIMED + 2 * (tiles(b, f) - 1) + i + 1)
                        dve.tensor_tensor(act_lo[:, i, :], act[:, 1 + i, :], act_hi[:, i, :].bitcast(F32),
                                          ALU.subtract).then_inc(act_lo_ready, 1)
                dve.wait_ge(z_done, PRIMED + b * FT + FT)
                for i in range(2):
                    dve.tensor_tensor(zm[:, i, :], z_ps[i][:, :], maskT[:, i, :], ALU.mult).then_inc(z_masked, 1)
                dve.wait_ge(z_masked, PRIMED + 2 * b + 2)
                dve.tensor_tensor(zm[:, 2, :], zm[:, 0, :], zm[:, 1, :], ALU.add).then_inc(z_summed, 1)
                dve.wait_ge(z_hi_ready, PRIMED + b + 1)
                dve.tensor_tensor(z_lo[:, :], zm[:, 2, :], z_hi[:, :].bitcast(F32), ALU.subtract)\
                    .then_inc(z_lo_ready, 1)
                dve.wait_ge(out_stored, PRIMED + 16 * b)
                for t in range(TT):
                    k, n = y_slot(b, t)
                    dve.wait_ge(filled[k], PRIMED + n + 1)
                    dve.tensor_tensor(x3[:, t, :], bank[k][:, :], x2[:, t, :], ALU.add).then_inc(drained[k], 1)
                    dve.wait_ge(drained[k], PRIMED + n + 1)
                    last = dve.bn_stats(stats[:, t, :], x3[:, t, :])
                link(last)
                moments(dve, stats, part, mean[:, :], rstd[:, 0, :], link).then_inc(var_ready, 1)
                dve.wait_ge(std_ready, PRIMED + b + 1)
                link(dve.reciprocal(rstd[:, 2, :], rstd[:, 1, :]))
                for t in range(TT):
                    dve.tensor_scalar(x3[:, t, :], x3[:, t, :], mean[:, t:t + 1], rstd[:, 2, t:t + 1],
                                      ALU.subtract, ALU.mult).then_inc(normed, 1)
                assert done[0] == links

        @block.tensor
        def _(pe):
            def up(b, f, i):
                if i == 0:
                    pe.wait_ge(w_lo_ready, PRIMED + 2 * tiles(b, f) - 1)
                    pe.wait_ge(silu_ready, PRIMED + 2 * (tiles(b, f) - 1))
                else:
                    pe.wait_ge(act_ready, PRIMED + 2 * (tiles(b, f) - 1))
                s = f % 2
                for c in range(KT):
                    cols = slice(i * D + c * P, i * D + (c + 1) * P)
                    matmul_split(pe, h_ps[i][:, :], up_hi[:, s, cols], up_lo[:, s, cols],
                                 xT_hi[:, c, :], xT_lo[:, c, :], c == 0, False)
                cols = slice(2 * D + i * P, 2 * D + (i + 1) * P)
                matmul_split(pe, h_ps[i][:, :], up_hi[:, s, cols], up_lo[:, s, cols],
                             umT_hi[:, i, :], umT_lo[:, i, :], False, True).then_inc(h_ready[i], 1)

            def second(b, f, i):
                if i == 0:
                    pe.wait_ge(silu_ready, PRIMED + 2 * tiles(b, f) - 1)
                else:
                    pe.wait_ge(act_ready, PRIMED + 2 * tiles(b, f) - 1)
                s = f % 2
                cols = slice(2 * D + i * P, 2 * D + (i + 1) * P)
                rhs = 2 + i
                last = None
                for l, r in ((up_hi, umT_hi), (up_lo, umT_hi), (up_hi, umT_lo)):
                    last = pe.matmul(h_ps[i][:, :], l[:, s, cols], r[:, rhs, :], start=False, stop=True,
                                     skip_group_check=True)
                last.then_inc(h_ready[i], 1)

            def down(b, f):
                pe.wait_ge(act_lo_ready, PRIMED + 2 * tiles(b, f))
                pe.wait_ge(w_lo_ready, PRIMED + 2 * tiles(b, f))
                s = f % 3
                for t in range(TT):
                    matmul_split(pe, bank[t][:, :], act_hi[:, 1, bass.ts(t, P)], act_lo[:, 1, bass.ts(t, P)],
                                 down_hi[:, s, P:DOWN], down_lo[:, s, P:DOWN], f == 0, False)

            def adapters(b, f):
                s = f % 3
                for i in (1, 0):
                    last = matmul_split(pe, z_ps[i][:, :], down_hi[:, s, 0:P], down_lo[:, s, 0:P],
                                        act_hi[:, 1 - i, :], act_lo[:, 1 - i, :], f == 0, f == FT - 1)
                last.then_inc(z_done, 1)

            pe.wait_ge(consts_ready, PRIMED + 5)
            with pe.Fori(0, B) as b:
                pe.wait_ge(x2_loaded, PRIMED + 16 * b + 16)
                for c in range(KT):
                    k, n = slot(b, XC0 + c)
                    pe.wait_ge(drained[k], PRIMED + n)
                    for t in range(TT):
                        last = pe.transpose(bank[k][:, bass.ts(t, P)], x2[:, t, bass.ts(c, P)], ident[:, :])
                    last.then_inc(filled[k], 1)
                for c in range(KT):
                    k, n = slot(b, XC0 + c)
                    pe.wait_ge(drained[k], PRIMED + n + 1)
                for t in range(TT):
                    k, n = slot(b, U0 + t)
                    for c in range(KT):
                        last = matmul_split(pe, bank[k][:, 0:NU], xT_hi[:, c, bass.ts(t, P)],
                                            xT_lo[:, c, bass.ts(t, P)], a_hi[:, c, :], a_lo[:, c, :],
                                            c == 0, c == KT - 1)
                    last.then_inc(filled[k], 1)
                for t in range(TT):
                    k, n = slot(b, U0 + t)
                    pe.wait_ge(drained[k], PRIMED + n + 1)
                for a in range(4):
                    k, n = slot(b, UM0 + a)
                    for t in range(TT):
                        last = pe.transpose(bank[k][:, bass.ts(t, P)], um[:, t, a // 2, a % 2, :], ident[:, :])
                    last.then_inc(filled[k], 1)
                k, n = slot(b, MT)
                pe.wait_ge(masks_ready, PRIMED + 2 * b + 2)
                pe.wait_ge(drained[k], PRIMED + n)
                half = bank[k][:, :].bitcast(BF16).rearrange("p (a t m) -> p a t m", a=2, t=TT)
                for a in range(2):
                    for t in range(TT):
                        last = pe.transpose(half[:, a, t, :], masks[:, a, t, :, :].rearrange("p e r -> p (e r)"),
                                            ident16[:, :])
                last.then_inc(filled[k], 1)
                pe.wait_ge(weight_ready, PRIMED + 3 * b + 3)
                for a in range(2):
                    k, n = slot(b, WB0 + a)
                    pe.wait_ge(drained[k], PRIMED + n)
                    for t in range(TT):
                        last = pe.matmul(bank[k][:, bass.ts(t, P)], weight_bc[:, a, t, :], ident[:, :],
                                         start=True, stop=True)
                    last.then_inc(filled[k], 1)
                for a in range(4):
                    k, n = slot(b, UM0 + a)
                    pe.wait_ge(drained[k], PRIMED + n + 1)
                for f in range(FT + 1):
                    if f < FT:
                        up(b, f, 0)
                        up(b, f, 1)
                    if f:
                        if f == 1:
                            for t in range(TT):
                                k, n = y_slot(b, t)
                                pe.wait_ge(drained[k], PRIMED + n)
                        down(b, f - 1)
                    if f < FT:
                        second(b, f, 0)
                        second(b, f, 1)
                    if f:
                        adapters(b, f - 1)
                pe.wait_ge(z_lo_ready, PRIMED + b + 1)
                for t in range(TT):
                    k, n = y_slot(b, t)
                    matmul_split(pe, bank[k][:, :], z_hi[:, bass.ts(t, P)], z_lo[:, bass.ts(t, P)],
                                 b2_hi[:, :], b2_lo[:, :], False, True).then_inc(filled[k], 1)



def decoder_layer(nc, a, out):
    x2 = nc.dram_tensor("x2_scratch", (B * T, D), F32, kind="Internal").ap()
    attention_and_experts(nc, a["xT"], a["x"], a["wT"], a["bias_rows"], a["bias_parts"], a["bias_pick"], a["bo"],
                          a["rope"], a["head_mask"], a["ident"], a["w1"], a["w2"], x2)
    mixture(nc, x2, a["a13g"], a["stream"], a["b2T"], a["ident"], a["descending"], out)



def host_arrays(inputs):
    import numpy as np
    x = np.ascontiguousarray(inputs["x"]).reshape(B * T, D)
    pos = np.arange(T, dtype=np.float32)
    inv = (1.0 / 10000.0 ** (np.arange(0, DK, 2, dtype=np.float32) / DK)).astype(np.float32)
    ang = pos[:, None] * inv[None, :]
    sin, cos = np.sin(ang), np.cos(ang)
    rope = np.empty((P, 2, TT, DK), np.float32)
    rope[:, 0] = np.repeat(cos, 2, axis=1).reshape(TT, P, DK).transpose(1, 0, 2)
    rope[:, 1] = np.stack([-sin, sin], axis=-1).reshape(TT, P, DK).transpose(1, 0, 2)
    mask = np.zeros((P, GH, E1), np.float32)
    for j in range(GH):
        mask[j * DK:(j + 1) * DK, j] = 1.0
    bias_rows = np.zeros((P, D), np.float32)
    bias_parts = np.zeros((P, 2), np.float32)
    bias_pick = np.zeros((P, 4, P), np.float32)
    for i, c in enumerate("qkvg"):
        for r in range(2):
            bias_rows[32 * i + r] = inputs[f"L0_attn_b{c}"]
            bias_parts[32 * i + r, r] = 1.0
            bias_pick[32 * i + r, i] = 1.0
    ffn = {k[7:]: np.asarray(v) for k, v in inputs.items() if k.startswith("L0_ffn")}
    stream = np.empty((FT, P, UP + DOWN), np.float32)
    for i, w in enumerate(("w1", "w3")):
        stream[:, :, i * D:(i + 1) * D] = ffn[w].reshape(FT, P, KT, P).transpose(0, 3, 2, 1).reshape(FT, P, D)
    for i, w in enumerate(("b1", "b3")):
        stream[:, :, 2 * D + i * P:2 * D + (i + 1) * P] = \
            ffn[w].transpose(0, 2, 1).reshape(P, FT, P).transpose(1, 0, 2)
    stream[:, :, UP:UP + P] = ffn["a2"].reshape(P, FT, P).transpose(1, 2, 0)
    stream[:, :, UP + P:] = ffn["w2"].T.reshape(FT, P, D)
    return dict(
        stream=stream,
        a13g=np.concatenate([ffn["a1"].reshape(P, D), ffn["a3"].reshape(P, D), ffn["gate_w"]]).T.copy(),
        b2T=np.ascontiguousarray(ffn["b2"].transpose(0, 2, 1).reshape(P, D)),
        descending=np.ascontiguousarray(np.broadcast_to(np.arange(E, 0, -1, dtype=np.float32), (P, E))),
        xT=np.ascontiguousarray(x.T), x=x,
        wT=np.stack([inputs[f"L0_attn_W{c}"].T for c in "qkvgo"]),
        bias_rows=bias_rows, bias_parts=bias_parts, bias_pick=bias_pick.reshape(P, 4 * P),
        bo=np.ascontiguousarray(np.broadcast_to(inputs["L0_attn_bo"], (P, D))),
        w1=np.ascontiguousarray(inputs["fside_BxS2xS2_0"].reshape(B * D, D)),
        w2=np.ascontiguousarray(inputs["ctx_1024"].reshape(B * D, D // 2)),
        rope=rope, head_mask=mask.reshape(P, GE), ident=np.eye(P, dtype=np.float32))


def kernel(**inputs):
    import concourse.bacc as bacc
    from concourse.bass_utils import run_bass_kernel_spmd

    nc = bacc.Bacc("TRN2", target_bir_lowering=False, num_devices=1)
    arrays = host_arrays(inputs)
    a = {name: nc.dram_tensor("in_" + name, v.shape, mybir.dt.from_np(v.dtype), kind="ExternalInput").ap()
         for name, v in arrays.items()}
    out = nc.dram_tensor("out", (B * T, D), F32, kind="ExternalOutput").ap()
    decoder_layer(nc, a, out)
    r = run_bass_kernel_spmd(nc, [{"in_" + name: v for name, v in arrays.items()}], core_ids=[0])
    return r.results[0]["out"].reshape(B, T, D)
```

```python
from contextlib import ExitStack

import concourse.bass as bass
from concourse import mybir

F32 = mybir.dt.float32
F32R = mybir.dt.float32r
BF16 = mybir.dt.bfloat16
ALU = mybir.AluOpType
ACT = mybir.ActivationFunctionType
AX = mybir.AxisListType

P = 128
B = 4
T = 512
D = 512
H = 16
DK = D // H
CS = 64
TT = T // P
KT = D // P
GH = P // DK
NG = H // GH
E1 = DK + 1
GE = GH * E1
LN_EPS = 1e-5
DEN_EPS = 1e-6

Q_EPS = 1e-6
QMAX = 127.0
ROUND = 1.5 * 2.0 ** 23
CHANNELS = (D, D // 2)

PRIMED = 1

RING = 4
QT, PQ, PK, PV, AT, PG, OUT = ("qT", "q", "k", "v", "attT", "gate", "out")
MX, MW, RS, SS, XT0, XT1, SW, WT0, WT1 = ("amax_x", "amax_w", "1/s", "s", "xT0", "xT1", "w_scale", "wT0", "wT1")
OX = tuple(f"out{t}" for t in range(TT))


def section(t):
    maxima, scaling = [(t // 2, MX), (t // 2, MW)], [(t // 2, RS), (t // 2, SS)]
    own = [[(t, QT)], [(t + 1, PQ)], [(t + 1, PK)], [(t + 1, PV)], [(t, AT), (t + 1, PG)], [(t, OUT)]]
    beside = {
        0: [[], [], [], [], maxima, []],
        1: [scaling, [], [], [(0, XT0), (0, XT1)], [], []],
        2: [[], [], [(0, SW), (0, WT0), (0, WT1)], [(0, o) for o in OX], [], maxima],
        3: [[], scaling, [], [(1, XT0)], [], [(1, SW), (1, WT0)] + [(1, o) for o in OX]],
    }[t]
    return [item for a, b in zip(own, beside) for item in a + b]


ORDER = [item for t in range(TT) for item in section(t)]
PER_BANK = len(ORDER) // RING
ATTENTION_ITEMS = (QT, PQ, PK, PV, AT, PG, OUT)


def present(iteration, place):
    t, item = ORDER[place]
    if item not in ATTENTION_ITEMS:
        return 1 <= iteration <= B
    if item in (PQ, PK, PV, PG):
        return 0 <= iteration * TT + t < B * TT
    return 0 <= iteration < B


def ring_steps():
    steps, value = {}, [0] * RING
    for iteration in range(-1, B + 1):
        for k in range(RING):
            there = [n for n in range(k, len(ORDER), RING) if present(iteration, n)]
            for n in there:
                after = (iteration + 1) * PER_BANK + (PER_BANK if n == there[-1] else n // RING + 1)
                steps[iteration, n] = (value[k], after - value[k])
                value[k] = after
    return steps


STEPS = ring_steps()
CONSTS = 16 * 7


def matmul_split(pe, out, lhs_hi, lhs_lo, rhs_hi, rhs_lo, start, stop):
    pe.matmul(out, lhs_hi, rhs_hi, start=start, stop=False)
    pe.matmul(out, lhs_lo, rhs_hi, start=False, stop=False)
    return pe.matmul(out, lhs_hi, rhs_lo, start=False, stop=stop)


def moments(dve, stats, part, mean, var_eps, wait):
    dve.tensor_tensor(part[:, :, 0:2], stats[:, :, 1:3], stats[:, :, 4:6], ALU.add)
    wait(dve.tensor_tensor(part[:, :, 2], stats[:, :, 1], stats[:, :, 4], ALU.subtract))
    dve.tensor_scalar(mean, part[:, :, 0], 0.5, None, ALU.mult)
    dve.tensor_scalar(part[:, :, 3], part[:, :, 1], 1.0 / D, LN_EPS, ALU.mult, ALU.add)
    wait(dve.scalar_tensor_tensor(part[:, :, 4], part[:, :, 2], 0.25, part[:, :, 2], ALU.mult, ALU.mult))
    return dve.tensor_tensor(var_eps, part[:, :, 3], part[:, :, 4], ALU.add)


def attention_and_experts(nc, xT, x, wT, bias_rows, bias_parts, bias_pick, bo, rope, head_mask, ident_in,
                          w1, w2, x2_dram):
    with ExitStack() as ctx:
        def sb(name, shape, dt=F32):
            return ctx.enter_context(nc.sbuf_tensor(name, shape, dt))

        primed = []

        def sem(name):
            primed.append(ctx.enter_context(nc.semaphore(name)))
            return primed[-1]

        def sems(name):
            return [sem(name + "1"), sem(name + "2")]

        w_raw = sb("w_raw", [P, KT, D])
        w_hi = sb("w_hi", [P, 5, KT, D], F32R)
        w_lo = sb("w_lo", [P, 5, KT, D], F32R)
        bias_hl = sb("bias_hl", [P, D], F32R)
        bias_part = sb("bias_part", [P, 2])
        pick = sb("pick", [P, 4, P], F32R)
        ident = sb("ident", [P, P])
        ident16 = sb("ident16", [P, P], BF16)
        ones = sb("ones", [P, P])
        mask = sb("mask", [P, GE])
        ropes = sb("ropes", [P, 2, TT, DK])
        bo_bc = sb("bo_bc", [P, D])
        x_tok = sb("x_tok", [P, TT, D])
        stats = sb("stats", [P, TT, 6])
        part = sb("part", [P, TT, 5])
        mean = sb("mean", [P, TT])
        rstd = sb("rstd", [P, 3, TT])
        xT_raw = sb("xT_raw", [P, 2, KT, P])
        xT_hi = sb("xT_hi", [P, 2, KT, P], F32R)
        xT_lo = sb("xT_lo", [P, 2, KT, P], F32R)
        qk = sb("qk", [P, 2 * D])
        rot_a = sb("rot_a", [P, 2 * D])
        rot_b = sb("rot_b", [P, 2 * D])
        feat = sb("feat", [P, 2 * D])
        v_ext = sb("v_ext", [P, 2, H, E1])
        gate = sb("gate", [P, D])
        q_T = sb("q_T", [P, NG, P])
        s_bd = sb("s_bd", [P, 2, NG, GE])
        rden = sb("rden", [P, 2, H])
        att = sb("att", [P, D])
        att_hi = sb("att_hi", [P, KT, P], F32R)
        att_lo = sb("att_lo", [P, KT, P], F32R)
        x1 = sb("x1", [P, TT, D])
        top = sb("top", [P, 2, D])
        diag = top[:, :, :].rearrange("p i (c t) -> p i c t", t=P)
        amax = sb("amax", [P, 2, KT])
        small = sb("small", [P, 4, KT])
        rows = sb("rows", [P, 2, D])
        row_max = sb("row_max", [P, 2, TT])
        scale = sb("scale", [P, 2, TT])
        inverse = sb("inverse", [P, 2, TT])
        scaled = [sb("scaled_x", [P, TT, D]), sb("scaled_w", [P, TT, D])]
        q = [sb("qx", [P, TT, D], BF16), sb("qw", [P, TT, D], BF16)]
        qT = [sb("qxT", [P, KT, T], BF16), sb("qwT", [P, KT, D], BF16)]
        gu = scaled[0]
        staging = [w_raw, scaled[0], scaled[1]]
        sl = scaled[1]
        act_in = sb("act_in", [P, TT, D // 2])
        e_stats = stats
        e_part = sb("e_part", [P, TT, 5])
        e_mean = sb("e_mean", [P, TT])
        e_rstd = sb("e_rstd", [P, 3, TT])
        e_shift = e_mean

        ring = [ctx.enter_context(nc.psum_tensor(f"ring{i}", [P, 512], F32)) for i in range(RING)]
        s_ps = ctx.enter_context(nc.psum_tensor("s_ps", [P, 2, 512], F32))
        n_ps = ctx.enter_context(nc.psum_tensor("n_ps", [P, 2, 512], F32))

        consts_loaded = sem("consts_loaded")
        w_loaded = [sem(f"w_loaded{i}") for i in range(5)]
        w_hi_ready = sem("w_hi_ready")
        w_lo_ready = sem("w_lo_ready")
        bias_hi_ready = sem("bias_hi_ready")
        bias_ready = sem("bias_ready")
        ones_ready = sem("ones_ready")
        v_ones_ready = sem("v_ones_ready")
        xT_loaded = sems("xT_loaded")
        x_loaded = sem("x_loaded")
        xhi_ready = sem("xhi_ready")
        xlo_ready = sem("xlo_ready")
        filled = [sem(f"filled{i}") for i in range(RING)]
        drained = [sem(f"drained{i}") for i in range(RING)]
        rot_a_ready = sem("rot_a_ready")
        rot_b_ready = sem("rot_b_ready")
        rotated = sem("rotated")
        neg_ready = sem("neg_ready")
        exp_ready = sem("exp_ready")
        feat_ready = sem("feat_ready")
        s_updated = sem("s_updated")
        s_masked = sem("s_masked")
        num_ready = sem("num_ready")
        den_ready = sem("den_ready")
        rden_ready = sem("rden_ready")
        gated = sem("gated")
        att_ready = sem("att_ready")
        att_hi_ready = sem("att_hi_ready")
        xres_ready = sem("xres_ready")
        stats_ready = sem("stats_ready")
        moment_ready = sem("moment_ready")
        var_ready = sem("var_ready")
        std_ready = sem("std_ready")
        rstd_ready = sem("rstd_ready")
        normed = sem("normed")
        ew_loaded = sems("ew_loaded")
        x_top_ready = sems("x_top_ready")
        w_top_ready = sems("w_top_ready")
        small_done = sem("small_done")
        ratio_ready = sems("ratio_ready")
        root_ready = sems("root_ready")
        s_ready = sems("s_ready")
        diag_ready = sems("diag_ready")
        x_scaled = sems("x_scaled")
        w_scaled = sems("w_scaled")
        scale_ready = sems("scale_ready")
        sw_diag_ready = sems("sw_diag_ready")
        shifted = sems("shifted")
        clamped = sems("clamped")
        q_ready = sems("q_ready")
        silu_ready = sem("silu_ready")
        act_ready = sem("act_ready")
        summed = sem("summed")
        e_stats_ready = sem("e_stats_ready")
        e_moment_ready = sem("e_moment_ready")
        e_var_ready = sem("e_var_ready")
        e_std_ready = sem("e_std_ready")
        e_rstd_ready = sem("e_rstd_ready")
        e_normed = sem("e_normed")
        x2_stored = sem("x2_stored")

        def place(iteration, key):
            n = ORDER.index(key)
            if isinstance(iteration, int):
                before, step = STEPS[iteration, n]
            else:
                before, step = (iteration + 1) * PER_BANK + n // RING, 1
            return n % RING, before, before + step, step

        def slot(b, t, item):
            if item in (PQ, PK, PV, PG):
                return place(b - 1, (TT, item)) if t == 0 else place(b, (t, item))
            return place(b, (t, item))

        def tile_no(b, t):
            return b * TT + t + 1

        def ahead(b, t, n):
            return b + (t + n) // TT, (t + n) % TT

        def following(b, t):
            return ahead(b, t, 1)

        def exists(b, t):
            return not isinstance(b, int) or tile_no(b, t) <= B * TT

        def has_next(b, t):
            return exists(*following(b, t))

        def has_expert(b):
            return not isinstance(b, int) or b > 0

        def iterations(eng, body):
            body(0)
            with eng.Fori(1, B - 1) as b:
                body(b)
            body(B - 1)

        def expert_tokens(i, which):
            return (x1, act_in)[which] if i == 0 else w_raw

        with nc.Block() as start:
            @start.gpsimd
            def _(pool):
                for semaphore in primed:
                    pool.sem_inc(semaphore, PRIMED)

        block = ctx.enter_context(nc.Block())

        @block.sync
        def _(sp):
            for t in range(2):
                sp.dma_start(xT_raw[:, t, :, :], xT[:, bass.ts(t, P)]
                             .rearrange("(k p) t -> p k t", p=P)).then_inc(xT_loaded[t], 16)
            for i in range(5):
                if i == 1:
                    sp.wait_ge(w_loaded[0], PRIMED + 16)
                if i >= 3:
                    sp.wait_ge(w_lo_ready, PRIMED + i - 2)
                sp.dma_start(staging[i % 3][:, :, :], wT[i].rearrange("(k p) n -> p k n", p=P))\
                    .then_inc(w_loaded[i], 16)
            sp.dma_start(x_tok[:, :, :], x[0:T, :].rearrange("(t p) d -> p t d", p=P)).then_inc(x_loaded, 16)
            sp.wait_ge(w_lo_ready, PRIMED + 5)

            def load_w(e, which):
                C = CHANNELS[which]
                if which:
                    sp.wait_ge(w_scaled[0], PRIMED + e + 1)
                elif not (isinstance(e, int) and e == 0):
                    sp.wait_ge(w_scaled[1], PRIMED + e)
                sp.dma_start(w_raw[:, :, 0:C], (w1, w2)[which][bass.ts(e, D), :]
                             .rearrange("(t p) d -> p t d", p=P)).then_inc(ew_loaded[which], 16)

            def store_x2(e):
                for h in range(2):
                    sp.wait_ge(e_normed, PRIMED + e * TT + 2 * h + 2)
                    sp.dma_start(x2_dram[bass.ds(e * T + h * 2 * P, 2 * P), :].rearrange("(t p) d -> p t d", p=P),
                                 gu[:, 2 * h:2 * h + 2, :]).then_inc(x2_stored, 16)

            def body(b):
                if has_expert(b):
                    load_w(b - 1, 1)
                load_w(b, 0)
                if has_next(b, TT - 1):
                    sp.wait_ge(normed, PRIMED + b * TT + TT)
                    sp.dma_start(x_tok[:, :, :], x[bass.ts(b + 1, T), :]
                                 .rearrange("(t p) d -> p t d", p=P)).then_inc(x_loaded, 16)
                if has_expert(b):
                    store_x2(b - 1)
            iterations(sp, body)
            load_w(B - 1, 1)
            store_x2(B - 1)
            sp.wait_ge(x2_stored, PRIMED + 32 * B)

        @block.gpsimd
        def _(pool):
            for s in range(2):
                pool.memset(v_ext[:, s, :, DK:E1], 1.0).then_inc(v_ones_ready, 1)
            pool.wait_ge(consts_loaded, PRIMED + CONSTS)

            def split(b, t):
                pool.wait_ge(xhi_ready, PRIMED + tile_no(b, t))
                pool.tensor_tensor(xT_lo[:, t % 2, :, :], xT_raw[:, t % 2, :, :],
                                   xT_hi[:, t % 2, :, :].bitcast(F32), ALU.subtract).then_inc(xlo_ready, 1)

            def rotate(b, t):
                sin = ropes[:, 1, t, :].rearrange("p (i two) -> p i two", two=2)
                for i, item in enumerate((PQ, PK)):
                    k, _, done, _ = slot(b, t, item)
                    pool.wait_ge(drained[k], PRIMED + done)
                    if not (isinstance(b, int) and tile_no(b, t) == 1):
                        pool.wait_ge(feat_ready, PRIMED + 2 * (tile_no(b, t) - 1) - 1 + i)
                    q4 = qk[:, bass.ts(i, D)].rearrange("p (h i two) -> p h i two", i=DK // 2, two=2)
                    b4 = rot_b[:, bass.ts(i, D)].rearrange("p (h i two) -> p h i two", i=DK // 2, two=2)
                    for two in range(2):
                        pool.tensor_tensor(b4[:, :, :, two], q4[:, :, :, 1 - two],
                                           sin[:, :, two].unsqueeze(1).to_broadcast([P, H, DK // 2]),
                                           ALU.mult).then_inc(rot_b_ready, 1)
                    if i == 0:
                        pool.tensor_tensor(rot_a[:, 0:D].rearrange("p (h i) -> p h i", i=DK),
                                           qk[:, 0:D].rearrange("p (h i) -> p h i", i=DK),
                                           ropes[:, 0, t, :].unsqueeze(1).to_broadcast([P, H, DK]), ALU.mult)\
                            .then_inc(rot_a_ready, 1)

            def residual(b, t):
                if t == 0:
                    pool.wait_ge(x_loaded, PRIMED + b * 16 + 16)
                pool.tensor_tensor(x_tok[:, t, :], x_tok[:, t, :], bo_bc[:, :], ALU.add).then_inc(xres_ready, 1)

            def diagonals(e, which):
                kc = CHANNELS[which] // P
                pool.wait_ge(s_ready[which], PRIMED + e + 1)
                if isinstance(e, int) and e == 0:
                    pool.wait_ge(consts_loaded, PRIMED + CONSTS)
                for i in range(2):
                    pool.tensor_tensor(diag[:, i, 0:kc, :],
                                       ident[:, :].unsqueeze(1).to_broadcast([P, kc, P]),
                                       small[:, 3 - i, 0:kc].unsqueeze(2).to_broadcast([P, kc, P]),
                                       ALU.mult).then_inc(diag_ready[which], 1)

            def scale_weights(e, which):
                C = CHANNELS[which]
                k, _, done, _ = place(e + 1, (which, SS))
                pool.wait_ge(drained[k], PRIMED + done)
                pool.tensor_tensor(scaled[1][:, :, 0:C], w_raw[:, :, 0:C],
                                   rows[:, 1, 0:C].unsqueeze(1).to_broadcast([P, TT, C]),
                                   ALU.mult).then_inc(w_scaled[which], 1)

            def scales_diagonal(e, which):
                pool.wait_ge(scale_ready[which], PRIMED + 2 * e + 2)
                pool.tensor_tensor(diag[:, 0, :, :],
                                   ident[:, :].unsqueeze(1).to_broadcast([P, KT, P]),
                                   scale[:, 1, :].unsqueeze(2).to_broadcast([P, KT, P]),
                                   ALU.mult).then_inc(sw_diag_ready[which], 1)

            def expert_residual(e):
                for t in range(TT):
                    k, _, done, _ = place(e + 1, (1, OX[t]))
                    pool.wait_ge(drained[k], PRIMED + done)
                    pool.tensor_tensor(gu[:, t, :], gu[:, t, :], x1[:, t, :], ALU.add).then_inc(summed, 1)

            for t in range(2):
                split(0, t)
            rotate(0, 0)

            def body(b):
                for t in range(TT):
                    which, second = divmod(t, 2)
                    residual(b, t)
                    if has_expert(b) and second:
                        scale_weights(b - 1, which)
                    if has_next(b, t):
                        rotate(*following(b, t))
                    if has_expert(b) and second:
                        scales_diagonal(b - 1, which)
                    if exists(*ahead(b, t, 2)):
                        split(*ahead(b, t, 2))
                    if has_expert(b) and not second:
                        diagonals(b - 1, which)
                if has_expert(b):
                    expert_residual(b - 1)
            iterations(pool, body)
            for which in range(2):
                diagonals(B - 1, which)
                scale_weights(B - 1, which)
                scales_diagonal(B - 1, which)
            expert_residual(B - 1)

        @block.scalar
        def _(act):
            for dst, src in ((bias_part[:, :], bias_parts), (att[:, :], bias_rows),
                             (gate[:, :], bias_pick), (ident[:, :], ident_in), (mask[:, :], head_mask),
                             (ropes[:, :, :, :], rope), (bo_bc[:, :], bo)):
                act.dma_start(dst, src).then_inc(consts_loaded, 16)

            def x_hi(b, t):
                act.wait_ge(xT_loaded[t % 2], PRIMED + 16 * (b * 2 + t // 2 + 1))
                if not (isinstance(b, int) and tile_no(b, t) <= 2):
                    k, _, done, _ = slot(*ahead(b, t, -2), PG)
                    act.wait_ge(filled[k], PRIMED + done)
                act.activation(xT_hi[:, t % 2, :, :], xT_raw[:, t % 2, :, :], ACT.Copy).then_inc(xhi_ready, 1)

            def load_xT(b, t):
                act.wait_ge(xlo_ready, PRIMED + tile_no(b, t) - 2)
                act.dma_start(xT_raw[:, t % 2, :, :], xT[:, bass.ds(b * T + t * P, P)]
                              .rearrange("(k p) t -> p k t", p=P)).then_inc(xT_loaded[t % 2], 16)

            for t in range(2):
                x_hi(0, t)
            load_xT(0, 2)

            def weight_hi(i):
                act.wait_ge(w_loaded[i], PRIMED + 16)
                act.activation(w_hi[:, i, :, :], staging[i % 3][:, :, :], ACT.Copy).then_inc(w_hi_ready, 1)

            def qk_out(b, t, item):
                k, _, done, step = slot(b, t, item)
                act.wait_ge(filled[k], PRIMED + done)
                if not (isinstance(b, int) and tile_no(b, t) == 1):
                    act.wait_ge(rot_b_ready, PRIMED + (4 * (tile_no(b, t) - 1) - (2 if item == PQ else 0)))
                    act.wait_ge(rot_a_ready, PRIMED + (2 * (tile_no(b, t) - 1) - (1 if item == PQ else 0)))
                act.activation(qk[:, bass.ts((PQ, PK).index(item), D)], ring[k][:, :], ACT.Copy)\
                    .then_inc(drained[k], step)

            def v_out(b, t):
                k, _, done, step = slot(b, t, PV)
                act.wait_ge(filled[k], PRIMED + done)
                act.wait_ge(s_updated, PRIMED + 2 * (tile_no(b, t) - 1))
                if t < 2:
                    act.wait_ge(v_ones_ready, PRIMED + 2)
                act.activation(v_ext[:, t % 2, :, 0:DK], ring[k][:, :].rearrange("p (h e) -> p h e", e=DK),
                               ACT.Copy).then_inc(drained[k], step)

            def gate_out(b, t):
                k, _, done, step = slot(b, t, PG)
                act.wait_ge(filled[k], PRIMED + done)
                if isinstance(b, int) and b == 0 and t == 0:
                    act.wait_ge(bias_ready, PRIMED + 2)
                act.wait_ge(gated, PRIMED + 2 * (tile_no(b, t) - 1))
                act.activation(gate[:, :], ring[k][:, :], ACT.Tanh, scale=0.5).then_inc(drained[k], step)

            def exponential(b, t):
                for i in range(2):
                    act.wait_ge(neg_ready, PRIMED + 2 * (tile_no(b, t) - 1) + i + 1)
                    half = bass.ts(i, D)
                    act.activation(rot_b[:, half], rot_b[:, half], ACT.Exp).then_inc(exp_ready, 1)

            def qT_out(b, t):
                k, _, done, step = slot(b, t, QT)
                act.wait_ge(filled[k], PRIMED + done)
                act.wait_ge(num_ready, PRIMED + 2 * (tile_no(b, t) - 1))
                act.activation(q_T[:, :, :], ring[k][:, :].rearrange("p (g t) -> p g t", g=NG), ACT.Copy)\
                    .then_inc(drained[k], step)

            def attT_hi(b, t):
                k, _, done, _ = slot(b, t, AT)
                act.wait_ge(filled[k], PRIMED + done)
                if not (isinstance(b, int) and tile_no(b, t) == 1):
                    before = ahead(b, t, -1)
                    k_out, _, done, _ = slot(*before, OUT)
                    act.wait_ge(filled[k_out], PRIMED + done)
                act.activation(att_hi[:, :, :], ring[k][:, :].rearrange("p (g t) -> p g t", g=KT), ACT.Copy)\
                    .then_inc(att_hi_ready, 1)

            def roots(e, which):
                kc = CHANNELS[which] // P
                act.wait_ge(ratio_ready[which], PRIMED + e + 1)
                act.activation(small[:, 2, 0:kc], small[:, 1, 0:kc], ACT.Sqrt).then_inc(root_ready[which], 1)

            def channel_rows(e, which):
                C = CHANNELS[which]
                for i, item in enumerate((RS, SS)):
                    k, _, done, step = place(e + 1, (which, item))
                    act.wait_ge(filled[k], PRIMED + done)
                    act.activation(rows[:, i, 0:C], ring[k][:, 0:C], ACT.Copy).then_inc(drained[k], step)

            def quantised(e, which, i):
                act.wait_ge(clamped[which], PRIMED + 2 * e + i + 1)
                for j in range(CHANNELS[which] // P // 2):
                    pair = bass.ts(j, 2 * P)
                    act.activation(q[i][:, :, pair], scaled[i][:, :, pair], ACT.Copy, bias=-ROUND)\
                        .then_inc(q_ready[which], 1)

            def transposed_out(e, which, i):
                for j in range(CHANNELS[which] // P // 2):
                    k, _, done, step = place(e + 1, (which, ((XT0, XT1), (WT0, WT1))[i][j]))
                    act.wait_ge(filled[k], PRIMED + done)
                    act.activation(qT[i][:, 2 * j:2 * j + 2, :],
                                   ring[k][:, :].bitcast(BF16).rearrange("p (c t) -> p c t", c=2),
                                   ACT.Copy).then_inc(drained[k], step)

            def scales_row(e, which):
                k, _, done, step = place(e + 1, (which, SW))
                act.wait_ge(filled[k], PRIMED + done)
                act.activation(rows[:, 0, :], ring[k][:, :], ACT.Copy).then_inc(drained[k], step)

            def silu(e):
                k, _, done, _ = place(e + 1, (0, OX[TT - 1]))
                act.wait_ge(drained[k], PRIMED + done)
                act.activation(sl[:, :, 0:D // 2], gu[:, :, 0:D // 2], ACT.Silu).then_inc(silu_ready, 1)

            def expert_deviation(e):
                act.wait_ge(e_var_ready, PRIMED + e + 1)
                act.activation(e_rstd[:, 1, :], e_rstd[:, 0, :], ACT.Sqrt).then_inc(e_std_ready, 1)

            def expert_normalise(e):
                act.wait_ge(e_rstd_ready, PRIMED + 2 * e + 2)
                for t in range(TT):
                    act.activation(gu[:, t, :], gu[:, t, :], ACT.Identity, scale=e_rstd[:, 2, t:t + 1],
                                   bias=e_shift[:, t:t + 1]).then_inc(e_normed, 1)

            def deviation(b):
                act.wait_ge(var_ready, PRIMED + b + 1)
                act.activation(rstd[:, 1, :], rstd[:, 0, :], ACT.Sqrt).then_inc(std_ready, 1)

            for i in range(3):
                weight_hi(i)
            qk_out(0, 0, PQ)
            qk_out(0, 0, PK)
            weight_hi(3)
            v_out(0, 0)
            weight_hi(4)
            exponential(0, 0)
            gate_out(0, 0)

            def q_out(b, t):
                qT_out(b, t)
                if has_expert(b) and t == 1:
                    channel_rows(b - 1, 0)
                if has_next(b, t):
                    qk_out(*following(b, t), PQ)

            q_out(0, 0)

            def body(b):
                for t in range(TT):
                    which, second = divmod(t, 2)
                    expert, more = has_expert(b), has_next(b, t)
                    if expert and t == 2:
                        quantised(b - 1, 0, 1)
                    if expert and t == 3:
                        channel_rows(b - 1, 1)
                    if more:
                        qk_out(*following(b, t), PK)
                    if expert and t == 2:
                        scales_row(b - 1, 0)
                        transposed_out(b - 1, 0, 1)
                    if expert and second:
                        quantised(b - 1, which, 0)
                    if more:
                        v_out(*following(b, t))
                    if expert and second:
                        transposed_out(b - 1, which, 0)
                    attT_hi(b, t)
                    if expert and t == 2:
                        silu(b - 1)
                    if more:
                        exponential(*following(b, t))
                    if expert and t == 3:
                        quantised(b - 1, 1, 1)
                    if more:
                        gate_out(*following(b, t))
                    if expert and t == 3:
                        scales_row(b - 1, 1)
                        transposed_out(b - 1, 1, 1)
                    if exists(*ahead(b, t, 3)):
                        load_xT(*ahead(b, t, 3))
                    if exists(*ahead(b, t, 2)):
                        x_hi(*ahead(b, t, 2))
                    if expert and not second:
                        roots(b - 1, which)
                    if t == TT - 1:
                        deviation(b)
                    if more:
                        q_out(*following(b, t))
                if has_expert(b):
                    expert_deviation(b - 1)
                    expert_normalise(b - 1)
            iterations(act, body)
            for which in range(2):
                roots(B - 1, which)
                channel_rows(B - 1, which)
                quantised(B - 1, which, 0)
                transposed_out(B - 1, which, 0)
                quantised(B - 1, which, 1)
                scales_row(B - 1, which)
                transposed_out(B - 1, which, 1)
                if which == 0:
                    silu(B - 1)
            expert_deviation(B - 1)
            expert_normalise(B - 1)

        @block.vector
        def _(dve):
            dve.wait_ge(consts_loaded, PRIMED + CONSTS)
            dve.tensor_copy(ident16[:, :], ident[:, :]).then_inc(ones_ready, 1)
            dve.memset(ones[:, :], 1.0).then_inc(ones_ready, 1)
            dve.memset(scale[:, :, :], 0.0).then_inc(ones_ready, 1)
            dve.tensor_copy(pick[:, :, :], gate[:, :].rearrange("p (i m) -> p i m", m=P)).then_inc(bias_ready, 1)
            hi = att_hi[:, :, :].rearrange("p k t -> p (k t)")
            dve.tensor_copy(hi, att[:, :]).then_inc(bias_hi_ready, 1)
            dve.wait_ge(bias_hi_ready, PRIMED + 1)
            dve.tensor_tensor(att[:, :], att[:, :], hi.bitcast(F32), ALU.subtract).then_inc(bias_hi_ready, 1)
            dve.tensor_scalar(feat[:, 0:D], hi.bitcast(F32), bias_part[:, 0:1], None, ALU.mult)\
                .then_inc(bias_hi_ready, 1)
            dve.wait_ge(bias_hi_ready, PRIMED + 3)
            dve.scalar_tensor_tensor(bias_hl[:, :], att[:, :], bias_part[:, 1:2], feat[:, 0:D],
                                     ALU.mult, ALU.add).then_inc(bias_ready, 1)
            for i in range(5):
                dve.wait_ge(w_hi_ready, PRIMED + i + 1)
                dve.tensor_tensor(w_lo[:, i, :, :], staging[i % 3][:, :, :], w_hi[:, i, :, :].bitcast(F32),
                                  ALU.subtract).then_inc(w_lo_ready, 1)

            def rotated_sum(b, t, i):
                half = bass.ts(i, D)
                n = 2 * (tile_no(b, t) - 1) + i + 1
                dve.wait_ge(rot_b_ready, PRIMED + 2 * n)
                if i:
                    k, _, done, _ = slot(b, t, PK)
                    dve.wait_ge(drained[k], PRIMED + done)
                    dve.tensor_tensor(rot_a[:, half].rearrange("p (h i) -> p h i", i=DK),
                                      qk[:, half].rearrange("p (h i) -> p h i", i=DK),
                                      ropes[:, 0, t, :].unsqueeze(1).to_broadcast([P, H, DK]), ALU.mult)\
                        .then_inc(rot_a_ready, 1)
                dve.wait_ge(rot_a_ready, PRIMED + n)
                dve.tensor_tensor(rot_a[:, half], rot_a[:, half], rot_b[:, half], ALU.add).then_inc(rotated, 1)
                dve.wait_ge(rotated, PRIMED + n)
                dve.tensor_scalar(rot_b[:, half], rot_a[:, half], 0.0, None, ALU.min).then_inc(neg_ready, 1)

            def features(b, t, i):
                half = bass.ts(i, D)
                dve.wait_ge(exp_ready, PRIMED + 2 * (tile_no(b, t) - 1) + i + 1)
                dve.wait_ge(s_updated, PRIMED + 2 * (tile_no(b, t) - 1))
                dve.scalar_tensor_tensor(feat[:, half], rot_a[:, half], 0.0, rot_b[:, half], ALU.max, ALU.add)\
                    .then_inc(feat_ready, 1)

            def mask_state(b, t, c):
                dve.wait_ge(s_updated, PRIMED + 2 * (tile_no(b, t) - 1) + c + 1)
                dve.wait_ge(num_ready, PRIMED + 2 * (tile_no(b, t) - 1))
                dve.tensor_tensor(s_bd[:, c, :, :].rearrange("p (a g) n -> p a g n", a=2),
                                  s_ps[:, :, 0:2 * GE].rearrange("p a (g n) -> p a g n", g=2),
                                  mask[:, :].unsqueeze(1).unsqueeze(1).to_broadcast([P, 2, 2, GE]),
                                  ALU.mult).then_inc(s_masked, 1)

            def attend(b, t):
                dve.wait_ge(num_ready, PRIMED + 2 * tile_no(b, t))
                n4 = n_ps[:, :, 0:2 * GE].rearrange("p a (h e) -> p a h e", e=E1)
                dve.tensor_scalar(rden[:, 0, :].rearrange("p (a h) -> p a h", a=2), n4[:, :, :, DK],
                                  DEN_EPS, 2.0, ALU.add, ALU.mult).then_inc(den_ready, 1)
                k, _, done, _ = slot(b, t, PG)
                dve.wait_ge(drained[k], PRIMED + done)
                if not (isinstance(b, int) and tile_no(b, t) == 1):
                    before = ahead(b, t, -1)
                    k, _, done, _ = slot(*before, AT)
                    dve.wait_ge(filled[k], PRIMED + done)
                for a in range(2):
                    half = bass.ts(a, D // 2)
                    dve.scalar_tensor_tensor(att[:, half].rearrange("p (h e) -> p h e", e=DK),
                                             gate[:, half].rearrange("p (h e) -> p h e", e=DK), 1.0,
                                             n4[:, a, :, 0:DK], ALU.add, ALU.mult).then_inc(gated, 1)
                dve.wait_ge(den_ready, PRIMED + tile_no(b, t))
                dve.reciprocal(rden[:, 1, :], rden[:, 0, :]).then_inc(rden_ready, 1)
                dve.wait_ge(rden_ready, PRIMED + tile_no(b, t))
                dve.wait_ge(gated, PRIMED + 2 * tile_no(b, t))
                att3 = att[:, :].rearrange("p (h e) -> p h e", e=DK)
                dve.tensor_tensor(att3, att3, rden[:, 1, :].unsqueeze(2).to_broadcast([P, H, DK]), ALU.mult)\
                    .then_inc(att_ready, 1)

            def attT_lo(b, t):
                k, _, _, step = slot(b, t, AT)
                dve.wait_ge(att_hi_ready, PRIMED + tile_no(b, t))
                dve.tensor_tensor(att_lo[:, :, :], ring[k][:, :].rearrange("p (g t) -> p g t", g=KT),
                                  att_hi[:, :, :].bitcast(F32), ALU.subtract).then_inc(drained[k], step)

            def add_residual(b, t):
                k, _, done, step = slot(b, t, OUT)
                dve.wait_ge(filled[k], PRIMED + done)
                dve.wait_ge(xres_ready, PRIMED + tile_no(b, t))
                dve.tensor_tensor(x_tok[:, t, :], ring[k][:, :], x_tok[:, t, :], ALU.add).then_inc(drained[k], step)
                dve.wait_ge(drained[k], PRIMED + done)
                dve.bn_stats(stats[:, t, :], x_tok[:, t, :]).then_inc(stats_ready, 1)

            def waiter(semaphore, before):
                level = [0]

                def wait(ins):
                    level[0] += 1
                    ins.then_inc(semaphore, 1)
                    dve.wait_ge(semaphore, PRIMED + before + level[0])
                return wait

            def variance(b):
                dve.wait_ge(stats_ready, PRIMED + b * TT + TT)
                moments(dve, stats, part, mean[:, :], rstd[:, 0, :], waiter(moment_ready, b * 2))\
                    .then_inc(var_ready, 1)

            def normalise(b):
                dve.wait_ge(std_ready, PRIMED + b + 1)
                dve.reciprocal(rstd[:, 2, :], rstd[:, 1, :]).then_inc(rstd_ready, 1)
                dve.wait_ge(rstd_ready, PRIMED + b + 1)
                if has_expert(b):
                    dve.wait_ge(summed, PRIMED + b * TT)
                for t in range(TT):
                    dve.tensor_scalar(x1[:, t, :], x_tok[:, t, :], mean[:, t:t + 1], rstd[:, 2, t:t + 1],
                                      ALU.subtract, ALU.mult).then_inc(normed, 1)

            LINKED = 7

            def linked(e, which, first):
                return waiter(small_done, (e * 2 + which) * LINKED + first)

            def channel_top(e, which, i):
                C = CHANNELS[which]
                if i == 0 and which == 0:
                    dve.wait_ge(normed, PRIMED + e * TT + TT)
                if i == 1:
                    dve.wait_ge(ew_loaded[which], PRIMED + 16 * e + 16)
                dve.tensor_reduce(top[:, i, 0:C], expert_tokens(i, which)[:, :, 0:C].rearrange("p t c -> p c t"),
                                  AX.X, ALU.max, apply_absolute_value=True).then_inc((x_top_ready, w_top_ready)[i][which], 1)

            def channel_ratio(e, which):
                C, kc = CHANNELS[which], CHANNELS[which] // P
                link = linked(e, which, 0)
                for i, item in enumerate((MX, MW)):
                    k, _, done, step = place(e + 1, (which, item))
                    dve.wait_ge(filled[k], PRIMED + done)
                    dve.tensor_reduce(amax[:, i, 0:kc], ring[k][:, 0:C].rearrange("p (c t) -> p c t", t=P),
                                      AX.X, ALU.max).then_inc(drained[k], step)
                    dve.wait_ge(drained[k], PRIMED + done)
                link(dve.tensor_scalar(amax[:, :, 0:kc], amax[:, :, 0:kc], Q_EPS, None, ALU.max))
                link(dve.reciprocal(small[:, 0, 0:kc], amax[:, 1, 0:kc]))
                dve.tensor_tensor(small[:, 1, 0:kc], amax[:, 0, 0:kc], small[:, 0, 0:kc], ALU.mult)\
                    .then_inc(ratio_ready[which], 1)

            def channel_scale(e, which):
                kc = CHANNELS[which] // P
                link = linked(e, which, 2)
                dve.wait_ge(root_ready[which], PRIMED + e + 1)
                link(dve.tensor_scalar(small[:, 2, 0:kc], small[:, 2, 0:kc], Q_EPS, None, ALU.max))
                dve.reciprocal(small[:, 3, 0:kc], small[:, 2, 0:kc]).then_inc(s_ready[which], 1)

            def scale_tokens(e, which):
                C = CHANNELS[which]
                if which == 0 and not (isinstance(e, int) and e == 0):
                    dve.wait_ge(x2_stored, PRIMED + 32 * e)
                k, _, done, _ = place(e + 1, (which, RS))
                dve.wait_ge(drained[k], PRIMED + done)
                dve.tensor_tensor(scaled[0][:, :, 0:C], expert_tokens(0, which)[:, :, 0:C],
                                  rows[:, 0, 0:C].unsqueeze(1).to_broadcast([P, TT, C]),
                                  ALU.mult).then_inc(x_scaled[which], 1)

            def quantise(e, which, i):
                row_scale(e, which, i)
                round_rows(e, which, i)

            def row_scale(e, which, i):
                C = CHANNELS[which]
                out = scaled[i]
                link = linked(e, which, 3 + 2 * i)
                dve.wait_ge((x_scaled, w_scaled)[i][which], PRIMED + e + 1)
                link(dve.tensor_reduce(row_max[:, i, :], out[:, :, 0:C], AX.X, ALU.max,
                                       apply_absolute_value=True))
                dve.tensor_scalar(scale[:, i, :], row_max[:, i, :], Q_EPS, 1.0 / QMAX, ALU.max, ALU.mult)\
                    .then_inc(scale_ready[which], 1)
                dve.wait_ge(scale_ready[which], PRIMED + 2 * e + i + 1)
                link(dve.reciprocal(inverse[:, i, :], scale[:, i, :]))

            def round_rows(e, which, i):
                C = CHANNELS[which]
                out = scaled[i]
                for t in range(TT):
                    dve.tensor_scalar(out[:, t, 0:C], out[:, t, 0:C], inverse[:, i, t:t + 1], ROUND,
                                      ALU.mult, ALU.add).then_inc(shifted[which], 1)
                dve.wait_ge(shifted[which], PRIMED + (2 * e + i + 1) * TT)
                dve.tensor_scalar(out[:, :, 0:C], out[:, :, 0:C], ROUND + QMAX, ROUND - QMAX,
                                  ALU.min, ALU.max).then_inc(clamped[which], 1)

            def linear_out(e, which):
                k, _, done, _ = place(e + 1, (which, SW))
                dve.wait_ge(drained[k], PRIMED + done)
                for t in range(TT):
                    k, _, done, step = place(e + 1, (which, OX[t]))
                    dve.wait_ge(filled[k], PRIMED + done)
                    dve.scalar_tensor_tensor(gu[:, t, :], ring[k][:, :], scale[:, 0, t:t + 1], rows[:, 0, :],
                                             ALU.mult, ALU.mult).then_inc(drained[k], step)

            def activated(e):
                dve.wait_ge(silu_ready, PRIMED + e + 1)
                dve.tensor_tensor(act_in[:, :, :], sl[:, :, 0:D // 2], gu[:, :, D // 2:D], ALU.mult)\
                    .then_inc(act_ready, 1)
                dve.wait_ge(act_ready, PRIMED + e + 1)

            def expert_variance(e):
                for t in range(TT):
                    dve.wait_ge(summed, PRIMED + e * TT + t + 1)
                    dve.bn_stats(e_stats[:, t, :], gu[:, t, :]).then_inc(e_stats_ready, 1)
                dve.wait_ge(e_stats_ready, PRIMED + e * TT + TT)
                moments(dve, e_stats, e_part, e_mean[:, :], e_rstd[:, 0, :], waiter(e_moment_ready, e * 2))\
                    .then_inc(e_var_ready, 1)

            def expert_shift(e):
                dve.wait_ge(e_std_ready, PRIMED + e + 1)
                dve.reciprocal(e_rstd[:, 2, :], e_rstd[:, 1, :]).then_inc(e_rstd_ready, 1)
                dve.wait_ge(e_rstd_ready, PRIMED + 2 * e + 1)
                dve.scalar_tensor_tensor(e_shift[:, :], e_mean[:, :], -1.0, e_rstd[:, 2, :],
                                         ALU.mult, ALU.mult).then_inc(e_rstd_ready, 1)

            for i in range(2):
                rotated_sum(0, 0, i)
            for i in range(2):
                features(0, 0, i)
            mask_state(0, 0, 0)

            def body(b):
                expert = has_expert(b)
                for t in range(TT):
                    which, second = divmod(t, 2)
                    if expert and t == 0:
                        channel_top(b - 1, 0, 0)
                    if expert and t == 1:
                        scale_tokens(b - 1, 0)
                        row_scale(b - 1, 0, 0)
                    mask_state(b, t, 1)
                    if expert and t == 0:
                        channel_top(b - 1, 0, 1)
                    if expert and t == 1:
                        round_rows(b - 1, 0, 0)
                    if expert and t == 3:
                        scale_tokens(b - 1, 1)
                        quantise(b - 1, 1, 0)
                    attend(b, t)
                    if has_next(b, t):
                        rotated_sum(*following(b, t), 0)
                    if expert and second:
                        row_scale(b - 1, which, 1)
                    if expert and t == 2:
                        linear_out(b - 1, 0)
                    attT_lo(b, t)
                    if expert and t == 3:
                        round_rows(b - 1, 1, 1)
                    if has_next(b, t):
                        rotated_sum(*following(b, t), 1)
                    if expert and t == 2:
                        activated(b - 1)
                        channel_top(b - 1, 1, 0)
                        channel_top(b - 1, 1, 1)
                    if expert and t == 0:
                        channel_ratio(b - 1, 0)
                    if has_next(b, t):
                        features(*following(b, t), 0)
                        features(*following(b, t), 1)
                    if expert and t == 0:
                        channel_scale(b - 1, 0)
                    add_residual(b, t)
                    if t == TT - 1:
                        variance(b)
                    if expert and t == 2:
                        channel_ratio(b - 1, 1)
                        channel_scale(b - 1, 1)
                    if t == TT - 1 and not has_next(b, t):
                        channel_top(b, 0, 1)
                    if expert and t == 3:
                        linear_out(b - 1, 1)
                    if has_next(b, t):
                        mask_state(*following(b, t), 0)
                    if expert and t == 1:
                        round_rows(b - 1, 0, 1)
                if expert:
                    expert_variance(b - 1)
                normalise(b)
                if expert:
                    expert_shift(b - 1)
            iterations(dve, body)
            e = B - 1
            for which in range(2):
                if which:
                    activated(e)
                    channel_top(e, 1, 1)
                channel_top(e, which, 0)
                channel_ratio(e, which)
                channel_scale(e, which)
                scale_tokens(e, which)
                quantise(e, which, 0)
                quantise(e, which, 1)
                linear_out(e, which)
            expert_variance(e)
            expert_shift(e)

        @block.tensor
        def _(pe):
            def project(b, t, item):
                k, free, _, step = slot(b, t, item)
                i = (PQ, PK, PV, PG).index(item)
                if item == PQ:
                    pe.wait_ge(xlo_ready, PRIMED + tile_no(b, t))
                pe.wait_ge(drained[k], PRIMED + free)
                pe.matmul(ring[k][:, :], pick[:, i, :], bias_hl[:, :], start=True, stop=False)
                for c in range(KT):
                    last = matmul_split(pe, ring[k][:, :], xT_hi[:, t % 2, c, :], xT_lo[:, t % 2, c, :],
                                        w_hi[:, i, c, :], w_lo[:, i, c, :], False, c == KT - 1)
                last.then_inc(filled[k], step)

            def q_transposed(b, t):
                k, free, _, step = slot(b, t, QT)
                pe.wait_ge(feat_ready, PRIMED + 2 * tile_no(b, t) - 1)
                pe.wait_ge(drained[k], PRIMED + free)
                for g in range(NG):
                    last = pe.transpose(ring[k][:, bass.ts(g, P)], feat[:, bass.ts(g, P)], ident[:, :])
                last.then_inc(filled[k], step)

            def update_state(b, t, c):
                if c == 0:
                    k, _, done, _ = slot(b, t, PV)
                    pe.wait_ge(drained[k], PRIMED + done)
                    pe.wait_ge(feat_ready, PRIMED + 2 * tile_no(b, t))
                pe.wait_ge(s_masked, PRIMED + 2 * (tile_no(b, t) - 1) + c)
                rows_c = slice(c * CS, (c + 1) * CS)
                for g in range(NG):
                    first = t == 0 and c == 0 and g % 2 == 0
                    last = pe.matmul(s_ps[:, g // 2, (g % 2) * GE:(g % 2 + 1) * GE],
                                     feat[rows_c, D + g * P:D + (g + 1) * P],
                                     v_ext[rows_c, t % 2, g * GH:(g + 1) * GH, :].rearrange("p h e -> p (h e)"),
                                     start=first, stop=True, skip_group_check=True)
                last.then_inc(s_updated, 1)

            def numerators(b, t, c):
                pe.wait_ge(s_masked, PRIMED + 2 * (tile_no(b, t) - 1) + c + 1)
                if c == 0:
                    k, _, done, _ = slot(b, t, QT)
                    pe.wait_ge(drained[k], PRIMED + done)
                    pe.wait_ge(gated, PRIMED + 2 * (tile_no(b, t) - 1))
                    pe.wait_ge(den_ready, PRIMED + tile_no(b, t) - 1)
                rows_c = slice(c * CS, (c + 1) * CS)
                for g in range(NG):
                    last = pe.matmul(n_ps[rows_c, g // 2, (g % 2) * GE:(g % 2 + 1) * GE],
                                     q_T[:, g, rows_c], s_bd[:, c, g, :], start=True, stop=True)
                last.then_inc(num_ready, 1)

            def att_transposed(b, t):
                k, free, _, step = slot(b, t, AT)
                pe.wait_ge(att_ready, PRIMED + tile_no(b, t))
                pe.wait_ge(drained[k], PRIMED + free)
                for g in range(NG):
                    last = pe.transpose(ring[k][:, bass.ts(g, P)], att[:, bass.ts(g, P)], ident[:, :])
                last.then_inc(filled[k], step)

            def output(b, t):
                k, free, _, step = slot(b, t, OUT)
                k_at, _, done, _ = slot(b, t, AT)
                pe.wait_ge(drained[k_at], PRIMED + done)
                pe.wait_ge(drained[k], PRIMED + free)
                for c in range(KT):
                    last = matmul_split(pe, ring[k][:, :], att_hi[:, c, :], att_lo[:, c, :],
                                        w_hi[:, 4, c, :], w_lo[:, 4, c, :], c == 0, c == KT - 1)
                last.then_inc(filled[k], step)

            def maxima(e, which):
                for i, item in enumerate((MX, MW)):
                    k, free, _, step = place(e + 1, (which, item))
                    pe.wait_ge((x_top_ready, w_top_ready)[i][which], PRIMED + e + 1)
                    pe.wait_ge(drained[k], PRIMED + free)
                    for c in range(CHANNELS[which] // P):
                        last = pe.transpose(ring[k][:, bass.ts(c, P)], top[:, i, bass.ts(c, P)], ident[:, :])
                    last.then_inc(filled[k], step)

            def channel_rows(e, which):
                C = CHANNELS[which]
                for i, item in enumerate((RS, SS)):
                    k, free, _, step = place(e + 1, (which, item))
                    pe.wait_ge(diag_ready[which], PRIMED + 2 * e + i + 1)
                    pe.wait_ge(drained[k], PRIMED + free)
                    pe.matmul(ring[k][:, 0:C], ones[:, :], diag[:, i, 0:C // P, :].rearrange("p c t -> p (c t)"),
                              start=True, stop=True).then_inc(filled[k], step)

            def transposed(e, which, i):
                pairs = CHANNELS[which] // P // 2
                for j in range(pairs):
                    pe.wait_ge(q_ready[which], PRIMED + (2 * e + i) * pairs + j + 1)
                    k, free, _, step = place(e + 1, (which, ((XT0, XT1), (WT0, WT1))[i][j]))
                    pe.wait_ge(drained[k], PRIMED + free)
                    half = ring[k][:, :].bitcast(BF16).rearrange("p (c t m) -> p c t m", c=2, t=TT)
                    for c in range(2):
                        for t in range(TT):
                            last = pe.transpose(half[:, c, t, :], q[i][:, t, bass.ts(2 * j + c, P)],
                                                ident16[:, :])
                    last.then_inc(filled[k], step)

            def weights_quantised(e, which):
                k, free, _, step = place(e + 1, (which, SW))
                pe.wait_ge(sw_diag_ready[which], PRIMED + e + 1)
                pe.wait_ge(drained[k], PRIMED + free)
                pe.matmul(ring[k][:, :], ones[:, :], diag[:, 0, :, :].rearrange("p c t -> p (c t)"),
                          start=True, stop=True).then_inc(filled[k], step)
                transposed(e, which, 1)

            def linear(e, which):
                kc = CHANNELS[which] // P
                for items in ((XT0, XT1), (WT0, WT1)):
                    for j in range(kc // 2):
                        k, _, done, _ = place(e + 1, (which, items[j]))
                        pe.wait_ge(drained[k], PRIMED + done)
                for t in range(TT):
                    k, free, _, step = place(e + 1, (which, OX[t]))
                    pe.wait_ge(drained[k], PRIMED + free)
                    for c in range(kc):
                        last = pe.matmul(ring[k][:, :], qT[0][:, c, bass.ts(t, P)], qT[1][:, c, :],
                                         start=c == 0, stop=c == kc - 1)
                    last.then_inc(filled[k], step)

            pe.wait_ge(bias_ready, PRIMED + 2)
            pe.wait_ge(consts_loaded, PRIMED + CONSTS)
            pe.wait_ge(ones_ready, PRIMED + 3)
            pe.wait_ge(v_ones_ready, PRIMED + 2)
            for i, item in enumerate((PQ, PK, PV, PG)):
                pe.wait_ge(w_lo_ready, PRIMED + i + 1)
                project(0, 0, item)
            pe.wait_ge(w_lo_ready, PRIMED + 5)

            def body(b):
                for t in range(TT):
                    which, second = divmod(t, 2)
                    expert, more = has_expert(b), has_next(b, t)
                    q_transposed(b, t)
                    update_state(b, t, 0)
                    if expert and t == 1:
                        channel_rows(b - 1, 0)
                    if more:
                        project(*following(b, t), PQ)
                    numerators(b, t, 0)
                    update_state(b, t, 1)
                    if expert and t == 3:
                        channel_rows(b - 1, 1)
                    if more:
                        project(*following(b, t), PK)
                    numerators(b, t, 1)
                    if expert and t == 2:
                        weights_quantised(b - 1, 0)
                    if more:
                        project(*following(b, t), PV)
                    if expert and second:
                        transposed(b - 1, which, 0)
                    if expert and t == 2:
                        linear(b - 1, 0)
                    att_transposed(b, t)
                    if more:
                        project(*following(b, t), PG)
                    if expert and t == 0:
                        maxima(b - 1, 0)
                    output(b, t)
                    if expert and t == 2:
                        maxima(b - 1, 1)
                    if expert and t == 3:
                        weights_quantised(b - 1, 1)
                        linear(b - 1, 1)
            iterations(pe, body)
            for which in range(2):
                maxima(B - 1, which)
                channel_rows(B - 1, which)
                transposed(B - 1, which, 0)
                weights_quantised(B - 1, which)
                linear(B - 1, which)



F = 1408
FT = F // P
E = 8
R = 16
LORA_SCALE = 2.0
NU = 2 * P + E
UP = 2 * D + 2 * P
DOWN = P + D
RAW = 3
FAR = -3.0e38
XC0, U0, UM0, MT, WB0, PREPARED = 0, 4, 8, 12, 13, 15


def mixture(nc, x2_dram, a13g, stream, b2T, ident_in, descending, out_dram):
    with ExitStack() as ctx:
        def sb(name, shape, dt=F32):
            return ctx.enter_context(nc.sbuf_tensor("f_" + name, shape, dt))

        primed = []

        def sem(name):
            primed.append(ctx.enter_context(nc.semaphore("f_" + name)))
            return primed[-1]

        def pb(name):
            return ctx.enter_context(nc.psum_tensor("f_" + name, [P, 512], F32))

        ident = sb("ident", [P, P])
        ident16 = sb("ident16", [P, P], BF16)
        desc = sb("desc", [P, E])
        a_raw = sb("a_raw", [P, KT, NU])
        a_hi = sb("a_hi", [P, KT, NU], F32R)
        a_lo = sb("a_lo", [P, KT, NU], F32R)
        b2_raw = sb("b2_raw", [P, D])
        b2_hi = sb("b2_hi", [P, D], F32R)
        b2_lo = sb("b2_lo", [P, D], F32R)
        w_raw = sb("w_raw", [P, RAW, UP + DOWN])
        up_hi = sb("up_hi", [P, 2, UP], F32R)
        up_lo = sb("up_lo", [P, 2, UP], F32R)
        down_hi = sb("down_hi", [P, 3, DOWN], F32R)
        down_lo = sb("down_lo", [P, 3, DOWN], F32R)
        x2 = sb("x2", [P, TT, D])
        xT_hi = sb("xT_hi", [P, KT, T], F32R)
        xT_lo = sb("xT_lo", [P, KT, T], F32R)
        ax = sb("ax", [P, TT, NU])
        pick = sb("pick", [P, 4, TT, E])
        best = sb("best", [P, 4, TT])
        soft = sb("soft", [P, 4, TT])
        weight = sb("weight", [P, 2, TT])
        coef = sb("coef", [P, 2, TT, E])
        masks = sb("masks", [P, 2, TT, E, R], BF16)
        weight_bc = sb("weight_bc", [P, 2, TT, P])
        um = sb("um", [P, TT, 2, 2, P])
        umT_hi = sb("umT_hi", [P, 4, T], F32R)
        umT_lo = sb("umT_lo", [P, 4, T], F32R)
        maskT = sb("maskT", [P, 2, T], BF16)
        weightT = sb("weightT", [P, 2, T])
        silu = sb("silu", [P, 2, T])
        gated = sb("gated", [P, 2, T])
        act = sb("act", [P, 3, T])
        act_hi = sb("act_hi", [P, 2, T], F32R)
        act_lo = sb("act_lo", [P, 2, T], F32R)
        zm = sb("zm", [P, 3, T])
        z_hi = sb("z_hi", [P, T], F32R)
        z_lo = sb("z_lo", [P, T], F32R)
        x3 = sb("x3", [P, TT, D])
        stats = sb("stats", [P, TT, 6])
        part = sb("part", [P, TT, 5])
        mean = sb("mean", [P, TT])
        rstd = sb("rstd", [P, 3, TT])

        h_ps = [pb("h1"), pb("h3")]
        z_ps = [pb("z_sum"), pb("z_second")]
        y_ps = [pb(f"y{t}") for t in range(TT)]

        ident_loaded = sem("ident_loaded")
        consts_loaded = sem("consts_loaded")
        consts_ready = sem("consts_ready")
        x2_loaded = sem("x2_loaded")
        streamed = [sem(f"streamed{i}") for i in range(RAW)]
        x3_loaded = sem("x3_loaded")
        up_hi_ready = sem("up_hi_ready")
        up_lo_ready = sem("up_lo_ready")
        down_hi_ready = sem("down_hi_ready")
        down_lo_ready = sem("down_lo_ready")
        filled = [sem(f"filled{i}") for i in range(2)]
        drained = [sem(f"drained{i}") for i in range(2)]
        y_ready = sem("y_ready")
        y_added = sem("y_added")
        xT_hi_ready = sem("xT_hi_ready")
        step_done = sem("step_done")
        gap_ready = sem("gap_ready")
        exp_ready = sem("exp_ready")
        weight_ready = sem("weight_ready")
        masks_ready = sem("masks_ready")
        um_ready = sem("um_ready")
        um_hi_ready = sem("um_hi_ready")
        norm_step = sem("norm_step")
        h_ready = [sem("h1_ready"), sem("h3_ready")]
        silu_ready = sem("silu_ready")
        gated_ready = sem("gated_ready")
        act_ready = sem("act_ready")
        sum_ready = sem("sum_ready")
        act_hi_ready = sem("act_hi_ready")
        act_lo_ready = sem("act_lo_ready")
        z_done = sem("z_done")
        z_masked = sem("z_masked")
        z_summed = sem("z_summed")
        z_hi_ready = sem("z_hi_ready")
        z_lo_ready = sem("z_lo_ready")
        var_ready = sem("var_ready")
        std_ready = sem("std_ready")
        normed = sem("normed")
        out_stored = sem("out_stored")

        def slot(b, n):
            return n % 2, b * ((PREPARED + 1 - n % 2) // 2) + n // 2

        def batches(eng, prepare, hidden, close):
            prepare(0)
            with eng.Fori(0, B - 1) as b:
                hidden(b)
                close(b, prepare)
            hidden(B - 1)
            close(B - 1, None)

        def tiles(b, f):
            return b * FT + f + 1

        with nc.Block() as start:
            @start.gpsimd
            def _(pool):
                for semaphore in primed:
                    pool.sem_inc(semaphore, PRIMED)

        block = ctx.enter_context(nc.Block())

        @block.sync
        def _(sp):
            sp.dma_start(ident[:, :], ident_in).then_inc(ident_loaded, 16)
            sp.dma_start(x2[:, :, :], x2_dram[0:T, :].rearrange("(t p) d -> p t d", p=P)).then_inc(x2_loaded, 16)
            for dst, src in ((desc[:, :], descending),
                             (a_raw[:, :, :], a13g.rearrange("(k p) n -> p k n", p=P)), (b2_raw[:, :], b2T)):
                sp.dma_start(dst, src).then_inc(consts_loaded, 16)

            def load_x2(b):
                sp.dma_start(x2[:, :, :], x2_dram[bass.ts(b, T), :].rearrange("(t p) d -> p t d", p=P))\
                    .then_inc(x2_loaded, 16)

            def load_x3(b):
                sp.dma_start(x3[:, :, :], x2_dram[bass.ts(b, T), :].rearrange("(t p) d -> p t d", p=P))\
                    .then_inc(x3_loaded, 16)

            def store(b):
                for h in range(2):
                    sp.wait_ge(normed, PRIMED + b * TT + 2 * h + 2)
                    sp.dma_start(out_dram[bass.ds(b * T + h * 2 * P, 2 * P), :].rearrange("(t p) d -> p t d", p=P),
                                 x3[:, 2 * h:2 * h + 2, :]).then_inc(out_stored, 16)

            sp.wait_ge(consts_loaded, PRIMED + 48)
            load_x3(0)
            with sp.Fori(0, B - 1) as b:
                for n in (XC0 + KT - 2, XC0 + KT - 1):
                    k, before = slot(b, n)
                    sp.wait_ge(filled[k], PRIMED + before + 1)
                load_x2(b + 1)
                store(b)
                sp.wait_ge(out_stored, PRIMED + 32 * b + 32)
                load_x3(b + 1)
            store(B - 1)
            sp.wait_ge(out_stored, PRIMED + 32 * B)

        @block.gpsimd
        def _(pool):
            def split_up(b, f):
                pool.wait_ge(up_hi_ready, PRIMED + tiles(b, f))
                pool.tensor_tensor(up_lo[:, f % 2, :], w_raw[:, f % RAW, 0:UP], up_hi[:, f % 2, :].bitcast(F32),
                                   ALU.subtract).then_inc(up_lo_ready, 1)

            def split_down(b, f):
                pool.wait_ge(down_hi_ready, PRIMED + tiles(b, f))
                pool.tensor_tensor(down_lo[:, f % 3, :], w_raw[:, f % RAW, UP:UP + DOWN],
                                   down_hi[:, f % 3, :].bitcast(F32), ALU.subtract).then_inc(down_lo_ready, 1)

            def prepare(b):
                for f in range(2):
                    split_up(b, f)
                for f in range(2):
                    split_down(b, f)

            def hidden(b):
                for f in range(2, FT):
                    split_up(b, f)
                    split_down(b, f)

            def close(b, following):
                if following:
                    following(b + 1)

            batches(pool, prepare, hidden, close)

        @block.scalar
        def _(sc):
            def fetch(b, f):
                before = tiles(b, f - RAW) if f >= RAW else b * FT
                sc.wait_ge(up_lo_ready, PRIMED + before)
                sc.wait_ge(down_lo_ready, PRIMED + before)
                sc.dma_start(w_raw[:, f % RAW, :], stream[f, :, :]).then_inc(streamed[f % RAW], 16)

            PER = [len(range(r, FT, RAW)) for r in range(RAW)]

            def split_up(b, f):
                r = f % RAW
                sc.wait_ge(streamed[r], PRIMED + 16 * (b * PER[r] + f // RAW + 1))
                sc.wait_ge(h_ready[1], PRIMED + (2 * tiles(b, f - 2) if f >= 2 else 2 * b * FT))
                sc.activation(up_hi[:, f % 2, :], w_raw[:, r, 0:UP], ACT.Copy).then_inc(up_hi_ready, 1)

            def split_down(b, f):
                r = f % RAW
                sc.wait_ge(z_done, PRIMED + (tiles(b, f - 3) if f >= 3 else b * FT))
                sc.activation(down_hi[:, f % 3, :], w_raw[:, r, UP:UP + DOWN], ACT.Copy).then_inc(down_hi_ready, 1)

            def x_hi(b):
                for c in range(KT):
                    k, n = slot(b, XC0 + c)
                    sc.wait_ge(filled[k], PRIMED + n + 1)
                    sc.activation(xT_hi[:, c, :], h_ps[k][:, :], ACT.Copy).then_inc(xT_hi_ready, 1)

            def split_ups(b):
                for f in range(RAW):
                    fetch(b, f)
                for f in range(2):
                    split_up(b, f)

            def softmax_exp(b):
                sc.wait_ge(gap_ready, PRIMED + b + 1)
                sc.activation(soft[:, 1, :], soft[:, 0, :], ACT.Exp).then_inc(exp_ready, 1)

            def masked_out(b, pair):
                for a in (2 * pair, 2 * pair + 1):
                    k, n = slot(b, UM0 + a)
                    sc.wait_ge(filled[k], PRIMED + n + 1)
                    sc.activation(umT_hi[:, a, :], h_ps[k][:, :], ACT.Copy).then_inc(um_hi_ready, 1)

            def masks_out(b):
                k, n = slot(b, MT)
                sc.wait_ge(filled[k], PRIMED + n + 1)
                sc.wait_ge(z_masked, PRIMED + 2 * b)
                sc.activation(maskT[:, :, :], h_ps[k][:, :].bitcast(BF16).rearrange("p (a t) -> p a t", a=2),
                              ACT.Copy).then_inc(drained[k], 1)
                for a in range(2):
                    k, n = slot(b, WB0 + a)
                    sc.wait_ge(filled[k], PRIMED + n + 1)
                    sc.activation(weightT[:, a, :], h_ps[k][:, :], ACT.Copy).then_inc(drained[k], 1)

            def z_split(b):
                sc.wait_ge(z_summed, PRIMED + b + 1)
                sc.activation(z_hi[:, :], zm[:, 2, :], ACT.Copy).then_inc(z_hi_ready, 1)

            def deviation(b):
                sc.wait_ge(var_ready, PRIMED + b + 1)
                sc.activation(rstd[:, 1, :], rstd[:, 0, :], ACT.Sqrt).then_inc(std_ready, 1)

            def activation_hi(b, f):
                sc.wait_ge(z_done, PRIMED + tiles(b, f) - 1)
                sc.wait_ge(act_ready, PRIMED + 2 * tiles(b, f))
                sc.activation(act_hi[:, 0, :], act[:, 1, :], ACT.Copy).then_inc(act_hi_ready, 1)
                sc.wait_ge(sum_ready, PRIMED + tiles(b, f))
                sc.activation(act_hi[:, 1, :], act[:, 2, :], ACT.Copy).then_inc(act_hi_ready, 1)

            def prepare(b):
                x_hi(b)
                sc.wait_ge(consts_loaded, PRIMED + 48)
                sc.activation(a_hi[:, :, :], a_raw[:, :, :], ACT.Copy).then_inc(consts_ready, 1)
                sc.activation(b2_hi[:, :], b2_raw[:, :], ACT.Copy).then_inc(consts_ready, 1)
                split_ups(b)
                softmax_exp(b)
                for f in range(2):
                    split_down(b, f)
                masked_out(b, 0)
                masked_out(b, 1)
                masks_out(b)

            def hidden(b):
                for f in range(FT):
                    if f + RAW < FT:
                        fetch(b, f + RAW)
                    for choice in range(2):
                        n = 2 * (tiles(b, f) - 1) + choice
                        sc.wait_ge(h_ready[0], PRIMED + n + 1)
                        sc.wait_ge(gated_ready, PRIMED + 2 * (tiles(b, f) - 1))
                        sc.activation(silu[:, choice, :], h_ps[0][:, :], ACT.Silu).then_inc(silu_ready, 1)
                    if f < FT - 1:
                        activation_hi(b, f)
                    if f + 2 < FT:
                        split_up(b, f + 2)
                        split_down(b, f + 2)

            def close(b, following):
                if following:
                    x_hi(b + 1)
                activation_hi(b, FT - 1)
                if following:
                    split_ups(b + 1)
                    softmax_exp(b + 1)
                    for f in range(2):
                        split_down(b + 1, f)
                    masked_out(b + 1, 0)
                z_split(b)
                if following:
                    masked_out(b + 1, 1)
                    masks_out(b + 1)
                deviation(b)

            batches(sc, prepare, hidden, close)

        @block.vector
        def _(dve):
            dve.wait_ge(ident_loaded, PRIMED + 16)
            dve.tensor_copy(ident16[:, :], ident[:, :]).then_inc(consts_ready, 1)

            def waiter(semaphore, before):
                level = [0]

                def wait(ins):
                    level[0] += 1
                    ins.then_inc(semaphore, 1)
                    dve.wait_ge(semaphore, PRIMED + before + level[0])
                return wait

            def x_lo(b):
                for c in range(KT):
                    k, n = slot(b, XC0 + c)
                    dve.wait_ge(xT_hi_ready, PRIMED + b * KT + c + 1)
                    dve.tensor_tensor(xT_lo[:, c, :], h_ps[k][:, :], xT_hi[:, c, :].bitcast(F32), ALU.subtract)\
                        .then_inc(drained[k], 1)

            def choose(b):
                link = waiter(step_done, b * 13)
                for t in range(TT):
                    k, n = slot(b, U0 + t)
                    dve.wait_ge(filled[k], PRIMED + n + 1)
                    dve.tensor_copy(ax[:, t, :], h_ps[k][:, 0:NU]).then_inc(drained[k], 1)
                k, n = slot(b, U0 + TT - 1)
                dve.wait_ge(drained[k], PRIMED + n + 1)
                k, n = slot(b, U0 + TT - 2)
                dve.wait_ge(drained[k], PRIMED + n + 1)
                logits = ax[:, :, 2 * P:NU]

                def one_hot(values, m, where):
                    link(dve.tensor_reduce(best[:, m, :], values, AX.X, ALU.max))
                    link(dve.tensor_tensor(where, values, best[:, m, :].unsqueeze(2).to_broadcast([P, TT, E]),
                                           ALU.is_equal))
                    link(dve.tensor_tensor(where, where, desc[:, :].unsqueeze(1).to_broadcast([P, TT, E]), ALU.mult))
                    link(dve.tensor_reduce(best[:, m + 1, :], where, AX.X, ALU.max))
                    link(dve.tensor_tensor(where, where, best[:, m + 1, :].unsqueeze(2).to_broadcast([P, TT, E]),
                                           ALU.is_equal))

                one_hot(logits, 0, pick[:, 1, :, :])
                link(dve.scalar_tensor_tensor(pick[:, 2, :, :], pick[:, 1, :, :], FAR, logits,
                                              ALU.mult, ALU.add))
                one_hot(pick[:, 2, :, :], 2, pick[:, 3, :, :])
                dve.tensor_tensor(soft[:, 0, :], best[:, 2, :], best[:, 0, :], ALU.subtract).then_inc(gap_ready, 1)
                link(dve.tensor_tensor(pick[:, 0, :, :], pick[:, 3, :, :], pick[:, 1, :, :], ALU.subtract))
                for a in range(2):
                    last = dve.tensor_scalar(coef[:, a, :, :], pick[:, 1 - a, :, :], LORA_SCALE, None, ALU.mult)
                link(last)

            def mask_rows(b):
                for a in range(2):
                    for t in range(TT):
                        ins = dve.tensor_tensor(
                            um[:, t, a, :, :].rearrange("p s (e r) -> p s e r", e=E),
                            ax[:, t, 0:2 * P].rearrange("p (s e r) -> p s e r", s=2, e=E),
                            coef[:, a, t, :].unsqueeze(1).unsqueeze(3).to_broadcast([P, 2, E, R]), ALU.mult)
                    ins.then_inc(um_ready, 1)

            def rows_lo(b, pair):
                for a in (2 * pair, 2 * pair + 1):
                    k, n = slot(b, UM0 + a)
                    dve.wait_ge(um_hi_ready, PRIMED + b * 4 + a + 1)
                    dve.tensor_tensor(umT_lo[:, a, :], h_ps[k][:, :], umT_hi[:, a, :].bitcast(F32), ALU.subtract)\
                        .then_inc(drained[k], 1)

            def mask(b):
                for a in range(2):
                    dve.tensor_copy(masks[:, a, :, :, :],
                                    coef[:, a, :, :].unsqueeze(3).to_broadcast([P, TT, E, R])).then_inc(masks_ready, 1)
                dve.wait_ge(exp_ready, PRIMED + b + 1)
                dve.tensor_scalar(soft[:, 2, :], soft[:, 1, :], 1.0, None, ALU.add).then_inc(weight_ready, 1)
                dve.wait_ge(weight_ready, PRIMED + 4 * b + 1)
                dve.reciprocal(weight[:, 0, :], soft[:, 2, :]).then_inc(weight_ready, 1)
                dve.wait_ge(weight_ready, PRIMED + 4 * b + 2)
                dve.tensor_tensor(weight[:, 1, :], soft[:, 1, :], weight[:, 0, :], ALU.mult).then_inc(weight_ready, 1)
                dve.wait_ge(weight_ready, PRIMED + 4 * b + 3)
                dve.tensor_copy(weight_bc[:, :, :, :], weight[:, :, :].unsqueeze(3).to_broadcast([P, 2, TT, P]))\
                    .then_inc(weight_ready, 1)

            def prepare(b):
                x_lo(b)
                dve.wait_ge(consts_loaded, PRIMED + 48)
                dve.wait_ge(consts_ready, PRIMED + 3)
                dve.tensor_tensor(a_lo[:, :, :], a_raw[:, :, :], a_hi[:, :, :].bitcast(F32), ALU.subtract)\
                    .then_inc(consts_ready, 1)
                dve.tensor_tensor(b2_lo[:, :], b2_raw[:, :], b2_hi[:, :].bitcast(F32), ALU.subtract)\
                    .then_inc(consts_ready, 1)
                choose(b)
                mask_rows(b)
                rows_lo(b, 0)
                mask(b)
                rows_lo(b, 1)

            def activation_lo(b, f):
                for i in range(2):
                    dve.wait_ge(act_hi_ready, PRIMED + 2 * (tiles(b, f) - 1) + i + 1)
                    dve.tensor_tensor(act_lo[:, i, :], act[:, 1 + i, :], act_hi[:, i, :].bitcast(F32),
                                      ALU.subtract).then_inc(act_lo_ready, 1)

            def activation(b, f, choice):
                n = 2 * (tiles(b, f) - 1) + choice
                dve.wait_ge(silu_ready, PRIMED + n + 1)
                dve.tensor_tensor(gated[:, choice, :], silu[:, choice, :], weightT[:, choice, :], ALU.mult)\
                    .then_inc(gated_ready, 1)
                dve.wait_ge(gated_ready, PRIMED + n + 1)
                dve.wait_ge(h_ready[1], PRIMED + n + 1)
                dve.tensor_tensor(act[:, choice, :], h_ps[1][:, :], gated[:, choice, :], ALU.mult)\
                    .then_inc(act_ready, 1)

            def hidden(b):
                for k in range(2):
                    kk, n = slot(b, WB0 + k)
                    dve.wait_ge(drained[kk], PRIMED + n + 1)
                for f in range(FT):
                    activation(b, f, 0)
                    activation(b, f, 1)
                    dve.wait_ge(act_ready, PRIMED + 2 * tiles(b, f))
                    dve.tensor_tensor(act[:, 2, :], act[:, 0, :], act[:, 1, :], ALU.add).then_inc(sum_ready, 1)
                    if f < FT - 1:
                        activation_lo(b, f)

            def mask_z(b):
                dve.wait_ge(z_done, PRIMED + b * FT + FT)
                for i in range(2):
                    dve.tensor_tensor(zm[:, i, :], z_ps[i][:, :], maskT[:, i, :], ALU.mult)\
                        .then_inc(z_masked, 1)
                dve.wait_ge(z_masked, PRIMED + 2 * b + 2)
                dve.tensor_tensor(zm[:, 2, :], zm[:, 0, :], zm[:, 1, :], ALU.add).then_inc(z_summed, 1)

            def z_split(b):
                dve.wait_ge(z_hi_ready, PRIMED + b + 1)
                dve.tensor_tensor(z_lo[:, :], zm[:, 2, :], z_hi[:, :].bitcast(F32), ALU.subtract)\
                    .then_inc(z_lo_ready, 1)

            def normalise(b):
                dve.wait_ge(x3_loaded, PRIMED + 16 * b + 16)
                for t in range(TT):
                    dve.wait_ge(y_ready, PRIMED + b * TT + t + 1)
                    dve.tensor_tensor(x3[:, t, :], y_ps[t][:, :], x3[:, t, :], ALU.add).then_inc(y_added, 1)
                    dve.wait_ge(y_added, PRIMED + b * TT + t + 1)
                    last = dve.bn_stats(stats[:, t, :], x3[:, t, :])
                link = waiter(norm_step, b * 4)
                link(last)
                moments(dve, stats, part, mean[:, :], rstd[:, 0, :], link).then_inc(var_ready, 1)
                dve.wait_ge(std_ready, PRIMED + b + 1)
                link(dve.reciprocal(rstd[:, 2, :], rstd[:, 1, :]))
                for t in range(TT):
                    dve.tensor_scalar(x3[:, t, :], x3[:, t, :], mean[:, t:t + 1], rstd[:, 2, t:t + 1],
                                      ALU.subtract, ALU.mult).then_inc(normed, 1)

            def close(b, following):
                if following:
                    x_lo(b + 1)
                activation_lo(b, FT - 1)
                if following:
                    choose(b + 1)
                if following:
                    mask_rows(b + 1)
                mask_z(b)
                if following:
                    rows_lo(b + 1, 0)
                z_split(b)
                if following:
                    mask(b + 1)
                    rows_lo(b + 1, 1)
                normalise(b)

            batches(dve, prepare, hidden, close)

        @block.tensor
        def _(pe):
            def up(b, f, i):
                if i == 0:
                    pe.wait_ge(up_lo_ready, PRIMED + tiles(b, f))
                    pe.wait_ge(silu_ready, PRIMED + 2 * (tiles(b, f) - 1))
                else:
                    pe.wait_ge(act_ready, PRIMED + 2 * (tiles(b, f) - 1))
                s = f % 2
                for c in range(KT):
                    cols = slice(i * D + c * P, i * D + (c + 1) * P)
                    matmul_split(pe, h_ps[i][:, :], up_hi[:, s, cols], up_lo[:, s, cols],
                                 xT_hi[:, c, :], xT_lo[:, c, :], c == 0, False)
                cols = slice(2 * D + i * P, 2 * D + (i + 1) * P)
                matmul_split(pe, h_ps[i][:, :], up_hi[:, s, cols], up_lo[:, s, cols],
                             umT_hi[:, i, :], umT_lo[:, i, :], False, True).then_inc(h_ready[i], 1)

            def second(b, f, i):
                if i == 0:
                    pe.wait_ge(silu_ready, PRIMED + 2 * tiles(b, f) - 1)
                else:
                    pe.wait_ge(act_ready, PRIMED + 2 * tiles(b, f) - 1)
                s = f % 2
                cols = slice(2 * D + i * P, 2 * D + (i + 1) * P)
                rhs = 2 + i
                last = None
                for l, r in ((up_hi, umT_hi), (up_lo, umT_hi), (up_hi, umT_lo)):
                    last = pe.matmul(h_ps[i][:, :], l[:, s, cols], r[:, rhs, :], start=False, stop=True,
                                     skip_group_check=True)
                last.then_inc(h_ready[i], 1)

            def down(b, f):
                pe.wait_ge(act_lo_ready, PRIMED + 2 * tiles(b, f))
                pe.wait_ge(down_lo_ready, PRIMED + tiles(b, f))
                if f == 0:
                    pe.wait_ge(y_added, PRIMED + b * TT)
                s = f % 3
                for t in range(TT):
                    matmul_split(pe, y_ps[t][:, :], act_hi[:, 1, bass.ts(t, P)], act_lo[:, 1, bass.ts(t, P)],
                                 down_hi[:, s, P:DOWN], down_lo[:, s, P:DOWN], f == 0, False)

            def adapters(b, f):
                if f == 0:
                    pe.wait_ge(z_masked, PRIMED + 2 * b)
                s = f % 3
                for i in (1, 0):
                    last = matmul_split(pe, z_ps[i][:, :], down_hi[:, s, 0:P], down_lo[:, s, 0:P],
                                        act_hi[:, 1 - i, :], act_lo[:, 1 - i, :], f == 0, f == FT - 1)
                last.then_inc(z_done, 1)

            def x_transposed(b):
                pe.wait_ge(x2_loaded, PRIMED + 16 * b + 16)
                for c in range(KT):
                    k, n = slot(b, XC0 + c)
                    if c == 0:
                        pe.wait_ge(silu_ready, PRIMED + 2 * b * FT)
                    if c == 1:
                        pe.wait_ge(act_ready, PRIMED + 2 * b * FT)
                    pe.wait_ge(drained[k], PRIMED + n)
                    for t in range(TT):
                        last = pe.transpose(h_ps[k][:, bass.ts(t, P)], x2[:, t, bass.ts(c, P)], ident[:, :])
                    last.then_inc(filled[k], 1)

            def adapters_in(b):
                for c in range(KT - 2, KT):
                    k, n = slot(b, XC0 + c)
                    pe.wait_ge(drained[k], PRIMED + n + 1)
                for t in range(TT):
                    k, n = slot(b, U0 + t)
                    pe.wait_ge(drained[k], PRIMED + n)
                    for c in range(KT):
                        last = matmul_split(pe, h_ps[k][:, 0:NU], xT_hi[:, c, bass.ts(t, P)],
                                            xT_lo[:, c, bass.ts(t, P)], a_hi[:, c, :], a_lo[:, c, :],
                                            c == 0, c == KT - 1)
                    last.then_inc(filled[k], 1)

            def masked_transposed(b, pair):
                for a in (2 * pair, 2 * pair + 1):
                    k, n = slot(b, UM0 + a)
                    if a % 2 == 0:
                        pe.wait_ge(um_ready, PRIMED + 2 * b + a // 2 + 1)
                    pe.wait_ge(drained[k], PRIMED + n)
                    for t in range(TT):
                        last = pe.transpose(h_ps[k][:, bass.ts(t, P)], um[:, t, a // 2, a % 2, :], ident[:, :])
                    last.then_inc(filled[k], 1)

            def masks_transposed(b):
                k, n = slot(b, MT)
                pe.wait_ge(masks_ready, PRIMED + 2 * b + 2)
                pe.wait_ge(drained[k], PRIMED + n)
                half = h_ps[k][:, :].bitcast(BF16).rearrange("p (a t m) -> p a t m", a=2, t=TT)
                for a in range(2):
                    for t in range(TT):
                        last = pe.transpose(half[:, a, t, :], masks[:, a, t, :, :].rearrange("p e r -> p (e r)"),
                                            ident16[:, :])
                last.then_inc(filled[k], 1)
                pe.wait_ge(weight_ready, PRIMED + 4 * b + 4)
                for a in range(2):
                    k, n = slot(b, WB0 + a)
                    pe.wait_ge(drained[k], PRIMED + n)
                    for t in range(TT):
                        last = pe.matmul(h_ps[k][:, bass.ts(t, P)], weight_bc[:, a, t, :], ident[:, :],
                                         start=True, stop=True)
                    last.then_inc(filled[k], 1)

            def adapters_out(b):
                pe.wait_ge(z_lo_ready, PRIMED + b + 1)
                for t in range(TT):
                    matmul_split(pe, y_ps[t][:, :], z_hi[:, bass.ts(t, P)], z_lo[:, bass.ts(t, P)],
                                 b2_hi[:, :], b2_lo[:, :], False, True).then_inc(y_ready, 1)

            def prepare(b):
                x_transposed(b)
                pe.wait_ge(consts_ready, PRIMED + 5)
                adapters_in(b)
                masked_transposed(b, 0)
                masked_transposed(b, 1)
                masks_transposed(b)

            def hidden(b):
                for n in (WB0, WB0 + 1):
                    k, before = slot(b, n)
                    pe.wait_ge(drained[k], PRIMED + before + 1)
                for f in range(FT):
                    up(b, f, 0)
                    up(b, f, 1)
                    if f:
                        down(b, f - 1)
                    second(b, f, 0)
                    second(b, f, 1)
                    if f:
                        adapters(b, f - 1)

            def close(b, following):
                if following:
                    x_transposed(b + 1)
                    adapters_in(b + 1)
                down(b, FT - 1)
                adapters(b, FT - 1)
                if following:
                    masked_transposed(b + 1, 0)
                    masked_transposed(b + 1, 1)
                adapters_out(b)
                if following:
                    masks_transposed(b + 1)

            pe.wait_ge(ident_loaded, PRIMED + 16)
            batches(pe, prepare, hidden, close)


def decoder_layer(nc, a, out):
    x2 = nc.dram_tensor("x2_scratch", (B * T, D), F32, kind="Internal").ap()
    attention_and_experts(nc, a["xT"], a["x"], a["wT"], a["bias_rows"], a["bias_parts"], a["bias_pick"], a["bo"],
                          a["rope"], a["head_mask"], a["ident"], a["w1"], a["w2"], x2)
    mixture(nc, x2, a["a13g"], a["stream"], a["b2T"], a["ident"], a["descending"], out)



def host_arrays(inputs):
    import numpy as np
    x = np.ascontiguousarray(inputs["x"]).reshape(B * T, D)
    pos = np.arange(T, dtype=np.float32)
    inv = (1.0 / 10000.0 ** (np.arange(0, DK, 2, dtype=np.float32) / DK)).astype(np.float32)
    ang = pos[:, None] * inv[None, :]
    sin, cos = np.sin(ang), np.cos(ang)
    rope = np.empty((P, 2, TT, DK), np.float32)
    rope[:, 0] = np.repeat(cos, 2, axis=1).reshape(TT, P, DK).transpose(1, 0, 2)
    rope[:, 1] = np.stack([-sin, sin], axis=-1).reshape(TT, P, DK).transpose(1, 0, 2)
    mask = np.zeros((P, GH, E1), np.float32)
    for j in range(GH):
        mask[j * DK:(j + 1) * DK, j] = 1.0
    bias_rows = np.zeros((P, D), np.float32)
    bias_parts = np.zeros((P, 2), np.float32)
    bias_pick = np.zeros((P, 4, P), np.float32)
    for i, c in enumerate("qkvg"):
        for r in range(2):
            bias_rows[32 * i + r] = inputs[f"L0_attn_b{c}"]
            bias_parts[32 * i + r, r] = 1.0
            bias_pick[32 * i + r, i] = 1.0
    ffn = {k[7:]: np.asarray(v) for k, v in inputs.items() if k.startswith("L0_ffn")}
    stream = np.empty((FT, P, UP + DOWN), np.float32)
    for i, w in enumerate(("w1", "w3")):
        stream[:, :, i * D:(i + 1) * D] = ffn[w].reshape(FT, P, KT, P).transpose(0, 3, 2, 1).reshape(FT, P, D)
    for i, w in enumerate(("b1", "b3")):
        stream[:, :, 2 * D + i * P:2 * D + (i + 1) * P] = \
            ffn[w].transpose(0, 2, 1).reshape(P, FT, P).transpose(1, 0, 2)
    stream[:, :, UP:UP + P] = ffn["a2"].reshape(P, FT, P).transpose(1, 2, 0)
    stream[:, :, UP + P:] = ffn["w2"].T.reshape(FT, P, D)
    return dict(
        stream=stream,
        a13g=np.concatenate([ffn["a1"].reshape(P, D), ffn["a3"].reshape(P, D), ffn["gate_w"]]).T.copy(),
        b2T=np.ascontiguousarray(ffn["b2"].transpose(0, 2, 1).reshape(P, D)),
        descending=np.ascontiguousarray(np.broadcast_to(np.arange(E, 0, -1, dtype=np.float32), (P, E))),
        xT=np.ascontiguousarray(x.T), x=x,
        wT=np.stack([inputs[f"L0_attn_W{c}"].T for c in "qkvgo"]),
        bias_rows=bias_rows, bias_parts=bias_parts, bias_pick=bias_pick.reshape(P, 4 * P),
        bo=np.ascontiguousarray(np.broadcast_to(inputs["L0_attn_bo"], (P, D))),
        w1=np.ascontiguousarray(inputs["fside_BxS2xS2_0"].reshape(B * D, D)),
        w2=np.ascontiguousarray(inputs["ctx_1024"].reshape(B * D, D // 2)),
        rope=rope, head_mask=mask.reshape(P, GE), ident=np.eye(P, dtype=np.float32))


def kernel(**inputs):
    import concourse.bacc as bacc
    from concourse.bass_utils import run_bass_kernel_spmd

    nc = bacc.Bacc("TRN2", target_bir_lowering=False, num_devices=1)
    arrays = host_arrays(inputs)
    a = {name: nc.dram_tensor("in_" + name, v.shape, mybir.dt.from_np(v.dtype), kind="ExternalInput").ap()
         for name, v in arrays.items()}
    out = nc.dram_tensor("out", (B * T, D), F32, kind="ExternalOutput").ap()
    decoder_layer(nc, a, out)
    r = run_bass_kernel_spmd(nc, [{"in_" + name: v for name, v in arrays.items()}], core_ids=[0])
    return r.results[0]["out"].reshape(B, T, D)
```
